# Optimizing a Trainium2 kernel written in Bass

```python
import numpy as np
import jax
import jax.numpy as jnp

def _softmax(x, axis=-1):
    return jax.nn.softmax(x, axis=axis)

def _gelu(x):
    return jax.nn.gelu(x, approximate=True)

def _silu(x):
    return jax.nn.silu(x)

def _sigmoid(x):
    return jax.nn.sigmoid(x)

def _layernorm(x, axis=-1, eps=1e-05):
    m = jnp.mean(x, axis=axis, keepdims=True)
    v = jnp.var(x, axis=axis, keepdims=True)
    return (x - m) / jnp.sqrt(v + eps)

def _scatter_add(tgt, idx, src, axis=0):
    return tgt.at[idx].add(src)

def _segment_sum(src, seg, n):
    return jax.ops.segment_sum(src, seg, n)
kernel_name = 'mk_gnn_resnorm_d2_gnn_r32_6296af'

def setup_inputs(seed: int=0):
    np.random.seed(seed)
    _w = jnp.asarray

    def _rec_inputs():
        import jax
        import jax.numpy as jnp
        _gk = jax.random.key(seed)
        x = -0.0002117 + 1 * jax.random.normal(jax.random.fold_in(_gk, 1), (3125, 256), jnp.float32)
        src = jax.random.randint(jax.random.fold_in(_gk, 2), (50000,), 0, 3125, jnp.int32)
        dst = jax.random.randint(jax.random.fold_in(_gk, 3), (50000,), 0, 3125, jnp.int32)
        _o = jnp.argsort(dst, stable=True)
        src = src[_o]
        dst = dst[_o]
        return (x, src, dst)
    x, src, dst = _rec_inputs()

    def _L0_gnn_setup():
        import jax, jax.numpy as jnp
        import numpy as np
        N_NODES = 3125
        N_EDGES = 50000
        D = 256

        def _sage_layer(x, src, dst, inv_deg, W_self, W_neigh, b):
            agg = jax.ops.segment_sum(x[src], dst, num_segments=N_NODES)
            mean = agg * inv_deg[:, None]
            return x @ W_self + mean @ W_neigh + b
        key = jax.random.key(seed)
        ks = jax.random.split(key, 16)
        inp = {'features': jax.random.normal(ks[0], (N_NODES, D), dtype=jnp.float32), 'src': jax.random.randint(ks[1], (N_EDGES,), 0, N_NODES, dtype=jnp.int32), 'dst': jax.random.randint(ks[2], (N_EDGES,), 0, N_NODES, dtype=jnp.int32)}
        scale = 1.0 / np.sqrt(D)
        for i in range(3):
            inp[f'W{i}_self'] = jax.random.normal(ks[3 + 4 * i], (D, D), dtype=jnp.float32) * scale
            inp[f'W{i}_neigh'] = jax.random.normal(ks[4 + 4 * i], (D, D), dtype=jnp.float32) * scale
            inp[f'b{i}'] = jnp.zeros((D,), dtype=jnp.float32)
        return inp
    _L0_gnn_all = _L0_gnn_setup()
    _L0_gnn_in = {k: v for k, v in _L0_gnn_all.items() if k in ('W0_self', 'W0_neigh', 'b0', 'W1_self', 'W1_neigh', 'b1', 'W2_self', 'W2_neigh', 'b2')}
    del _L0_gnn_all

    def _L1_gnn_setup():
        import jax, jax.numpy as jnp
        import numpy as np
        N_NODES = 10000
        N_EDGES = 5000
        F_IN = 256
        HEADS = 4
        F_OUT = 256
        NEG_SLOPE = 0.2
        EPS = 1e-05

        def gat_conv(x, src, dst, W, a_src, a_dst, bias, concat):
            N = x.shape[0]
            H, C = a_src.shape
            h = (x @ W).reshape(N, H, C)
            al_s = jnp.einsum('nhc,hc->nh', h, a_src)
            al_d = jnp.einsum('nhc,hc->nh', h, a_dst)
            e = jax.nn.leaky_relu(al_s[src] + al_d[dst], NEG_SLOPE)
            m = jax.ops.segment_max(e, dst, num_segments=N)
            ex = jnp.exp(e - m[dst])
            denom = jax.ops.segment_sum(ex, dst, num_segments=N)
            alpha = ex / denom[dst]
            out = jax.ops.segment_sum(h[src] * alpha[:, :, None], dst, num_segments=N)
            out = out.reshape(N, H * C) if concat else out.mean(axis=1)
            return out + bias

        def graph_norm(x, w, b, ms):
            mean = x.mean(axis=0, keepdims=True)
            sh = x - ms * mean
            var = (sh * sh).mean(axis=0, keepdims=True)
            return w * sh / jnp.sqrt(var + EPS) + b
        key = jax.random.key(seed)
        ks = jax.random.split(key, 12)
        H1 = HEADS * F_IN
        s = 0.05
        return {'x': jax.random.normal(ks[0], (N_NODES, F_IN), jnp.float32), 'edge_index': jax.random.randint(ks[1], (2, N_EDGES), 0, N_NODES, jnp.int64), 'W1': jax.random.normal(ks[2], (F_IN, HEADS * F_IN), jnp.float32) * s, 'att_src1': jax.random.normal(ks[3], (HEADS, F_IN), jnp.float32) * s, 'att_dst1': jax.random.normal(ks[4], (HEADS, F_IN), jnp.float32) * s, 'b1': jnp.zeros((H1,), jnp.float32), 'gn_w': jnp.ones((H1,), jnp.float32), 'gn_b': jnp.zeros((H1,), jnp.float32), 'gn_ms': jnp.ones((H1,), jnp.float32), 'W2': jax.random.normal(ks[5], (H1, F_OUT), jnp.float32) * s, 'att_src2': jax.random.normal(ks[6], (1, F_OUT), jnp.float32) * s, 'att_dst2': jax.random.normal(ks[7], (1, F_OUT), jnp.float32) * s, 'b2': jnp.zeros((F_OUT,), jnp.float32)}
    _L1_gnn_all = _L1_gnn_setup()
    _L1_gnn_in = {k: v for k, v in _L1_gnn_all.items() if k in ('W1', 'att_src1', 'att_dst1', 'b1', 'gn_w', 'gn_b', 'gn_ms', 'W2', 'att_src2', 'att_dst2', 'b2')}
    del _L1_gnn_all
    return {'x': x, 'src': src, 'dst': dst, 'L0_gnn_W0_self': _L0_gnn_in['W0_self'], 'L0_gnn_W0_neigh': _L0_gnn_in['W0_neigh'], 'L0_gnn_b0': _L0_gnn_in['b0'], 'L0_gnn_W1_self': _L0_gnn_in['W1_self'], 'L0_gnn_W1_neigh': _L0_gnn_in['W1_neigh'], 'L0_gnn_b1': _L0_gnn_in['b1'], 'L0_gnn_W2_self': _L0_gnn_in['W2_self'], 'L0_gnn_W2_neigh': _L0_gnn_in['W2_neigh'], 'L0_gnn_b2': _L0_gnn_in['b2'], 'L1_gnn_W1': _L1_gnn_in['W1'], 'L1_gnn_att_src1': _L1_gnn_in['att_src1'], 'L1_gnn_att_dst1': _L1_gnn_in['att_dst1'], 'L1_gnn_b1': _L1_gnn_in['b1'], 'L1_gnn_gn_w': _L1_gnn_in['gn_w'], 'L1_gnn_gn_b': _L1_gnn_in['gn_b'], 'L1_gnn_gn_ms': _L1_gnn_in['gn_ms'], 'L1_gnn_W2': _L1_gnn_in['W2'], 'L1_gnn_att_src2': _L1_gnn_in['att_src2'], 'L1_gnn_att_dst2': _L1_gnn_in['att_dst2'], 'L1_gnn_b2': _L1_gnn_in['b2']}

def reference(x, src, dst, L0_gnn_W0_self, L0_gnn_W0_neigh, L0_gnn_b0, L0_gnn_W1_self, L0_gnn_W1_neigh, L0_gnn_b1, L0_gnn_W2_self, L0_gnn_W2_neigh, L0_gnn_b2, L1_gnn_W1, L1_gnn_att_src1, L1_gnn_att_dst1, L1_gnn_b1, L1_gnn_gn_w, L1_gnn_gn_b, L1_gnn_gn_ms, L1_gnn_W2, L1_gnn_att_src2, L1_gnn_att_dst2, L1_gnn_b2):
    import jax
    import jax.numpy as jnp

    def _L0_gnn_ref(features, src, dst, W0_self, W0_neigh, b0, W1_self, W1_neigh, b1, W2_self, W2_neigh, b2):
        import jax, jax.numpy as jnp
        import numpy as np
        N_NODES = 3125
        N_EDGES = 50000
        D = 256

        def _sage_layer(x, src, dst, inv_deg, W_self, W_neigh, b):
            agg = jax.ops.segment_sum(x[src], dst, num_segments=N_NODES)
            mean = agg * inv_deg[:, None]
            return x @ W_self + mean @ W_neigh + b
        deg = jax.ops.segment_sum(jnp.ones_like(src, dtype=features.dtype), dst, num_segments=N_NODES)
        inv_deg = 1.0 / jnp.maximum(deg, 1.0)
        h = _sage_layer(features, src, dst, inv_deg, W0_self, W0_neigh, b0)
        h = jax.nn.relu(h)
        h = _sage_layer(h, src, dst, inv_deg, W1_self, W1_neigh, b1)
        h = jax.nn.relu(h)
        h = _sage_layer(h, src, dst, inv_deg, W2_self, W2_neigh, b2)
        return h

    def _L1_gnn_ref(x, edge_index, W1, att_src1, att_dst1, b1, gn_w, gn_b, gn_ms, W2, att_src2, att_dst2, b2):
        import jax, jax.numpy as jnp
        import numpy as np
        N_NODES = 10000
        N_EDGES = 5000
        F_IN = 256
        HEADS = 4
        F_OUT = 256
        NEG_SLOPE = 0.2
        EPS = 1e-05

        def gat_conv(x, src, dst, W, a_src, a_dst, bias, concat):
            N = x.shape[0]
            H, C = a_src.shape
            h = (x @ W).reshape(N, H, C)
            al_s = jnp.einsum('nhc,hc->nh', h, a_src)
            al_d = jnp.einsum('nhc,hc->nh', h, a_dst)
            e = jax.nn.leaky_relu(al_s[src] + al_d[dst], NEG_SLOPE)
            m = jax.ops.segment_max(e, dst, num_segments=N)
            ex = jnp.exp(e - m[dst])
            denom = jax.ops.segment_sum(ex, dst, num_segments=N)
            alpha = ex / denom[dst]
            out = jax.ops.segment_sum(h[src] * alpha[:, :, None], dst, num_segments=N)
            out = out.reshape(N, H * C) if concat else out.mean(axis=1)
            return out + bias

        def graph_norm(x, w, b, ms):
            mean = x.mean(axis=0, keepdims=True)
            sh = x - ms * mean
            var = (sh * sh).mean(axis=0, keepdims=True)
            return w * sh / jnp.sqrt(var + EPS) + b
        N = x.shape[0]
        loop = jnp.arange(N, dtype=edge_index.dtype)
        src = jnp.concatenate([edge_index[0], loop])
        dst = jnp.concatenate([edge_index[1], loop])
        h = gat_conv(x, src, dst, W1, att_src1, att_dst1, b1, concat=True)
        h = graph_norm(h, gn_w, gn_b, gn_ms)
        h = jax.nn.relu(h)
        out = gat_conv(h, src, dst, W2, att_src2, att_dst2, b2, concat=False)
        return out
    edge_index = jnp.stack([src, dst])
    x = _layernorm(x + _L0_gnn_ref(x, src, dst, L0_gnn_W0_self, L0_gnn_W0_neigh, L0_gnn_b0, L0_gnn_W1_self, L0_gnn_W1_neigh, L0_gnn_b1, L0_gnn_W2_self, L0_gnn_W2_neigh, L0_gnn_b2), axis=-1)
    x = _layernorm(x + _L1_gnn_ref(x, edge_index, L1_gnn_W1, L1_gnn_att_src1, L1_gnn_att_dst1, L1_gnn_b1, L1_gnn_gn_w, L1_gnn_gn_b, L1_gnn_gn_ms, L1_gnn_W2, L1_gnn_att_src2, L1_gnn_att_dst2, L1_gnn_b2), axis=-1)
    return x

_drawn_inputs = setup_inputs


def setup_inputs(seed=0):
    import zlib

    import numpy as np

    out = dict(_drawn_inputs(seed))
    spreads = {'L0_gnn_b0': (0.0, 0.1),
     'L0_gnn_b1': (0.0, 0.1),
     'L0_gnn_b2': (0.0, 0.1),
     'L1_gnn_b1': (0.0, 0.1),
     'L1_gnn_gn_w': (1.0, 0.2),
     'L1_gnn_gn_b': (0.0, 0.1),
     'L1_gnn_gn_ms': (1.0, 0.2),
     'L1_gnn_b2': (0.0, 0.1)}
    factors = {}
    for name, (base, spread) in spreads.items():
        noise = np.random.default_rng([zlib.crc32(name.encode()), seed]).standard_normal(out[name].shape)
        drawn = base * np.exp(spread * noise) if base else spread * noise
        out[name] = jnp.asarray(drawn.astype(out[name].dtype))
    for name, factor in factors.items():
        out[name] = (out[name] * factor).astype(out[name].dtype)
    return out
```

```python
from contextlib import ExitStack

import concourse.bass as bass
from concourse import mybir

F32 = mybir.dt.float32
I32 = mybir.dt.int32
BF16 = mybir.dt.bfloat16
ALU = mybir.AluOpType
ACT = mybir.ActivationFunctionType
AX = mybir.AxisListType

P = 128


def build_gnn(nc, a, out):
    N, D = a["x"].shape
    E = a["src"].shape[0]
    H = a["L1_gnn_att_src1"].shape[0]
    KD = D // P
    HD = H * D
    KH = HD // P
    W = 64
    NW = -(-N // W)
    NP = NW * W
    NT = -(-N // P)
    ET = -(-E // P) + 1
    U = 8
    V = -(-(ET - 1 + NW - 1) // U) * U
    NG = V // U
    Q = 4
    VC = 4
    VR = V // VC
    NB = NW - 1
    EP = 125
    EK = E // EP
    FAR = 4095
    RW = D + H
    EPS = 1e-5
    SLOPE = 0.2
    SPREAD = 40.0
    assert E == EP * EK and VR * VC == V and VR <= P and D == 2 * P
    assert V - 1 - NB < ET and NW * W - (NT - 1) * P == W
    QUAD = 4

    def rows(m):
        return W if m == NT - 1 else P

    def real(m):
        return min(P, N - m * P)

    ctx = ExitStack()
    with ctx:
        def sb(name, shape, dt=F32):
            return ctx.enter_context(nc.sbuf_tensor(name, shape, dt))

        def sem(name):
            return ctx.enter_context(nc.semaphore(name))

        edge_src = nc.dram_tensor("edge_src", [ET, P], I32).ap()
        edge_dst = nc.dram_tensor("edge_dst", [ET, P], I32).ap()
        table_sage = [a["x"]] + [nc.dram_tensor(f"table_sage{i}", [NP, D], F32).ap() for i in (1, 2)]
        sorted_src = nc.dram_tensor("sorted_src", [ET * P, 1], I32).ap()
        sorted_dst = nc.dram_tensor("sorted_dst", [ET * P, 1], I32).ap()
        edge_win = nc.dram_tensor("edge_win", [ET * P], I32).ap()
        node_max = nc.dram_tensor("node_max", [NP * H], F32).ap()
        table_gat1 = nc.dram_tensor("table_gat1", [NP, RW], F32).ap()
        table_gat2 = nc.dram_tensor("table_gat2", [NP, D + 1], F32).ap()

        big = sb("big", [P, KH * NP])
        cols = sb("cols", [P, KD * NP])
        nat = sb("nat", [P, NT * RW])
        ring = sb("ring", [P, 2 * U * RW])
        onehot = sb("onehot", [P, 2 * U * W])
        onehot_w = sb("onehot_w", [P, 2 * U * H * W])
        src_of = sb("src_of", [P, V], I32)
        dst_in = sb("dst_in", [P, V])
        win_of = sb("win_of", [1, V], I32)
        idx = sb("idx", [P, Q * U], I32)
        ident = sb("ident", [P, P])
        ident_b = sb("ident_b", [P, P], BF16)
        ones = sb("ones", [P, P])
        iota_w = sb("iota_w", [P, W])
        bias_b = sb("bias_b", [P, 4 * D])
        att2 = sb("att2", [P, 2 * D])
        att1 = sb("att1", [P, KD * 2 * H])
        gvec = sb("gvec", [P, 4 * KH])
        den = sb("den", [W, NW * 3 * H])
        score_win = sb("score_win", [W, NW * 2 * H])
        s_nat = sb("s_nat", [P, NT * 2 * H])
        r_nat = sb("r_nat", [P, NT * H])
        e_nat = sb("e_nat", [P, NT * H])
        w_self = sb("w_self", [P, NT * H])
        rden = sb("rden", [P, NT * H])
        z_buf = sb("z_buf", [P, 3 * U * H])
        look_buf = sb("look_buf", [P, 2 * U * H])
        w_buf = sb("w_buf", [P, 2 * U * H])
        w_parts = sb("w_parts", [P, 2 * 3 * U * H], BF16)
        w_rest = sb("w_rest", [P, 2 * U * H])
        mv = sb("mv", [P, NT * 2])
        stats = sb("stats", [P, NT * 6])
        rstd = sb("rstd", [P, NT])
        gn_sum = sb("gn_sum", [P, KH * 8])
        gn_v = sb("gn_v", [P, 6 * KH])
        small = sb("small", [P, 16])
        ext = sb("ext", [P, 32])
        small_i = sb("small_i", [P, 8], I32)
        flag_i = sb("flag_i", [1, 3], I32)
        smax_nat = sb("smax_nat", [P, NT * H])

        ps = ctx.enter_context(nc.psum_tensor("ps", [P, QUAD, 512], F32))
        ps_t = ctx.enter_context(nc.psum_tensor("ps_t", [P, 2, 512], F32))
        ps_d = ctx.enter_context(nc.psum_tensor("ps_d", [P, 512], F32))
        ps_n = ctx.enter_context(nc.psum_tensor("ps_n", [P, 512], F32))

        sums_sage = big[:, 0:KD * NP].rearrange("p (k n) -> p k n", k=KD)
        o = KD * NP
        self_nat = big[:, o:o + NT * D].rearrange("p (m d) -> p m d", m=NT)
        o += NT * D
        x_nat = big[:, o:o + NT * D].rearrange("p (m d) -> p m d", m=NT)
        o += NT * D
        w_sage = big[:, o:o + 6 * KD * D].rearrange("p (w k d) -> p w k d", w=6, k=KD)
        o += 6 * KD * D
        assert o <= KH * NP
        w1_pre = nat[:, 0:KD * HD].rearrange("p (k n) -> p k n", k=KD)
        prod_pre = nat[:, KD * HD:2 * KD * HD].rearrange("p (k n) -> p k n", k=KD)
        att_pre = big[:, o:o + 2 * HD].rearrange("p (s n) -> p s n", s=2)
        assert o + 2 * HD <= KH * NP
        res_nat = big[:, KD * NP:KD * NP + NT * D].rearrange("p (m d) -> p m d", m=NT)
        w1_sb = ring[:, 0:KD * HD].rearrange("p (k n) -> p k n", k=KD)
        w2_sb = ring[:, KD * HD:KD * HD + KH * D].rearrange("p (c d) -> p c d", c=KH)
        colsv = cols[:, :].rearrange("p (k n) -> p k n", k=KD)
        bigv = big[:, :].rearrange("p (c n) -> p c n", c=KH)
        natv = nat[:, :].rearrange("p (m r) -> p m r", m=NT)
        ringv = ring[:, :].rearrange("p (v r) -> p v r", r=RW)
        oh = onehot[:, :].rearrange("p (b u w) -> p b u w", b=2, u=U)
        ohb = onehot[:, 0:U * W].bitcast(BF16).rearrange("p (b u w) -> p b u w", b=2, u=U)
        oht = cols[0:W, 0:U * P].bitcast(BF16).rearrange("p (b c) -> p b c", b=2)
        score_parts = cols[0:W, U * P:U * P + NW * 3 * H].bitcast(BF16)
        den_nat = cols[:, 2 * U * P:2 * U * P + NT * 3 * H]
        biasv = bias_b[:, :].rearrange("p (s d) -> p s d", s=4)
        att2v = att2[:, :].rearrange("p (s d) -> p s d", s=2)
        att1v = att1[:, :].rearrange("p (k s) -> p k s", k=KD)
        gv = gvec[:, :].rearrange("p (s c) -> p s c", s=4)
        winf = ring[:, 0:V]
        s0 = V
        dst_all = ring[0:EP, s0:s0 + EK]
        cmp_bv = onehot_w[0:NB, 0:V]

        S = {}

        def s(name):
            if name not in S:
                S[name] = sem(name)
            return S[name]

        dst_i = nat[0:EP, 0:EK].bitcast(I32)
        next_i = nat[0:EP, EK:EK + 1].bitcast(I32)
        dst_f = nat[0:EP, 2 * EK:3 * EK]
        next_f = nat[0:EP, 3 * EK:3 * EK + 1]
        junk = onehot_w[0:EP, 0:8 * EK].rearrange("p (j k) -> p j k", j=8)
        below = nat[0:EP, 5 * EK:5 * EK + NB]
        iota_v = nat[:, 6 * EK:6 * EK + V]
        visit_rows_i = ring[0:VR, 0:2 * VC * P].bitcast(I32).rearrange("p (s c e) -> p s c e", s=2, c=VC)
        visit_rows = ring[0:VR, 2 * VC * P:4 * VC * P].rearrange("p (s c e) -> p s c e", s=2, c=VC)
        win_f = nat[:, 6 * EK + V:6 * EK + 2 * V]
        pad_i = nat[0:1, 6 * EK + 2 * V:6 * EK + 2 * V + 4 * P].bitcast(I32)
        iota_c = small[:, 0:VC]
        iota_b = small[:, VC:VC + 1]
        first_i = small_i[0:NB, 0:1]
        tile_i = small_i[0:NB, 1:2]
        tile_f = small[0:NB, VC + 1:VC + 2]
        event = small[0:NB, VC + 2:VC + 3]
        viol = small[0:EP, VC + 3:VC + 5]
        win_all = nat[0:EP, 4 * EK:5 * EK].bitcast(I32)
        flag_f = small[0:1, VC + 5:VC + 6]
        row_i = small_i[0:VR, 2:2 + VC]
        EPAD = ET * P - E

        def score_v(heads):
            return score_win[:, 0:NW * 2 * heads].rearrange("p (w s) -> p w s", s=2 * heads)

        def den_v(width):
            return den[:, 0:NW * width].rearrange("p (w h) -> p w h", h=width)

        def parts_v(heads):
            return score_parts[:, 0:NW * 6 * heads].rearrange("p (w j s) -> p w j s", j=3, s=2 * heads)

        def w_parts_v(heads, half):
            return w_parts[:, half * 3 * U * H:half * 3 * U * H + 3 * U * heads].rearrange("p (u j h) -> p u j h", j=3, h=heads)

        def ohw_v(heads):
            return onehot_w[:, 0:2 * U * heads * W].rearrange("p (b u n) -> p b u n", b=2, u=U)

        def diag_v(heads):
            return onehot_w[:, 0:2 * heads * P].rearrange("p (b h n) -> p b h n", b=2, h=heads)

        ch_order = [h * KD + f for f in range(KD) for h in range(H)]

        def nat_of(buf, m0, m1, heads):
            return buf[:, m0 * heads:m1 * heads].rearrange("p (m h) -> p m h", h=heads)

        def rb_v(b):
            if b % 2 == 0:
                return onehot_w[:, 2 * H * P:2 * H * P + H * 4 * P].rearrange("p (h n) -> p h n", h=H)
            return cols[:, 0:H * 4 * P].rearrange("p (h n) -> p h n", h=H)

        def junk_row(j):
            return cols[:, (H + j) * 4 * P:(H + j + 1) * 4 * P]

        deg_bank = [ps_n, ps_d]
        den_bank = [ps_n, ps_t[:, 1, :]]

        def ring_rows(n, q):
            if q < 2:
                return ringv[:, q * U:(q + 1) * U, :]
            if n < 3:
                return onehot_w[:, (q - 2) * U * D:(q - 1) * U * D].rearrange("p (u r) -> p u r", u=U)
            return nat[:, (q - 2) * U * RW:(q - 1) * U * RW].rearrange("p (u r) -> p u r", u=U)

        def windows_of(engine, gr):
            _, regs = nc.values_load_multi_w_load_instructions(
                win_of[0:1, bass.ds(gr * U, U)], engines=[engine], min_val=0, max_val=NW - 1,
                skip_runtime_bounds_check_because="a count of the NB boundaries is at most NB = NW - 1")
            return regs

        def rows_before(n, q):
            return n * 16 * U * len(range(q, NG, Q))

        def early(gr, k):
            return isinstance(gr, int) and gr < k

        def each_group(eng, body):
            for q in range(Q):
                body(q, q, 16 * U)
            with eng.Fori(1, NG // Q) as i:
                for q in range(Q):
                    body(i * Q + q, q, i * (16 * U) + 16 * U)
            for q in range(NG % Q):
                body(NG // Q * Q + q, q, (NG // Q + 1) * 16 * U)

        ctx.enter_context(nc.allow_non_contiguous_dma(reason="a few hundred single elements, once"))
        block = ctx.enter_context(nc.Block())

        @block.sync
        def _(sp):
            sp.dma_start(dst_i, a["dst"].rearrange("(p k) -> p k", p=EP)).then_inc(s("dst_loaded"), 16)
            sp.dma_start(next_i[0:EP - 1, :], a["dst"][EK:E].rearrange("(p k) -> p k", k=EK)[:, 0:1]).then_inc(s("next_loaded"), 16)
            sp.wait_ge(s("pads"), 2)
            es, ed = edge_src.rearrange("t e -> (t e)"), edge_dst.rearrange("t e -> (t e)")
            sp.dma_start(es[0:E], a["src"]).then_inc(s("edges_in"), 16)
            sp.dma_start(ed[0:E], a["dst"]).then_inc(s("edges_in"), 16)
            sp.dma_start(es[E:ET * P].rearrange("(p k) -> p k", p=1), pad_i[:, 0:EPAD]).then_inc(s("edges_in"), 16)
            sp.dma_start(ed[E:ET * P].rearrange("(p k) -> p k", p=1), pad_i[:, 2 * P:2 * P + EPAD]).then_inc(s("edges_in"), 16)
            sp.wait_ge(s("x_cleared"), 1)
            sp.dma_start(x_nat[:, 0:NT - 1, :], a["x"][0:(NT - 1) * P, :].rearrange("(m p) d -> p m d", p=P)).then_inc(s("x_loaded"), 16)
            sp.dma_start(x_nat[0:real(NT - 1), NT - 1, :], a["x"][(NT - 1) * P:N, :]).then_inc(s("x_loaded"), 16)
            for i in range(3):
                for j, kind in enumerate(("self", "neigh")):
                    sp.dma_start(w_sage[:, 2 * i + j], a[f"L0_gnn_W{i}_{kind}"].rearrange("(k p) d -> p k d", p=P)).then_inc(s("w_loaded"), 16)
            for i, name in enumerate(("L0_gnn_b0", "L0_gnn_b1", "L0_gnn_b2", "L1_gnn_b2")):
                sp.dma_start(biasv[:, i, :], a[name].rearrange("(a d) -> a d", a=1).broadcast_to([P, D])).then_inc(s("w_loaded"), 16)
            sp.dma_start(att2v[:, 0, :], a["L1_gnn_att_src2"].broadcast_to([P, D])).then_inc(s("w_loaded"), 16)
            sp.dma_start(att2v[:, 1, :], a["L1_gnn_att_dst2"].broadcast_to([P, D])).then_inc(s("w_loaded"), 16)
            for i, name in enumerate(("L1_gnn_b1", "L1_gnn_gn_w", "L1_gnn_gn_b", "L1_gnn_gn_ms")):
                sp.dma_start(gv[:, i, :], a[name].rearrange("(c p) -> p c", p=P)).then_inc(s("w_loaded"), 16)
            sp.wait_ge(s("setup_done"), 1)
            for i, name in enumerate(("L1_gnn_att_src1", "L1_gnn_att_dst1")):
                sp.dma_start(att_pre[:, i, :], a[name].rearrange("(a h) d -> a (h d)", a=1).broadcast_to([P, HD])).then_inc(s("att_loaded"), 16)
            sp.dma_start(w1_pre, a["L1_gnn_W1"].rearrange("(k p) n -> p k n", p=P)).then_inc(s("w1_pre_loaded"), 16)
            for i in (1, 2):
                for m in range(NT):
                    sp.wait_ge(s(f"row_ready{i}"), m + 1)
                    sp.dma_start(table_sage[i][m * P:m * P + rows(m), :], natv[0:rows(m), m, 0:D]).then_inc(s(f"table{i}"), 16)
            for m in range(NT):
                sp.wait_ge(s("gat1_row_ready"), m + 1)
                sp.dma_start(table_gat1[m * P:m * P + rows(m), :], natv[0:rows(m), m, :]).then_inc(s("table3"), 16)
            sp.wait_ge(s("agg_ready3"), V)
            sp.dma_start(w1_sb, a["L1_gnn_W1"].rearrange("(k p) n -> p k n", p=P)).then_inc(s("w1_loaded"), 16)
            sp.dma_start(w2_sb, a["L1_gnn_W2"].rearrange("(c p) d -> p c d", p=P)).then_inc(s("w2_loaded"), 16)
            for m in range(NT):
                sp.wait_ge(s("gat2_row_ready"), m + 1)
                sp.dma_start(table_gat2[m * P:m * P + rows(m), :], natv[0:rows(m), m, 0:D + 1]).then_inc(s("table4"), 16)
            sp.wait_ge(s("h2"), NT)
            sp.dma_start(res_nat[:, 0:NT - 1, :], table_gat1[0:(NT - 1) * P, 0:D].rearrange("(m p) d -> p m d", p=P)).then_inc(s("res_loaded"), 16)
            sp.dma_start(res_nat[0:W, NT - 1, :], table_gat1[(NT - 1) * P:NP, 0:D]).then_inc(s("res_loaded"), 16)
            for m in range(NT):
                sp.wait_ge(s("out_ready"), m + 1)
                sp.dma_start(out[m * P:m * P + real(m), :], natv[0:real(m), m, 0:D]).then_inc(s("out_stored"), 16)
            sp.wait_ge(s("out_stored"), 16 * NT)

        @block.gpsimd
        def _(pool):
            g = nc.gpsimd
            def sort_edges():
                o = [512]

                def buf(width):
                    o[0] += width
                    return onehot_w[:, o[0] - width:o[0]]

                row, eq, lower = buf(P), buf(P), buf(P)
                NBK = 64
                assert FAR // W == NBK - 1 and NBK > NW
                bucket, hot, run, count, wide = buf(NBK), buf(NBK), buf(NBK), buf(NBK), buf(P)
                cold = buf(8)
                row_t = buf(P).bitcast(I32)
                col_t = buf(4).bitcast(I32)
                once = [0]

                def link1(ins):
                    once[0] += 1
                    ins.then_inc(s("sort_once"), 1)
                    pool.wait_ge(s("sort_once"), once[0])

                link1(g.memset(lower, 1.0))
                link1(g.affine_select(out=lower, in_=lower, compare_op=ALU.is_gt, fill=0.0, base=0, pattern=[[-1, P]], channel_multiplier=1))
                link1(g.iota(bucket, [[1, NBK]], base=0, channel_multiplier=0, allow_small_or_imprecise_dtypes=True))
                link1(g.memset(run, 0.0))
                link1(g.memset(wide, 0.0))
                link1(g.tensor_copy(wide[0:EP, 0:NB], below))
                link1(g.partition_all_reduce(count, wide[:, 0:NBK], P, bass.bass_isa.ReduceOp.add))
                link1(g.tensor_copy(run[:, 1:1 + NB], count[:, 0:NB]))
                link1(g.memset(run[:, NBK - 1:NBK], float(E)))
                link1(g.memset(pad_i[:, 0:P], NBK - 1))
                pool.dma_start(edge_win[0:E].rearrange("(p k) -> p k", p=EP), win_all).then_inc(s("sort_dma"), 16)
                pool.dma_start(edge_win[E:ET * P - P].rearrange("(o c) -> o c", o=1), pad_i[:, 0:EPAD - P]).then_inc(s("sort_dma"), 16)
                pool.wait_ge(s("sort_dma"), 32)
                ws = edge_win.rearrange("(t e) -> t e", e=P)
                steps = 10 + 7 + 6
                with pool.Fori(0, ET - 1) as i:
                    at = [0]

                    def link(ins):
                        at[0] += 1
                        ins.then_inc(s("sort_step"), 1)
                        pool.wait_ge(s("sort_step"), i * steps + at[0])
                        pool.sem_inc(s("idx_passed"), 1)

                    pool.dma_start(row_t, ws[bass.ds(i, 1), :].broadcast_to([P, P])).then_inc(s("sort_dma"), 16)
                    for j, table in enumerate((ws, edge_src, edge_dst)):
                        pool.dma_start(col_t[:, j:j + 1], table[bass.ds(i, 1), :].rearrange("o e -> e o")).then_inc(s("sort_dma"), 16)
                    pool.wait_ge(s("sort_dma"), i * 96 + (32 + 64))
                    pool.sem_inc(s("idx_passed"), 1)
                    link(g.tensor_copy(row, row_t))
                    link(g.tensor_copy(cold[:, 0:1], col_t[:, 0:1]))
                    link(g.tensor_scalar(eq, row, cold[:, 0:1], None, ALU.is_equal))
                    link(g.tensor_tensor(eq, eq, lower, ALU.mult))
                    h = P // 2
                    while h:
                        link(g.tensor_tensor(eq[:, 0:h], eq[:, 0:h], eq[:, h:2 * h], ALU.add))
                        h //= 2
                    link(g.tensor_scalar(hot, bucket, cold[:, 0:1], None, ALU.is_equal))
                    link(g.tensor_tensor(wide[:, 0:NBK], hot, run, ALU.mult))
                    h = NBK // 2
                    while h:
                        link(g.tensor_tensor(wide[:, 0:h], wide[:, 0:h], wide[:, h:2 * h], ALU.add))
                        h //= 2
                    link(g.tensor_tensor(cold[:, 1:2], eq[:, 0:1], wide[:, 0:1], ALU.add))
                    link(g.tensor_copy(col_t[:, 3:4], cold[:, 1:2]))
                    link(g.partition_all_reduce(count, hot, P, bass.bass_isa.ReduceOp.add))
                    link(g.tensor_tensor(run, run, count, ALU.add))
                    assert at[0] == steps
                    for j, table in ((1, sorted_src), (2, sorted_dst)):
                        g.indirect_dma_start(table, bass.IndirectOffsetOnAxis(ap=col_t[:, 3:4], axis=0), col_t[:, j:j + 1], None).then_inc(s("sort_dma"), 16)
                    pool.wait_ge(s("sort_dma"), i * 96 + (32 + 96))
                for a_, b_ in ((edge_src, sorted_src), (edge_dst, sorted_dst)):
                    pool.dma_start(a_[0:ET - 1, :], b_[0:(ET - 1) * P, :].rearrange("(t e) o -> t (e o)", e=P)).then_inc(s("sort_dma"), 16)
                pool.wait_ge(s("sort_dma"), 32 + (ET - 1) * 96 + 32)

            g.memset(pad_i[:, 0:2 * P], 0).then_inc(s("pads"), 1)
            g.memset(pad_i[:, 2 * P:4 * P], FAR).then_inc(s("pads"), 1)
            g.iota(iota_v, [[1, V]], base=0, channel_multiplier=0, allow_small_or_imprecise_dtypes=True).then_inc(s("consts"), 1)
            g.iota(iota_w[:, :], [[1, W]], base=0, channel_multiplier=0, allow_small_or_imprecise_dtypes=True).then_inc(s("consts"), 1)
            g.iota(iota_c, [[VR, VC]], base=0, channel_multiplier=1, allow_small_or_imprecise_dtypes=True).then_inc(s("consts"), 1)
            g.iota(iota_b, [[1, 1]], base=1, channel_multiplier=1, allow_small_or_imprecise_dtypes=True).then_inc(s("consts"), 1)
            g.memset(ones[:, :], 1.0).then_inc(s("consts"), 1)
            g.memset(ident[:, :], 0.0).then_inc(s("ident_zero"), 1)
            pool.wait_ge(s("ident_zero"), 1)
            g.affine_select(out=ident[:, :], in_=ident[:, :], compare_op=ALU.not_equal, fill=1.0, base=0,
                            pattern=[[-1, P]], channel_multiplier=1).then_inc(s("ident_made"), 1)
            pool.wait_ge(s("ident_made"), 1)
            g.tensor_copy(ident_b[:, :], ident[:, :]).then_inc(s("consts"), 1)
            pool.wait_ge(s("edges_in"), 64)
            pool.wait_ge(s("order_known"), 1)
            unordered = pool.value_load(flag_i[0:1, 0:1], min_val=0, max_val=E)
            with pool.If(unordered > 0):
                sort_edges()
            pool.wait_ge(s("visit_rows_known"), 1)
            for c in range(VC):
                for k, t in enumerate((edge_src, edge_dst)):
                    g.indirect_dma_start(visit_rows_i[:, k, c, :], None, t,
                                         bass.IndirectOffsetOnAxis(ap=row_i[:, c:c + 1], axis=0)).then_inc(s("visit_rows"), 16)

            def exact_max(n, table, heads):
                m_all = big[0:1, 0:NW * W * heads].rearrange("p (w c) -> p w c", w=NW)
                cand = onehot_w[:, 0:W * heads]
                cand3 = cand.rearrange("p (c h) -> p c h", h=heads)
                red = onehot_w[:, H * W:H * W + W * heads]
                red2 = onehot_w[:, 6 * H * W:6 * H * W + W * heads]
                hot_f = onehot_w[:, 2 * H * W:2 * H * W + W]
                off_f = onehot_w[:, 3 * H * W:3 * H * W + W]
                hot, off = (b.rearrange("p (c h) -> p c h", h=1) for b in (hot_f, off_f))
                col = onehot_w[:, 4 * H * W:4 * H * W + 1]
                own = onehot_w[:, 5 * H * W:5 * H * W + NT * heads].rearrange("p (m h) -> p m h", h=heads)
                g.memset(m_all, -3.0e38).then_inc(s(f"max_step{n}"), 1)
                pool.wait_ge(s(f"table{n}"), 16 * NT)
                pool.wait_ge(s(f"max_step{n}"), 1)
                steps = 10
                with pool.Fori(0, V) as i:
                    at = [0]

                    def link(ins):
                        at[0] += 1
                        ins.then_inc(s(f"max_step{n}"), 1)
                        pool.wait_ge(s(f"max_step{n}"), i * steps + (1 + at[0]))
                        pool.sem_inc(s("idx_passed"), 1)

                    link(g.tensor_copy(idx[:, 0:1], src_of[:, bass.ds(i, 1)]))
                    g.indirect_dma_start(ringv[:, 0, 0:D + heads], None, table,
                                         bass.IndirectOffsetOnAxis(ap=idx[:, 0:1], axis=0)).then_inc(s(f"max_dma{n}"), 16)
                    link(g.tensor_copy(col, dst_in[:, bass.ds(i, 1)]))
                    link(g.tensor_scalar(hot_f, iota_w[:, :], col, None, ALU.is_equal))
                    link(g.tensor_scalar(off_f, hot_f, 3.0e38, -3.0e38, ALU.mult, ALU.add))
                    pool.wait_ge(s(f"max_dma{n}"), i * 16 + 16)
                    pool.sem_inc(s("idx_passed"), 1)
                    link(g.tensor_tensor(cand3, hot.broadcast_to([P, W, heads]),
                                         ringv[:, 0:1, D:D + heads].broadcast_to([P, W, heads]), ALU.mult))
                    link(g.tensor_tensor(cand3, cand3, off.broadcast_to([P, W, heads]), ALU.add))
                    link(g.partition_all_reduce(red, cand, P, bass.bass_isa.ReduceOp.max))
                    win = pool.value_load(win_of[0:1, bass.ds(i, 1)], min_val=0, max_val=NW - 1)
                    link(g.tensor_copy(red[0:1, :].rearrange("p (o c) -> p o c", o=1), m_all[0:1, bass.ds(win, 1), :]))
                    link(g.partition_all_reduce(red2, red, P, bass.bass_isa.ReduceOp.max))
                    link(g.tensor_copy(m_all[0:1, bass.ds(win, 1), :], red2[0:1, :].rearrange("p (o c) -> p o c", o=1)))
                    assert at[0] == steps
                flat = node_max[0:NP * heads]
                pool.dma_start(flat.rearrange("(o c) -> o c", o=1), big[0:1, 0:NP * heads]).then_inc(s(f"max_dma{n}"), 16)
                pool.wait_ge(s(f"max_dma{n}"), V * 16 + 16)
                edge = (NT - 1) * P * heads
                pool.dma_start(own[:, 0:NT - 1, :], flat[0:edge].rearrange("(m p h) -> p m h", p=P, h=heads)).then_inc(s(f"max_dma{n}"), 16)
                pool.dma_start(own[0:W, NT - 1, :], flat[edge:NP * heads].rearrange("(p h) -> p h", h=heads)).then_inc(s(f"max_dma{n}"), 16)
                pool.wait_ge(s(f"max_dma{n}"), V * 16 + 16 + 32)
                sm = nat_of(smax_nat, 0, NT, heads)
                g.tensor_copy(sm[:, 0:NT - 1, :], own[:, 0:NT - 1, :]).then_inc(s(f"max_step{n}"), 1)
                g.tensor_copy(sm[0:W, NT - 1:NT, :], own[0:W, NT - 1:NT, :]).then_inc(s(f"max_step{n}"), 1)
                pool.wait_ge(s(f"max_step{n}"), 1 + V * steps + 2)

            def settle_max(n, table, heads):
                pool.wait_ge(s(f"spread_known{n}"), 1)
                wide = pool.value_load(flag_i[0:1, n - 2:n - 1], min_val=0, max_val=1)
                with pool.If(wide > 0):
                    exact_max(n, table, heads)
                pool.sem_inc(s(f"max_settled{n}"), 1)

            def gather_pass(n, table, width, spare_free=None):
                def group(gr, q, _):
                    if not early(gr, Q):
                        pool.wait_ge(s(f"agg_ready{n}"), (gr - (Q - 1)) * U)
                    if early(gr, Q) and gr == 2 and spare_free:
                        pool.wait_ge(*spare_free)
                    g.tensor_copy(idx[:, q * U:q * U + U], src_of[:, bass.ds(gr * U, U)]).then_inc(s(f"idx{n}"), 1)
                    pool.wait_ge(s(f"idx{n}"), gr + 1)
                    pool.sem_inc(s("idx_passed"), 1)
                    for u in range(U):
                        g.indirect_dma_start(ring_rows(n, q)[:, u, 0:width], None, table,
                                             bass.IndirectOffsetOnAxis(ap=idx[:, q * U + u:q * U + u + 1], axis=0)).then_inc(s(f"rows_{q}"), 16)

                each_group(pool, group)

            pool.wait_ge(s("setup_done"), 2)
            gather_pass(0, table_sage[0], D)
            pool.wait_ge(s("table1"), 16 * NT)
            gather_pass(1, table_sage[1], D)
            pool.wait_ge(s("table2"), 16 * NT)
            gather_pass(2, table_sage[2], D)
            settle_max(3, table_gat1, H)
            pool.wait_ge(s("table3"), 16 * NT)
            gather_pass(3, table_gat1, RW, (s("self_sum3"), KD * NT))
            pool.wait_ge(s("h2"), NT)
            settle_max(4, table_gat2, 1)
            pool.wait_ge(s("table4"), 16 * NT)
            gather_pass(4, table_gat2, D + 1, (s("self_sum4"), KD * NT))

        @block.tensor
        def _(pe):
            t = nc.tensor
            pe.wait_ge(s("consts"), 6)
            pe.wait_ge(s("below_step"), NB)
            t.matmul(ps_d[0:NB, 0:1], lhsT=below, rhs=ones[0:EP, 0:1], start=True, stop=True).then_inc(s("bounds"), 1)
            pe.wait_ge(s("viol"), 1)
            t.matmul(ps_n[0:1, 8:10], lhsT=ones[0:EP, 0:1], rhs=viol, start=True, stop=True).then_inc(s("viol_sum"), 1)
            pe.wait_ge(s("cmp"), 1)
            t.matmul(ps[:, 0, 0:V], lhsT=ones[0:NB, :], rhs=cmp_bv, start=True, stop=True).then_inc(s("windows"), 1)
            for c in range(VC):
                t.matmul(ps_n[0:VR, c:c + 1], lhsT=cmp_bv[:, c * VR:(c + 1) * VR], rhs=ones[0:NB, 0:1],
                         start=True, stop=True).then_inc(s("windows"), 1)
            pe.wait_ge(s("visit_rows_f"), 1)
            for c in range(VC):
                for k in range(2):
                    t.transpose(ps[:, 1 + k, c * VR:(c + 1) * VR], visit_rows[:, k, c, :], ident[0:VR, 0:VR]).then_inc(s("visit_cols"), 1)

            turned = [0]

            def turn(src, gate, m):
                pe.wait_ge(*gate)
                if turned[0] >= 2:
                    pe.wait_ge(s("turned_out"), turned[0] - 1)
                b = turned[0] % 2
                for k in range(KD):
                    i = t.transpose(ps_t[:, b, k * P:k * P + rows(m)], src[0:rows(m), m, k * P:(k + 1) * P], ident[0:rows(m), 0:rows(m)])
                i.then_inc(s("turned"), 1)
                turned[0] += 1

            def sage_self(n):
                for m in range(NT):
                    turn(x_nat if n == 0 else natv, (s("x_loaded"), 32) if n == 0 else (s(f"row_ready{n}"), m + 1), m)
                pe.wait_ge(s("w_loaded"), 16 * 16)
                for m in range(NT):
                    pe.wait_ge(s("turned_out"), NT * n + m + 1)
                    if m >= 2:
                        pe.wait_ge(s(f"self_out{n}"), m - 1)
                    bank = ps_d if m % 2 == 0 else ps_n
                    for k in range(KD):
                        i = t.matmul(bank[0:rows(m), 0:D], lhsT=colsv[:, k, m * P:m * P + rows(m)], rhs=w_sage[:, 2 * n, k, :],
                                     start=(k == 0), stop=(k == KD - 1))
                    i.then_inc(s(f"self{n}"), 1)

            def sage_pass(n):
                def group(gr, q, rows_done):
                    half = q % 2
                    pe.wait_ge(s(f"rows_{q}"), rows_done + rows_before(n, q))
                    pe.wait_ge(s(f"oh{n}"), gr + 1)
                    if n == 0:
                        if not early(gr, 2):
                            pe.wait_ge(s("den_step0"), (gr - 1) * U)
                        for u in range(U):
                            i = t.matmul(deg_bank[half][0:W, u:u + 1], lhsT=oh[:, half, u, :], rhs=ones[:, 0:1], start=True, stop=True)
                        i.then_inc(s("den_ready0"), 1)
                    for u in range(U):
                        bank, at = 2 * half + u // 4, (u % 4) * KD * W
                        if not early(gr, 2) and u % 4 == 0:
                            pe.wait_ge(s(f"added{n}"), gr * U + (u + 4 - 2 * U))
                        for k in range(KD):
                            i = t.matmul(ps[:, bank, at + k * W:at + (k + 1) * W], lhsT=ring_rows(n, q)[:, u, k * P:(k + 1) * P],
                                         rhs=oh[:, half, u, :], start=True, stop=True)
                        i.then_inc(s(f"agg_ready{n}"), 1)

                each_group(pe, group)

            def sage_neigh(n):
                pe.wait_ge(s(f"added{n}"), V)
                for m in range(NT):
                    if m >= QUAD:
                        pe.wait_ge(s(f"neigh_out{n}"), m - QUAD + 1)
                    for k in range(KD):
                        i = t.matmul(ps[0:rows(m), m % QUAD, 0:D], lhsT=sums_sage[:, k, m * P:m * P + rows(m)], rhs=w_sage[:, 2 * n + 1, k, :],
                                     start=(k == 0), stop=(k == KD - 1))
                    i.then_inc(s(f"neigh{n}"), 1)

            def gat_pass(n, heads):
                def ahead(gr, half):
                    if not early(gr, 1):
                        pe.wait_ge(s(f"oht{n}"), gr)
                    pe.wait_ge(s(f"oh{n}"), gr + 1)
                    pe.sem_inc(s("oh_passed"), 1)
                    for u in range(U):
                        i = t.transpose(ps_t[0:W, 0, :].bitcast(BF16)[:, u * P:(u + 1) * P], ohb[:, half, u, :], ident_b[:, :])
                    i.then_inc(s(f"ohp{n}"), 1)

                def lookup(gr, half):
                    regs = windows_of(mybir.EngineType.PE, gr)
                    if not early(gr, 1):
                        pe.wait_ge(s(f"zs{n}"), (gr - 1) * 4 + 1)
                    pe.wait_ge(s(f"oht{n}"), gr + 1)
                    pe.sem_inc(s("oh_passed"), 1)
                    for u in range(U):
                        i = t.matmul(ps_d[:, u * 6 * heads:(u + 1) * 6 * heads], lhsT=oht[:, half, u * P:(u + 1) * P],
                                     rhs=parts_v(heads)[:, bass.ds(regs[u], 1), :, :], start=True, stop=True)
                    i.then_inc(s(f"look{n}"), 1)

                def denom(gr, half):
                    if not early(gr, 2):
                        pe.wait_ge(s(f"den_step{n}"), (gr - 1) * U)
                    pe.wait_ge(s(f"wparts{n}"), gr + 1)
                    for u in range(U):
                        i = t.matmul(den_bank[half][0:W, u * 3 * heads:(u + 1) * 3 * heads], lhsT=ohb[:, half, u, :],
                                     rhs=w_parts_v(heads, half)[:, u, :, :], start=True, stop=True)
                    i.then_inc(s(f"den_ready{n}"), 1)

                def agg(gr, q, us):
                    for u in us:
                        if u % 4 == 0:
                            pe.wait_ge(s(f"ohw{n}"), gr * 2 + (u // 4 + 1))
                        if not early(gr, 1) or u >= QUAD:
                            pe.wait_ge(s(f"added{n}"), gr * U + (u - QUAD + 1))
                        for k in range(KD):
                            i = t.matmul(ps[:, u % QUAD, k * heads * W:(k + 1) * heads * W], lhsT=ring_rows(n, q)[:, u, k * P:(k + 1) * P],
                                         rhs=ohw_v(heads)[:, q % 2, u, :], start=True, stop=True)
                        i.then_inc(s(f"agg_ready{n}"), 1)

                def step(gr, q, rows_done):
                    half = q % 2
                    last = isinstance(gr, int) and gr == NG - 1
                    pe.wait_ge(s(f"rows_{q}"), rows_done + rows_before(n, q))
                    agg(gr, q, range(0, 1))
                    if not last:
                        ahead(gr + 1, 1 - half)
                    denom(gr, half)
                    agg(gr, q, range(1, 3))
                    if not last:
                        lookup(gr + 1, 1 - half)
                    agg(gr, q, range(3, U))

                ahead(0, 0)
                lookup(0, 0)
                each_group(pe, step)

            for n in range(3):
                sage_self(n)
                pe.wait_ge(s(f"self_out{n}"), NT)
                sage_pass(n)
                sage_neigh(n)

            for m in range(NT):
                turn(natv, (s("ln0"), m + 1), m)
            pe.wait_ge(s("turned_out"), 4 * NT)
            pe.wait_ge(s("att1"), 2)
            for m in range(NT):
                for k in range(KD):
                    i = t.matmul(ps_d[0:rows(m), m * 2 * H:(m + 1) * 2 * H], lhsT=colsv[:, k, m * P:m * P + rows(m)], rhs=att1v[:, k, :],
                                 start=(k == 0), stop=(k == KD - 1))
            i.then_inc(s("scores3"), 1)

            def bound(n, heads):
                pe.wait_ge(s(f"smax_col{n}"), 1)
                t.transpose(ps_n[0:2 * heads, 0:P], ext[:, 0:2 * heads], ident[:, :]).then_inc(s(f"smax_row{n}"), 1)
                pe.wait_ge(s(f"smax_diag{n}"), 1)
                t.matmul(ps_n[:, P:P + 2 * heads], lhsT=ones[0:2 * heads, :], rhs=ext[0:2 * heads, 16:16 + 2 * heads], start=True, stop=True).then_inc(s(f"smax_all{n}"), 1)

            def self_terms(n, heads):
                for m in range(NT):
                    pe.wait_ge(s(f"diag{n}"), m + 1)
                    for k in range(KD):
                        b = (2 * m + k) % QUAD
                        if 2 * m + k >= QUAD:
                            pe.wait_ge(s(f"self_sum_out{n}"), 2 * m + k - QUAD + 1)
                        t.matmul(ps[:, b, 0:heads * P].rearrange("p (h n) -> p h n", h=heads)[:, :, 0:rows(m)],
                                 lhsT=natv[0:rows(m), m, k * P:(k + 1) * P],
                                 rhs=diag_v(heads)[0:rows(m), m % 2, :, 0:rows(m)], start=True, stop=True).then_inc(s(f"self_sum{n}"), 1)

            bound(3, H)
            self_terms(3, H)
            gat_pass(3, H)

            pe.wait_ge(s("w1_loaded"), 16)
            nblk = 0
            for b0 in range(0, NT, 4):
                bt = range(b0, min(b0 + 4, NT))
                width = sum(rows(m) for m in bt)
                for m in bt:
                    pe.wait_ge(s("rdiag"), m + 1)
                    if m >= 2:
                        pe.wait_ge(s("rden_out"), m - 1)
                    t.matmul(ps_t[:, m % 2, :].rearrange("p (h n) -> p h n", h=H)[:, :, 0:rows(m)], lhsT=ones[0:rows(m), :],
                             rhs=diag_v(H)[0:rows(m), m % 2, :, 0:rows(m)], start=True, stop=True).then_inc(s("rden_b"), 1)
                for h in range(H):
                    for f in range(KD):
                        if nblk >= QUAD:
                            pe.wait_ge(s("proj_out"), nblk - QUAD + 1)
                        for k in range(KD):
                            i = t.matmul(ps[:, nblk % QUAD, 0:width], lhsT=w1_sb[:, k, h * D + f * P:h * D + (f + 1) * P],
                                         rhs=bigv[:, k * H + h, b0 * P:b0 * P + width], start=(k == 0), stop=(k == KD - 1))
                        i.then_inc(s("proj"), 1)
                        nblk += 1

            pe.wait_ge(s("w2_loaded"), 16)
            pe.wait_ge(s("normed"), KH)
            for m in range(NT):
                if m >= QUAD:
                    pe.wait_ge(s("h2_out"), m - QUAD + 1)
                for c in range(KH):
                    i = t.matmul(ps[0:rows(m), m % QUAD, 0:D], lhsT=bigv[:, c, m * P:m * P + rows(m)], rhs=w2_sb[:, ch_order[c], :],
                                 start=(c == 0), stop=(c == KH - 1))
                i.then_inc(s("h2"), 1)
            bound(4, 1)
            self_terms(4, 1)
            gat_pass(4, 1)
            pe.wait_ge(s("added4"), V)
            for m in range(NT):
                if m >= QUAD:
                    pe.wait_ge(s("y_out"), m - QUAD + 1)
                for k in range(KD):
                    i = t.transpose(ps[0:rows(m), m % QUAD, k * P:(k + 1) * P], bigv[:, k, m * P:m * P + rows(m)], ident[:, :])
                i.then_inc(s("y_turned"), 1)

        @block.scalar
        def _(act):
            A = nc.scalar
            done = [0]

            def link(ins):
                done[0] += 1
                ins.then_inc(s("act_step"), 1)
                act.wait_ge(s("act_step"), done[0])

            turned = [0]

            def turn_out(m):
                act.wait_ge(s("turned"), turned[0] + 1)
                A.activation(colsv[:, :, m * P:m * P + rows(m)],
                             ps_t[:, turned[0] % 2, 0:KD * P].rearrange("p (k n) -> p k n", k=KD)[:, :, 0:rows(m)], ACT.Copy).then_inc(s("turned_out"), 1)
                turned[0] += 1

            def gat_pass(n, heads):
                act.preload_act_table(ACT.Exp)

                def step(gr, q, _):
                    half = q % 2
                    act.wait_ge(s(f"ohp{n}"), gr + 1)
                    A.activation(oht[:, half, :], ps_t[0:W, 0, :].bitcast(BF16), ACT.Copy).then_inc(s(f"oht{n}"), 1)
                    act.wait_ge(s(f"z{n}"), gr + 1)
                    if not early(gr, 2):
                        act.wait_ge(s(f"agg_ready{n}"), (gr - 1) * U)
                    A.activation(w_buf[:, half * U * heads:(half + 1) * U * heads], z_buf[:, 2 * U * H:2 * U * H + U * heads], ACT.Exp).then_inc(s(f"w{n}"), 1)
                    A.activation(w_parts_v(heads, half)[:, :, 0, :], z_buf[:, 2 * U * H:2 * U * H + U * heads].rearrange("p (u h) -> p u h", h=heads),
                                 ACT.Exp).then_inc(s(f"w{n}"), 1)

                each_group(act, step)

            for n in range(3):
                for m in range(NT):
                    turn_out(m)
                if n < 2:
                    for m in range(NT):
                        act.wait_ge(s(f"neigh_out{n}"), m + 1)
                        A.activation(natv[0:rows(m), m, 0:D], natv[0:rows(m), m, 0:D], ACT.Relu).then_inc(s(f"row_ready{n + 1}"), 1)
            act.wait_ge(s("ln_stats0"), 1)
            A.activation(rstd[:, :], rstd[:, :], ACT.Sqrt).then_inc(s("ln_sqrt0"), 1)
            for m in range(NT):
                turn_out(m)

            def self_terms(n, heads):
                act.wait_ge(s(f"self_z{n}"), 1)
                A.activation(w_self[:, 0:NT * heads], e_nat[:, 0:NT * heads], ACT.Exp).then_inc(s(f"self_w{n}"), 1)
                for m in range(NT):
                    for k in range(KD):
                        act.wait_ge(s(f"self_sum{n}"), 2 * m + k + 1)
                        A.activation(bigv[:, k * heads:(k + 1) * heads, m * P:m * P + rows(m)],
                                     ps[:, (2 * m + k) % QUAD, 0:heads * P].rearrange("p (h n) -> p h n", h=heads)[:, :, 0:rows(m)],
                                     ACT.Copy).then_inc(s(f"self_sum_out{n}"), 1)

            self_terms(3, H)
            gat_pass(3, H)
            nblk = 0
            for b0 in range(0, NT, 4):
                bt = range(b0, min(b0 + 4, NT))
                width = sum(rows(m) for m in bt)
                for m in bt:
                    act.wait_ge(s("rden_b"), m + 1)
                    if b0 >= 8:
                        act.wait_ge(s("proj_out"), (b0 // 4 - 1) * KH)
                    A.activation(rb_v(b0 // 4)[:, :, (m - b0) * P:(m - b0) * P + rows(m)],
                                 ps_t[:, m % 2, :].rearrange("p (h n) -> p h n", h=H)[:, :, 0:rows(m)], ACT.Copy).then_inc(s("rden_out"), 1)
                for h in range(H):
                    for f in range(KD):
                        act.wait_ge(s("proj_out"), nblk + 1)
                        nblk += 1
                        wr = min(width, N - b0 * P)
                        if nblk > 4:
                            act.wait_ge(s("col_sums"), nblk - 4)
                        A.activation(junk_row((nblk - 1) % 4)[:, 0:wr], bigv[:, f * H + h, b0 * P:b0 * P + wr], ACT.Copy,
                                     accum_out=gn_sum[:, (f * H + h) * 8 + b0 // 4:(f * H + h) * 8 + b0 // 4 + 1]).then_inc(s("col_sums"), 1)
            act.wait_ge(s("gn_mean"), 1)
            for c in range(KH):
                if c >= 2:
                    act.wait_ge(s("gn_var"), c - 1)
                A.activation(nat[:, (c % 2) * N:(c % 2 + 1) * N], bigv[:, c, 0:N], ACT.Square, bias=gn_v[:, KH + c:KH + c + 1],
                             accum_out=gn_v[:, 2 * KH + c:2 * KH + c + 1]).then_inc(s("gn_var"), 1)
            act.wait_ge(s("gn_var_in"), 1)
            A.activation(gn_v[:, 3 * KH:4 * KH], gn_v[:, 3 * KH:4 * KH], ACT.Sqrt).then_inc(s("gn_sqrt"), 1)
            act.wait_ge(s("gn_scale"), 1)
            for c in range(KH):
                A.activation(bigv[:, c, :], bigv[:, c, :], ACT.Relu, bias=gn_v[:, 5 * KH + c:5 * KH + c + 1],
                             scale=gn_v[:, 4 * KH + c:4 * KH + c + 1]).then_inc(s("normed"), 1)
            self_terms(4, 1)
            gat_pass(4, 1)
            act.wait_ge(s("ln_stats1"), 1)
            A.activation(rstd[:, :], rstd[:, :], ACT.Sqrt).then_inc(s("ln_sqrt1"), 1)

        @block.vector
        def _(v):
            X = nc.vector
            done = [0]

            def link(ins):
                done[0] += 1
                ins.then_inc(s("dve_step"), 1)
                v.wait_ge(s("dve_step"), done[0])

            X.memset(x_nat[:, NT - 1, :], 0.0).then_inc(s("x_cleared"), 1)
            X.memset(s_nat[:, :], 0.0)
            X.memset(r_nat[:, :], 0.0)
            X.memset(den[:, :], 0.0)
            X.memset(mv[:, :], 1.0)
            X.memset(w_self[:, :], 0.0)
            X.memset(score_win[:, :], 0.0)
            X.memset(rden[:, :], 0.0)
            X.memset(sums_sage, 0.0)
            link(X.memset(small_i[:, :], 0))
            v.wait_ge(s("dst_loaded"), 16)
            v.wait_ge(s("next_loaded"), 16)
            link(X.tensor_copy(dst_f, dst_i))
            link(X.tensor_copy(next_f[0:EP - 1, :], next_i[0:EP - 1, :]))
            X.tensor_scalar(win_all, dst_i, W.bit_length() - 1, None, ALU.arith_shift_right)
            link(X.memset(viol, 0.0))
            X.tensor_tensor(junk[:, 0, 0:EK - 1], dst_f[:, 0:EK - 1], dst_f[:, 1:EK], ALU.is_gt)
            link(X.tensor_tensor(viol[0:EP - 1, 1:2], dst_f[0:EP - 1, EK - 1:EK], next_f[0:EP - 1, :], ALU.is_gt))
            X.tensor_reduce(viol[:, 0:1], junk[:, 0, 0:EK - 1], AX.X, ALU.add).then_inc(s("viol"), 1)
            v.wait_ge(s("viol"), 1)
            for b in range(NB):
                if b >= 8:
                    v.wait_ge(s("below_step"), b - 7)
                X.tensor_scalar(junk[:, b % 8, :], dst_f, float(W * (b + 1)), 0.0, ALU.is_lt, ALU.add,
                                accum_out=below[:, b:b + 1]).then_inc(s("below_step"), 1)
            v.wait_ge(s("consts"), 6)
            v.wait_ge(s("bounds"), 1)
            link(X.tensor_copy(first_i, ps_d[0:NB, 0:1]))
            v.wait_ge(s("viol_sum"), 1)
            link(X.tensor_reduce(flag_f, ps_n[0:1, 8:10], AX.X, ALU.add))
            X.tensor_copy(flag_i[0:1, 0:1], flag_f).then_inc(s("order_known"), 1)
            link(X.tensor_scalar(tile_i, first_i, 7, None, ALU.arith_shift_right))
            link(X.tensor_copy(tile_f, tile_i))
            link(X.tensor_tensor(event, tile_f, iota_b[0:NB, :], ALU.add))
            X.tensor_scalar(cmp_bv, iota_v[0:NB, :], event, None, ALU.is_ge).then_inc(s("cmp"), 1)
            v.wait_ge(s("windows"), 1 + VC)
            X.tensor_tensor(row_i, iota_c[0:VR, :], ps_n[0:VR, 0:VC], ALU.subtract).then_inc(s("visit_rows_known"), 1)
            X.tensor_copy(win_of[:, :], ps[0:1, 0, 0:V]).then_inc(s("win_known"), 1)
            link(X.tensor_scalar(win_f, ps[:, 0, 0:V], float(W), None, ALU.mult))
            v.wait_ge(s("visit_rows"), 16 * 2 * VC)
            X.tensor_copy(visit_rows, visit_rows_i).then_inc(s("visit_rows_f"), 1)
            v.wait_ge(s("visit_cols"), 2 * VC)
            X.tensor_copy(src_of[:, :], ps[:, 1, 0:V])
            link(X.tensor_tensor(dst_in[:, :], ps[:, 2, 0:V], win_f, ALU.subtract))
            X.memset(small[:, 0:16], 0.0).then_inc(s("setup_done"), 2)

            turned = [0]

            def one_hots(n, gr, half):
                X.tensor_tensor((oh if n < 3 else ohb)[:, half, :, :], iota_w[:, :].rearrange("p (u w) -> p u w", u=1).broadcast_to([P, U, W]),
                                dst_in[:, bass.ds(gr * U, U)].rearrange("p (u w) -> p u w", w=1).broadcast_to([P, U, W]),
                                ALU.is_equal).then_inc(s(f"oh{n}"), 1)

            def sage_pass(n):
                def group(gr, q, _):
                    half = q % 2
                    regs = windows_of(mybir.EngineType.DVE, gr)
                    if not (isinstance(gr, int) and gr == NG - 1):
                        if not early(gr, 1):
                            v.wait_ge(s(f"agg_ready{n}"), gr * U)
                        one_hots(n, gr + 1, 1 - half)
                    if n == 0:
                        v.wait_ge(s("den_ready0"), gr + 1)
                    for u in range(U):
                        if u % 4 == 0:
                            v.wait_ge(s(f"agg_ready{n}"), gr * U + (u + 4))
                        if not (early(gr, 1) and u == 0):
                            v.wait_ge(s(f"added{n}"), gr * U + u)
                        place = sums_sage.rearrange("p k (w c) -> p k w c", c=W)[:, :, bass.ds(regs[u], 1), :]
                        bank, at = 2 * half + u // 4, (u % 4) * KD * W
                        X.tensor_tensor(place, place, ps[:, bank, at:at + KD * W].rearrange("p (k o c) -> p k o c", k=KD, o=1),
                                        ALU.add).then_inc(s(f"added{n}"), 1)
                        if n == 0:
                            if not (early(gr, 1) and u == 0):
                                v.wait_ge(s("den_step0"), gr * U + u)
                            dplace = den_v(1)[:, bass.ds(regs[u], 1), :]
                            X.tensor_tensor(dplace, dplace, deg_bank[half][0:W, u:u + 1].rearrange("p (o c) -> p o c", o=1),
                                            ALU.add).then_inc(s("den_step0"), 1)

                one_hots(n, 0, 0)
                each_group(v, group)

            def by_row(dst, src, heads, to_rows):
                w = src if to_rows else dst
                r = dst if to_rows else src
                for par in range(2):
                    wins = w[:, par::2, :]
                    rws = r[par * W:(par + 1) * W, 0:wins.shape[1], :]
                    i = X.tensor_copy(rws, wins) if to_rows else X.tensor_copy(wins, rws)
                return i

            def sage_self(n):
                for m in range(NT):
                    v.wait_ge(s(f"self{n}"), m + 1)
                    bank = ps_d if m % 2 == 0 else ps_n
                    X.tensor_tensor(self_nat[0:rows(m), m, :], bank[0:rows(m), 0:D], biasv[0:rows(m), n, :], ALU.add).then_inc(s(f"self_out{n}"), 1)
                if n == 2:
                    v.wait_ge(s("self_out2"), NT)
                    link(X.tensor_tensor(self_nat[:, 0:NT - 1, :], self_nat[:, 0:NT - 1, :], x_nat[:, 0:NT - 1, :], ALU.add))
                    link(X.tensor_tensor(self_nat[0:W, NT - 1, :], self_nat[0:W, NT - 1, :], x_nat[0:W, NT - 1, :], ALU.add))

            def sage_neigh(n):
                if n == 0:
                    v.wait_ge(s("den_step0"), V)
                    link(by_row(nat_of(rden, 0, NT, 1), den_v(1), 1, True))
                    link(X.tensor_scalar(rden[:, 0:NT], rden[:, 0:NT], 1.0, None, ALU.max))
                    link(X.reciprocal(rden[:, 0:NT], rden[:, 0:NT]))
                for m in range(NT):
                    v.wait_ge(s(f"neigh{n}"), m + 1)
                    if n:
                        v.wait_ge(s(f"table{n}"), 16 * NT)
                        v.wait_ge(s("turned"), NT * (n + 1))
                    X.scalar_tensor_tensor(out=natv[0:rows(m), m, 0:D], in0=ps[0:rows(m), m % QUAD, 0:D], scalar=rden[0:rows(m), m:m + 1],
                                           in1=self_nat[0:rows(m), m, :], op0=ALU.mult, op1=ALU.add).then_inc(s(f"neigh_out{n}"), 1)
                if n < 2:
                    v.wait_ge(s(f"neigh{n}"), NT)
                    link(X.memset(sums_sage, 0.0))

            def layer_norm(k, gate, eps=EPS):
                for m in range(NT):
                    v.wait_ge(gate, m + 1)
                    i = X.bn_stats(stats[0:rows(m), m * 6:(m + 1) * 6], natv[0:rows(m), m, 0:D])
                    link(i)
                    i = X.bn_aggr(mv[0:rows(m), 2 * m:2 * m + 2], stats[0:rows(m), m * 6:(m + 1) * 6])
                link(i)
                X.tensor_scalar(rstd[:, :].rearrange("p (m o) -> p m o", o=1), mv[:, :].rearrange("p (m s) -> p m s", s=2)[:, :, 1:2],
                                eps, None, ALU.add).then_inc(s(f"ln_stats{k}"), 1)
                v.wait_ge(s(f"ln_sqrt{k}"), 1)
                link(X.reciprocal(rstd[:, :], rstd[:, :]))
                for m in range(NT):
                    X.tensor_scalar(natv[0:rows(m), m, 0:D], natv[0:rows(m), m, 0:D], mv[0:rows(m), 2 * m:2 * m + 1], rstd[0:rows(m), m:m + 1],
                                    ALU.subtract, ALU.mult).then_inc(s("ln0" if k == 0 else "out_ready"), 1)

            def scores_nat(heads):
                return s_nat[:, 0:NT * 2 * heads].rearrange("p (m s) -> p m s", s=2 * heads)

            def bounds(n, heads):
                sv = scores_nat(heads)
                link(X.memset(ext[:, :], -3.0e38))
                link(X.memset(e_nat[:, 0:2 * heads], -3.0e38))
                X.tensor_reduce(ext[:, 0:heads], sv[:, 0:NT - 1, 0:heads].rearrange("p m h -> p h m"), AX.X, ALU.max)
                link(X.tensor_reduce(ext[:, heads:2 * heads], sv[:, 0:NT - 1, 0:heads].rearrange("p m h -> p h m"), AX.X, ALU.min))
                link(X.tensor_scalar(ext[:, heads:2 * heads], ext[:, heads:2 * heads], -1.0, None, ALU.mult))
                X.tensor_copy(e_nat[0:real(NT - 1), 0:heads], sv[0:real(NT - 1), NT - 1, 0:heads])
                link(X.tensor_scalar(e_nat[0:real(NT - 1), heads:2 * heads], sv[0:real(NT - 1), NT - 1, 0:heads], -1.0, None, ALU.mult))
                X.tensor_tensor(ext[:, 0:2 * heads], ext[:, 0:2 * heads], e_nat[:, 0:2 * heads], ALU.max).then_inc(s(f"smax_col{n}"), 1)
                v.wait_ge(s(f"smax_row{n}"), 1)
                link(X.tensor_reduce(ext[0:2 * heads, 8:9], ps_n[0:2 * heads, 0:P], AX.X, ALU.max))
                X.tensor_scalar(ext[0:2 * heads, 16:16 + 2 * heads], ident[0:2 * heads, 0:2 * heads], ext[0:2 * heads, 8:9], None, ALU.mult).then_inc(s(f"smax_diag{n}"), 1)
                v.wait_ge(s(f"smax_all{n}"), 1)
                link(X.tensor_copy(ext[:, 0:2 * heads], ps_n[:, P:P + 2 * heads]))
                rv, ev = nat_of(r_nat, 0, NT, heads), nat_of(e_nat, 0, NT, heads)
                sm = nat_of(smax_nat, 0, NT, heads)
                link(X.tensor_copy(sm, ext[:, 0:heads].rearrange("p (m h) -> p m h", m=1).broadcast_to([P, NT, heads])))
                link(X.tensor_tensor(ext[0:1, 8:8 + heads], ext[0:1, 0:heads], ext[0:1, heads:2 * heads], ALU.add))
                link(X.tensor_reduce(ext[0:1, 24:25], ext[0:1, 8:8 + heads], AX.X, ALU.max))
                link(X.tensor_scalar(ext[0:1, 25:26], ext[0:1, 24:25], SPREAD, None, ALU.is_gt))
                X.tensor_copy(flag_i[0:1, n - 2:n - 1], ext[0:1, 25:26]).then_inc(s(f"spread_known{n}"), 1)
                v.wait_ge(s(f"max_settled{n}"), 1)
                link(X.tensor_tensor(sm, sm, sv[:, :, 0:heads], ALU.max))
                link(X.tensor_tensor(rv, sv[:, :, heads:2 * heads], sm, ALU.add))
                link(X.scalar_tensor_tensor(out=rv, in0=rv, scalar=SLOPE, in1=rv, op0=ALU.mult, op1=ALU.max))
                link(X.tensor_tensor(ev, sv[:, :, 0:heads], sv[:, :, heads:2 * heads], ALU.add))
                link(X.scalar_tensor_tensor(out=ev, in0=ev, scalar=SLOPE, in1=ev, op0=ALU.mult, op1=ALU.max))
                link(X.tensor_tensor(ev, ev, rv, ALU.subtract))
                X.tensor_scalar(ev, ev, 0.0, None, ALU.min).then_inc(s(f"self_z{n}"), 1)
                wv = score_v(heads)
                by_row(wv[:, :, 0:heads], sv[:, :, heads:2 * heads], heads, False)
                link(by_row(wv[:, :, heads:2 * heads], rv, heads, False))
                pv = parts_v(heads)
                for j in range(3):
                    link(X.tensor_copy(pv[:, :, j, :], wv))
                    if j < 2:
                        link(X.tensor_tensor(wv, wv, pv[:, :, j, :], ALU.subtract))
                link(X.memset(den[:, :], 0.0))

            def diagonals(n, col, heads, gate, name, ms=range(NT)):
                for m in ms:
                    if m >= 2:
                        v.wait_ge(*gate(m))
                    X.tensor_tensor(diag_v(heads)[:, m % 2, :, :], ident[:, :].rearrange("p (h n) -> p h n", h=1).broadcast_to([P, heads, P]),
                                    col[:, m * heads:(m + 1) * heads].rearrange("p (h n) -> p h n", n=1).broadcast_to([P, heads, P]),
                                    ALU.mult).then_inc(s(name), 1)

            def gat_pass(n, heads):
                def place(reg):
                    return bigv[:, 0:KD * heads, :].rearrange("p c (w n) -> p c w n", n=W)[:, :, bass.ds(reg, 1), :]

                def z_steps(gr, q, rows_done):
                    sh = ring_rows(n, q)[:, :, D:D + heads]
                    parts = ps_d[:, 0:U * 6 * heads].rearrange("p (u j s) -> p u s j", u=U, j=3)
                    look = look_buf[:, 0:U * 2 * heads].rearrange("p (u s) -> p u s", u=U)
                    zz = [z_buf[:, i * U * H:i * U * H + U * heads].rearrange("p (u h) -> p u h", u=U) for i in range(3)]

                    def looked_up():
                        v.wait_ge(s(f"look{n}"), gr + 1)
                        X.tensor_reduce(look, parts, AX.X, ALU.add).then_inc(s(f"zs{n}"), 1)

                    def added():
                        v.wait_ge(s(f"rows_{q}"), rows_done + rows_before(n, q))
                        v.wait_ge(s(f"zs{n}"), gr * 4 + 1)
                        X.tensor_tensor(zz[0], sh, look[:, :, 0:heads], ALU.add).then_inc(s(f"zs{n}"), 1)

                    def leaky():
                        v.wait_ge(s(f"zs{n}"), gr * 4 + 2)
                        X.scalar_tensor_tensor(out=zz[1], in0=zz[0], scalar=SLOPE, in1=zz[0], op0=ALU.mult, op1=ALU.max).then_inc(s(f"zs{n}"), 1)

                    def less_r():
                        v.wait_ge(s(f"zs{n}"), gr * 4 + 3)
                        X.tensor_tensor(zz[0], zz[1], look[:, :, heads:2 * heads], ALU.subtract).then_inc(s(f"zs{n}"), 1)

                    def at_most_0():
                        v.wait_ge(s(f"zs{n}"), gr * 4 + 4)
                        if not early(gr, 1):
                            v.wait_ge(s(f"w{n}"), gr * 2)
                        X.tensor_scalar(zz[2], zz[0], 0.0, None, ALU.min).then_inc(s(f"z{n}"), 1)

                    return looked_up, added, leaky, less_r, at_most_0

                def w_in_parts(gr, half):
                    w = w_buf[:, half * U * heads:(half + 1) * U * heads].rearrange("p (u h) -> p u h", h=heads)
                    rest = w_rest[:, 0:U * heads].rearrange("p (u h) -> p u h", h=heads)
                    part = [w_parts_v(heads, half)[:, :, j, :] for j in range(3)]

                    def second():
                        v.wait_ge(s(f"w{n}"), gr * 2 + 2)
                        X.tensor_tensor(rest, w, part[0], ALU.subtract).then_inc(s(f"split{n}"), 1)
                        X.tensor_tensor(part[1], w, part[0], ALU.subtract).then_inc(s(f"split{n}"), 1)

                    def third():
                        v.wait_ge(s(f"split{n}"), gr * 2 + 2)
                        X.tensor_tensor(part[2], rest, part[1], ALU.subtract).then_inc(s(f"wparts{n}"), 1)

                    return second, third

                def weigh(gr, half, part):
                    v.wait_ge(s(f"w{n}"), gr * 2 + 1)
                    us = slice(4 * part, 4 * part + 4)
                    wv = w_buf[:, half * U * heads:(half + 1) * U * heads].rearrange("p (u h w) -> p u h w", u=U, w=1)[:, us]
                    X.tensor_tensor(ohw_v(heads)[:, half, us, :].rearrange("p u (h w) -> p u h w", h=heads),
                                    ohb[:, half, us, :].rearrange("p u (h w) -> p u h w", h=1).broadcast_to([P, 4, heads, W]),
                                    wv.broadcast_to([P, 4, heads, W]), ALU.mult).then_inc(s(f"ohw{n}"), 1)

                def adds(gr, half, us, regs):
                    for u in us:
                        v.wait_ge(s(f"agg_ready{n}"), gr * U + (u + 1))
                        if not (early(gr, 1) and u == 0):
                            v.wait_ge(s(f"added{n}"), gr * U + u)
                        pl = place(regs[u])
                        X.tensor_tensor(pl, pl, ps[:, u % QUAD, 0:KD * heads * W].rearrange("p (c o n) -> p c o n", c=KD * heads, o=1),
                                        ALU.add).then_inc(s(f"added{n}"), 1)
                        if not (early(gr, 1) and u == 0):
                            v.wait_ge(s(f"den_step{n}"), gr * U + u)
                        dpl = den_v(3 * heads)[:, bass.ds(regs[u], 1), :]
                        X.tensor_tensor(dpl, dpl, den_bank[half][0:W, u * 3 * heads:(u + 1) * 3 * heads].rearrange("p (o c) -> p o c", o=1),
                                        ALU.add).then_inc(s(f"den_step{n}"), 1)

                def step(gr, q, rows_done):
                    half = q % 2
                    last = isinstance(gr, int) and gr == NG - 1
                    regs = windows_of(mybir.EngineType.DVE, gr)
                    v.wait_ge(s(f"den_ready{n}"), gr + 1)
                    if last:
                        adds(gr, half, range(U), regs)
                        return
                    z = z_steps(gr + 1, (q + 1) % Q, rows_done if q < Q - 1 else rows_done + 16 * U)
                    second, third = w_in_parts(gr + 1, 1 - half)
                    adds(gr, half, range(0, 3), regs)
                    z[0]()
                    adds(gr, half, range(3, 4), regs)
                    z[1]()
                    adds(gr, half, range(4, 5), regs)
                    z[2]()
                    if not (isinstance(gr, int) and gr >= NG - 2):
                        one_hots(n, gr + 2, half)
                    z[3]()
                    adds(gr, half, range(5, 6), regs)
                    z[4]()
                    adds(gr, half, range(6, 7), regs)
                    if not early(gr, 1):
                        v.wait_ge(s(f"agg_ready{n}"), gr * U)
                    weigh(gr + 1, 1 - half, 0)
                    second()
                    adds(gr, half, range(7, 8), regs)
                    third()
                    weigh(gr + 1, 1 - half, 1)

                one_hots(n, 0, 0)
                one_hots(n, 1, 1)
                for z in z_steps(0, 0, 16 * U):
                    z()
                weigh(0, 0, 0)
                for part in w_in_parts(0, 0):
                    part()
                weigh(0, 0, 1)
                each_group(v, step)

            def denominators(n, heads):
                v.wait_ge(s(f"added{n}"), V)
                v.wait_ge(s(f"den_step{n}"), V)
                dn = den_nat[:, 0:NT * 3 * heads].rearrange("p (m j h) -> p m j h", j=3, h=heads)
                link(X.memset(den_nat, 0.0))
                link(by_row(den_nat[:, 0:NT * 3 * heads].rearrange("p (m h) -> p m h", m=NT), den_v(3 * heads), 3 * heads, True))
                link(X.tensor_tensor(nat_of(rden, 0, NT, heads), dn[:, :, 1, :], dn[:, :, 2, :], ALU.add))
                link(X.tensor_tensor(nat_of(rden, 0, NT, heads), nat_of(rden, 0, NT, heads), dn[:, :, 0, :], ALU.add))
                link(X.tensor_tensor(rden[:, 0:NT * heads], rden[:, 0:NT * heads], w_self[:, 0:NT * heads], ALU.add))
                link(X.tensor_scalar(rden[:, 0:NT * heads], rden[:, 0:NT * heads], 1.0e-30, None, ALU.max))
                link(X.reciprocal(rden[:, 0:NT * heads], rden[:, 0:NT * heads]))

            v.wait_ge(s("w1_pre_loaded"), 16)
            v.wait_ge(s("att_loaded"), 32)
            for j in range(2):
                link(X.tensor_tensor(prod_pre, w1_pre, att_pre[:, j, :].rearrange("p (k n) -> p k n", k=1).broadcast_to([P, KD, HD]), ALU.mult))
                X.tensor_reduce(att1v[:, :, j * H:(j + 1) * H], prod_pre.rearrange("p k (h d) -> p k h d", h=H), AX.X, ALU.add).then_inc(s("att1"), 1)
                v.wait_ge(s("att1"), j + 1)

            v.wait_ge(s("w_loaded"), 16 * 16)
            for n in range(3):
                sage_self(n)
                sage_pass(n)
                sage_neigh(n)

            layer_norm(0, s("neigh_out2"))
            v.wait_ge(s("scores3"), 1)
            sv = scores_nat(H)
            link(X.tensor_copy(sv[:, 0:NT - 1, :], ps_d[:, 0:(NT - 1) * 2 * H].rearrange("p (m s) -> p m s", s=2 * H)))
            link(X.tensor_copy(sv[0:W, NT - 1, :], ps_d[0:W, (NT - 1) * 2 * H:NT * 2 * H]))
            v.wait_ge(s("ln0"), NT)
            for m in range(NT):
                X.tensor_copy(natv[0:rows(m), m, D:D + H], sv[0:rows(m), m, 0:H]).then_inc(s("gat1_row_ready"), 1)
            bounds(3, H)
            v.wait_ge(s("self_w3"), 1)
            diagonals(3, w_self, H, lambda m: (s("self_sum3"), KD * (m - 1)), "diag3")
            v.wait_ge(s("self_sum_out3"), KD * NT)
            gat_pass(3, H)
            denominators(3, H)
            nblk = 0
            for b0 in range(0, NT, 4):
                bt = range(b0, min(b0 + 4, NT))
                width = sum(rows(m) for m in bt)
                diagonals(3, rden, H, lambda m: (s("rden_b"), m - 1), "rdiag", bt)
                v.wait_ge(s("rden_out"), bt[-1] + 1)
                for h in range(H):
                    v.wait_ge(s("proj"), nblk + KD)
                    for f in range(KD):
                        X.tensor_tensor(bigv[:, f * H + h, b0 * P:b0 * P + width], ps[:, nblk % QUAD, 0:width],
                                        rb_v(b0 // 4)[:, h, 0:width], ALU.mult).then_inc(s("proj_out"), 1)
                        nblk += 1
            v.wait_ge(s("col_sums"), nblk)
            NBK = -(-NT // 4)
            gq = [gn_v[:, i * KH:(i + 1) * KH] for i in range(6)]
            chunk = lambda i: gv[:, i, :].rearrange("p (h f) -> p f h", h=H)
            gc = lambda q: q.rearrange("p (f h) -> p f h", f=KD)
            link(X.tensor_reduce(gq[0], gn_sum[:, :].rearrange("p (c b) -> p c b", b=8)[:, :, 0:NBK], AX.X, ALU.add))
            link(X.tensor_scalar(gq[0], gq[0], 1.0 / N, None, ALU.mult))
            link(X.tensor_tensor(gc(gq[0]), gc(gq[0]), chunk(0), ALU.add))
            link(X.tensor_tensor(gc(gq[0]), gc(gq[0]), chunk(3), ALU.mult))
            X.tensor_tensor(gc(gq[1]), chunk(0), gc(gq[0]), ALU.subtract).then_inc(s("gn_mean"), 1)
            v.wait_ge(s("gn_var"), KH)
            X.tensor_scalar(gq[3], gq[2], 1.0 / N, EPS, ALU.mult, ALU.add).then_inc(s("gn_var_in"), 1)
            v.wait_ge(s("gn_sqrt"), 1)
            link(X.reciprocal(gq[3], gq[3]))
            link(X.tensor_tensor(gc(gq[4]), gc(gq[3]), chunk(1), ALU.mult))
            link(X.tensor_tensor(gq[5], gq[4], gq[1], ALU.mult))
            X.tensor_tensor(gc(gq[5]), gc(gq[5]), chunk(2), ALU.add).then_inc(s("gn_scale"), 1)
            sv = scores_nat(1)
            for m in range(NT):
                v.wait_ge(s("h2"), m + 1)
                X.tensor_copy(natv[0:rows(m), m, 0:D], ps[0:rows(m), m % QUAD, 0:D]).then_inc(s("h2_out"), 1)
                v.wait_ge(s("h2_out"), m + 1)
                for j in range(2):
                    i = X.tensor_tensor(cols[0:rows(m), (2 * (m % 2) + j) * D:(2 * (m % 2) + j + 1) * D],
                                    natv[0:rows(m), m, 0:D], att2v[0:rows(m), j, :], ALU.mult)
                link(i)
                link(X.tensor_reduce(sv[0:rows(m), m, :], cols[0:rows(m), 2 * (m % 2) * D:2 * (m % 2 + 1) * D].rearrange("p (j d) -> p j d", j=2), AX.X, ALU.add))
                X.tensor_copy(natv[0:rows(m), m, D:D + 1], sv[0:rows(m), m, 0:1]).then_inc(s("gat2_row_ready"), 1)
            bounds(4, 1)
            v.wait_ge(s("self_w4"), 1)
            diagonals(4, w_self, 1, lambda m: (s("self_sum4"), KD * (m - 1)), "diag4")
            v.wait_ge(s("self_sum_out4"), KD * NT)
            v.wait_ge(s("res_loaded"), 32)
            b2w = biasv[:, 3:4, :].broadcast_to([P, NT - 1, D])
            link(X.tensor_tensor(res_nat[:, 0:NT - 1, :], res_nat[:, 0:NT - 1, :], b2w, ALU.add))
            link(X.tensor_tensor(res_nat[0:W, NT - 1, :], res_nat[0:W, NT - 1, :], biasv[0:W, 3, :], ALU.add))
            gat_pass(4, 1)
            denominators(4, 1)
            for m in range(NT):
                v.wait_ge(s("y_turned"), m + 1)
                X.scalar_tensor_tensor(out=natv[0:rows(m), m, 0:D], in0=ps[0:rows(m), m % QUAD, 0:D], scalar=rden[0:rows(m), m:m + 1],
                                       in1=res_nat[0:rows(m), m, :], op0=ALU.mult, op1=ALU.add).then_inc(s("y_out"), 1)
            layer_norm(1, s("y_out"))


_INS = ["x", "src", "dst", "L0_gnn_W0_self", "L0_gnn_W0_neigh", "L0_gnn_b0", "L0_gnn_W1_self", "L0_gnn_W1_neigh", "L0_gnn_b1",
        "L0_gnn_W2_self", "L0_gnn_W2_neigh", "L0_gnn_b2", "L1_gnn_W1", "L1_gnn_att_src1", "L1_gnn_att_dst1", "L1_gnn_b1",
        "L1_gnn_gn_w", "L1_gnn_gn_b", "L1_gnn_gn_ms", "L1_gnn_W2", "L1_gnn_att_src2", "L1_gnn_att_dst2", "L1_gnn_b2"]


def kernel(**inputs):
    import numpy as _np
    import concourse.bacc as _bacc
    from concourse import mybir as _mybir
    from concourse.bass_utils import run_bass_kernel_spmd as _run

    nc = _bacc.Bacc("TRN2", target_bir_lowering=False, num_devices=1)
    arrays, args = {}, {}
    for name in _INS:
        arr = _np.ascontiguousarray(inputs[name])
        arrays[f"in_{name}"] = arr
        args[name] = nc.dram_tensor(f"in_{name}", arr.shape, _mybir.dt.from_np(arr.dtype), kind="ExternalInput").ap()
    out = nc.dram_tensor("out_0", args["x"].shape, _mybir.dt.float32, kind="ExternalOutput").ap()
    build_gnn(nc, args, out)
    r = _run(nc, [arrays], core_ids=[0])
    return r.results[0]["out_0"]
```

```python
from contextlib import ExitStack

import concourse.bass as bass
from concourse import mybir

F32 = mybir.dt.float32
I32 = mybir.dt.int32
BF16 = mybir.dt.bfloat16
ALU = mybir.AluOpType
ACT = mybir.ActivationFunctionType
AX = mybir.AxisListType

P = 128


def build_gnn(nc, a, out):
    N, D = a["x"].shape
    E = a["src"].shape[0]
    H = a["L1_gnn_att_src1"].shape[0]
    KD = D // P
    HD = H * D
    KH = HD // P
    W = 64
    NW = -(-N // W)
    NP = NW * W
    NT = -(-N // P)
    ET = -(-E // P) + 1
    U = 8
    V = -(-(ET - 1 + NW - 1) // U) * U
    NG = V // U
    Q = 4
    VC = 4
    VR = V // VC
    NB = NW - 1
    EP = 125
    EK = E // EP
    FAR = 4095
    RW = D + H
    EPS = 1e-5
    SLOPE = 0.2
    SPREAD = 40.0
    assert E == EP * EK and VR * VC == V and VR <= P and D == 2 * P
    assert V - 1 - NB < ET and NW * W - (NT - 1) * P == W
    UV = 4
    GAT1_STORES = [(m, min(m + 4, NT - 1)) for m in range(0, NT - 1, 4)]
    NBV = NB * 2 // 3
    QUAD = 4

    def rows(m):
        return W if m == NT - 1 else P

    def real(m):
        return min(P, N - m * P)

    ctx = ExitStack()
    with ctx:
        def sb(name, shape, dt=F32):
            return ctx.enter_context(nc.sbuf_tensor(name, shape, dt))

        def sem(name):
            return ctx.enter_context(nc.semaphore(name))

        edge_src = nc.dram_tensor("edge_src", [ET, P], I32).ap()
        edge_dst = nc.dram_tensor("edge_dst", [ET, P], I32).ap()
        table_sage = [a["x"]] + [nc.dram_tensor(f"table_sage{i}", [NP, D], F32).ap() for i in (1, 2)]
        sorted_src = nc.dram_tensor("sorted_src", [ET * P, 1], I32).ap()
        sorted_dst = nc.dram_tensor("sorted_dst", [ET * P, 1], I32).ap()
        edge_win = nc.dram_tensor("edge_win", [ET * P], I32).ap()
        node_max = nc.dram_tensor("node_max", [NP * H], F32).ap()
        rden_rows = nc.dram_tensor("rden_rows", [H, NT, P], F32).ap()
        table_gat1 = nc.dram_tensor("table_gat1", [NP, RW], F32).ap()
        table_gat2 = nc.dram_tensor("table_gat2", [NP, D + 1], F32).ap()

        big = sb("big", [P, KH * NP])
        cols = sb("cols", [P, KD * NP])
        nat = sb("nat", [P, NT * RW])
        ring = sb("ring", [P, 2 * U * RW])
        onehot = sb("onehot", [P, 2 * U * W])
        onehot_w = sb("onehot_w", [P, 2 * U * H * W])
        src_of = sb("src_of", [P, V], I32)
        dst_in = sb("dst_in", [P, V])
        win_of = sb("win_of", [1, V], I32)
        idx = sb("idx", [P, Q * U], I32)
        ident = sb("ident", [P, P])
        ident_b = sb("ident_b", [P, P], BF16)
        ones = sb("ones", [P, P])
        ones_b = sb("ones_b", [P, 1], BF16)
        iota_w = sb("iota_w", [P, W])
        bias_b = sb("bias_b", [P, 4 * D])
        att2 = sb("att2", [P, 2 * D])
        att1 = sb("att1", [P, KD * 2 * H])
        gvec = sb("gvec", [P, 4 * KH])
        den = sb("den", [W, NW * 3 * H])
        score_win = sb("score_win", [W, NW * 2 * H])
        s_nat = sb("s_nat", [P, NT * 2 * H])
        r_nat = sb("r_nat", [P, NT * H])
        e_nat = sb("e_nat", [P, NT * H])
        w_self = sb("w_self", [P, NT * H])
        rden = sb("rden", [P, NT * H])
        z_buf = sb("z_buf", [P, 3 * U * H])
        look_buf = sb("look_buf", [P, 2 * U * H])
        w_buf = sb("w_buf", [P, 2 * U * H])
        w_parts = sb("w_parts", [P, 2 * 3 * U * H], BF16)
        w_rest = sb("w_rest", [P, U * H])
        mv = sb("mv", [P, NT * 2])
        stats = sb("stats", [P, NT * 6])
        rstd = sb("rstd", [P, NT])
        gn_v = sb("gn_v", [P, 8 * KH])
        small = sb("small", [P, 16])
        ext = sb("ext", [P, 32])
        small_i = sb("small_i", [P, 8], I32)
        flag_i = sb("flag_i", [1, 3], I32)
        smax_nat = sb("smax_nat", [P, NT * H])

        ps = ctx.enter_context(nc.psum_tensor("ps", [P, QUAD, 512], F32))
        ps_t = ctx.enter_context(nc.psum_tensor("ps_t", [P, 2, 512], F32))
        ps_d = ctx.enter_context(nc.psum_tensor("ps_d", [P, 512], F32))
        ps_n = ctx.enter_context(nc.psum_tensor("ps_n", [P, 512], F32))

        sums_sage = big[:, 0:KD * NP].rearrange("p (k n) -> p k n", k=KD)
        o = KD * NP
        self_nat = big[:, o:o + NT * D].rearrange("p (m d) -> p m d", m=NT)
        o += NT * D
        x_nat = big[:, o:o + NT * D].rearrange("p (m d) -> p m d", m=NT)
        o += NT * D
        w_sage = big[:, o:o + 6 * KD * D].rearrange("p (w k d) -> p w k d", w=6, k=KD)
        o += 6 * KD * D
        assert o <= KH * NP
        w1_pre = nat[:, 0:KD * HD].rearrange("p (k n) -> p k n", k=KD)
        prod_pre = nat[:, KD * HD:2 * KD * HD].rearrange("p (k n) -> p k n", k=KD)
        att_pre = big[:, o:o + 2 * HD].rearrange("p (s n) -> p s n", s=2)
        assert o + 2 * HD <= KH * NP
        res_nat = big[:, KD * NP:KD * NP + NT * D].rearrange("p (m d) -> p m d", m=NT)
        w1_sb = ring[:, 0:KD * HD].rearrange("p (k n) -> p k n", k=KD)
        w2_sb = ring[:, KD * HD:KD * HD + KH * D].rearrange("p (c d) -> p c d", c=KH)
        colsv = cols[:, :].rearrange("p (k n) -> p k n", k=KD)
        bigv = big[:, :].rearrange("p (c n) -> p c n", c=KH)
        natv = nat[:, :].rearrange("p (m r) -> p m r", m=NT)
        ringv = ring[:, :].rearrange("p (v r) -> p v r", r=RW)
        oh = onehot[:, :].rearrange("p (b u w) -> p b u w", b=2, u=U)
        ohb = onehot[:, 0:U * W].bitcast(BF16).rearrange("p (b u w) -> p b u w", b=2, u=U)
        ohd = nat[:, 2 * KD * HD:2 * KD * HD + U * W].bitcast(BF16).rearrange("p (b u w) -> p b u w", b=2, u=U)
        oht = cols[0:W, 0:U * P].bitcast(BF16).rearrange("p (b c) -> p b c", b=2)
        score_parts = cols[0:W, U * P:U * P + NW * 3 * H].bitcast(BF16)
        den_nat = cols[:, 2 * U * P:2 * U * P + NT * 3 * H]
        biasv = bias_b[:, :].rearrange("p (s d) -> p s d", s=4)
        att2v = att2[:, :].rearrange("p (s d) -> p s d", s=2)
        att1v = att1[:, :].rearrange("p (k s) -> p k s", k=KD)
        gv = gvec[:, :].rearrange("p (s c) -> p s c", s=4)
        winf = ring[:, 0:V]
        s0 = V
        dst_all = ring[0:EP, s0:s0 + EK]
        cmp_bv = onehot_w[0:NB, 0:V]

        S = {}

        def s(name):
            if name not in S:
                S[name] = sem(name)
            return S[name]

        dst_i = nat[0:EP, 0:EK].bitcast(I32)
        next_i = nat[0:EP, EK:EK + 1].bitcast(I32)
        dst_f = nat[0:EP, 2 * EK:3 * EK]
        next_f = nat[0:EP, 3 * EK:3 * EK + 1]
        junk = onehot_w[0:EP, 0:8 * EK].rearrange("p (j k) -> p j k", j=8)
        below = nat[0:EP, 5 * EK:5 * EK + NB]
        bound_2 = nat[:, 5 * EK + 128:5 * EK + 128 + NB - NBV]
        bound_at = nat[:, 5 * EK + 256:5 * EK + 256 + NB - NBV]
        junk_act = cols[0:EP, 0:2 * EK].rearrange("p (j k) -> p j k", j=2)
        iota_v = nat[:, 6 * EK:6 * EK + V]
        visit_rows_i = ring[0:VR, 0:2 * VC * P].bitcast(I32).rearrange("p (s c e) -> p s c e", s=2, c=VC)
        visit_rows = ring[0:VR, 2 * VC * P:4 * VC * P].rearrange("p (s c e) -> p s c e", s=2, c=VC)
        win_f = nat[:, 6 * EK + V:6 * EK + 2 * V]
        pad_i = nat[0:1, 6 * EK + 2 * V:6 * EK + 2 * V + 4 * P].bitcast(I32)
        iota_c = small[:, 0:VC]
        iota_b = small[:, VC:VC + 1]
        first_i = small_i[0:NB, 0:1]
        tile_i = small_i[0:NB, 1:2]
        tile_f = small[0:NB, VC + 1:VC + 2]
        event = small[0:NB, VC + 2:VC + 3]
        viol = small[0:EP, VC + 3:VC + 5]
        win_all = nat[0:EP, 4 * EK:5 * EK].bitcast(I32)
        flag_f = small[0:1, VC + 5:VC + 6]
        row_i = small_i[0:VR, 2:2 + VC]
        EPAD = ET * P - E

        def score_v(heads):
            return score_win[:, 0:NW * 2 * heads].rearrange("p (w s) -> p w s", s=2 * heads)

        def den_v(width):
            return den[:, 0:NW * width].rearrange("p (w h) -> p w h", h=width)

        def parts_v(heads):
            return score_parts[:, 0:NW * 6 * heads].rearrange("p (w j s) -> p w j s", j=3, s=2 * heads)

        def w_parts_v(heads, half):
            return w_parts[:, half * 3 * U * H:half * 3 * U * H + 3 * U * heads].rearrange("p (u j h) -> p u j h", j=3, h=heads)

        def ohw_v(heads):
            return onehot_w[:, 0:2 * U * heads * W].rearrange("p (b u n) -> p b u n", b=2, u=U)

        def diag_v(heads):
            return onehot_w[:, 0:2 * heads * P].rearrange("p (b h n) -> p b h n", b=2, h=heads)

        ch_order = [h * KD + f for f in range(KD) for h in range(H)]

        def nat_of(buf, m0, m1, heads):
            return buf[:, m0 * heads:m1 * heads].rearrange("p (m h) -> p m h", h=heads)

        rden_by_head = r_nat[:, :]
        rden_by_row = onehot[0:NT * H, U * W + 3 * P:U * W + 4 * P]

        def rb_v(b):
            if b % 2 == 0:
                return onehot_w[:, 2 * H * P:2 * H * P + H * 4 * P].rearrange("p (h n) -> p h n", h=H)
            return cols[:, 0:H * 4 * P].rearrange("p (h n) -> p h n", h=H)

        blocks = [range(b0, min(b0 + 4, NT)) for b0 in range(0, NT, 4)]
        norm_blocks = [range(0, 1), range(1, 4)] + blocks[1:]
        NBK = len(blocks)
        ln_batches = [range(b0, min(b0 + 5, NT)) for b0 in range(0, NT, 5)]
        gn_stats = onehot[:, U * W:U * W + KH * NBK * 6]
        gn_mv = gn_v[:, 6 * KH:8 * KH]

        deg_bank = [ps_n, ps_d]
        den_bank = [ps_n, ps_t[:, 1, :]]

        def ring_rows(n, q):
            if q < 2:
                return ringv[:, q * U:(q + 1) * U, :]
            if n < 3:
                return onehot_w[:, (q - 2) * U * D:(q - 1) * U * D].rearrange("p (u r) -> p u r", u=U)
            return nat[:, (q - 2) * U * RW:(q - 1) * U * RW].rearrange("p (u r) -> p u r", u=U)

        def windows_of(engine, gr):
            _, regs = nc.values_load_multi_w_load_instructions(
                win_of[0:1, bass.ds(gr * U, U)], engines=[engine], min_val=0, max_val=NW - 1,
                skip_runtime_bounds_check_because="a count of the NB boundaries is at most NB = NW - 1")
            return regs

        def rows_before(n, q):
            return n * 8 * U * len(range(q, NG, Q))

        def early(gr, k):
            return isinstance(gr, int) and gr < k

        def each_group(eng, body):
            for q in range(Q):
                body(q, q, 8 * U)
            with eng.Fori(1, NG // Q) as i:
                for q in range(Q):
                    body(i * Q + q, q, i * (8 * U) + 8 * U)
            for q in range(NG % Q):
                body(NG // Q * Q + q, q, (NG // Q + 1) * 8 * U)

        ctx.enter_context(nc.allow_non_contiguous_dma(reason="a few hundred single elements, once"))
        block = ctx.enter_context(nc.Block())

        @block.sync
        def _(sp):
            sp.dma_start(dst_i, a["dst"].rearrange("(p k) -> p k", p=EP)).then_inc(s("dst_loaded"), 16)
            sp.dma_start(next_i[0:EP - 1, :], a["dst"][EK:E].rearrange("(p k) -> p k", k=EK)[:, 0:1]).then_inc(s("next_loaded"), 16)
            sp.wait_ge(s("pads"), 2)
            es, ed = edge_src.rearrange("t e -> (t e)"), edge_dst.rearrange("t e -> (t e)")
            sp.dma_start(es[0:E], a["src"]).then_inc(s("edges_in"), 16)
            sp.dma_start(ed[0:E], a["dst"]).then_inc(s("edges_in"), 16)
            sp.dma_start(es[E:ET * P].rearrange("(p k) -> p k", p=1), pad_i[:, 0:EPAD]).then_inc(s("edges_in"), 16)
            sp.dma_start(ed[E:ET * P].rearrange("(p k) -> p k", p=1), pad_i[:, 2 * P:2 * P + EPAD]).then_inc(s("edges_in"), 16)
            sp.wait_ge(s("x_cleared"), 1)
            sp.dma_start(x_nat[:, 0:NT - 1, :], a["x"][0:(NT - 1) * P, :].rearrange("(m p) d -> p m d", p=P)).then_inc(s("x_loaded"), 16)
            sp.dma_start(x_nat[0:real(NT - 1), NT - 1, :], a["x"][(NT - 1) * P:N, :]).then_inc(s("x_loaded"), 16)
            for i in range(3):
                for j, kind in enumerate(("self", "neigh")):
                    sp.dma_start(w_sage[:, 2 * i + j], a[f"L0_gnn_W{i}_{kind}"].rearrange("(k p) d -> p k d", p=P)).then_inc(s("w_loaded"), 16)
            for i, name in enumerate(("L0_gnn_b0", "L0_gnn_b1", "L0_gnn_b2", "L1_gnn_b2")):
                sp.dma_start(biasv[:, i, :], a[name].rearrange("(a d) -> a d", a=1).broadcast_to([P, D])).then_inc(s("w_loaded"), 16)
            sp.dma_start(att2v[:, 0, :], a["L1_gnn_att_src2"].broadcast_to([P, D])).then_inc(s("w_loaded"), 16)
            sp.dma_start(att2v[:, 1, :], a["L1_gnn_att_dst2"].broadcast_to([P, D])).then_inc(s("w_loaded"), 16)
            for i, name in enumerate(("L1_gnn_b1", "L1_gnn_gn_w", "L1_gnn_gn_b", "L1_gnn_gn_ms")):
                sp.dma_start(gv[:, i, :], a[name].rearrange("(c p) -> p c", p=P)).then_inc(s("w_loaded"), 16)
            sp.wait_ge(s("setup_done"), 1)
            for i, name in enumerate(("L1_gnn_att_src1", "L1_gnn_att_dst1")):
                sp.dma_start(att_pre[:, i, :], a[name].rearrange("(a h) d -> a (h d)", a=1).broadcast_to([P, HD])).then_inc(s("att_loaded"), 16)
            sp.dma_start(w1_pre, a["L1_gnn_W1"].rearrange("(k p) n -> p k n", p=P)).then_inc(s("w1_pre_loaded"), 16)
            for i in (1, 2):
                for m in range(NT):
                    sp.wait_ge(s(f"row_ready{i}"), m + 1)
                    sp.dma_start(table_sage[i][m * P:m * P + rows(m), :], natv[0:rows(m), m, 0:D]).then_inc(s(f"table{i}"), 16)
            sp.wait_ge(s("gat1_rows_ready"), 2)
            for m0, m1 in GAT1_STORES:
                sp.dma_start(table_gat1[m0 * P:m1 * P, :].rearrange("(m p) r -> p m r", p=P), natv[:, m0:m1, :]).then_inc(s("table3"), 16)
            sp.dma_start(table_gat1[(NT - 1) * P:NP, :], natv[0:W, NT - 1, :]).then_inc(s("table3"), 16)
            sp.wait_ge(s("agg_ready3"), V)
            sp.dma_start(w1_sb, a["L1_gnn_W1"].rearrange("(k p) n -> p k n", p=P)).then_inc(s("w1_loaded"), 16)
            sp.dma_start(w2_sb, a["L1_gnn_W2"].rearrange("(c p) d -> p c d", p=P)).then_inc(s("w2_loaded"), 16)
            sp.wait_ge(s("rden_turned_out"), 1)
            sp.dma_start(rden_rows.rearrange("h m n -> (h m) n"), rden_by_row).then_inc(s("rden_stored"), 16)
            sp.wait_ge(s("rden_stored"), 16)
            for b, bt in enumerate(blocks):
                if b >= 2:
                    sp.wait_ge(s("proj_out"), (b - 1) * KH)
                sp.dma_start(rb_v(b)[:, :, 0:len(bt) * P], rden_rows[:, bt[0]:bt[-1] + 1, :].rearrange("h m n -> h (m n)").rearrange("(o h) n -> o h n", o=1)
                             .broadcast_to([P, H, len(bt) * P])).then_inc(s(f"rden_loaded{b % 2}"), 16)
            for m in range(NT):
                sp.wait_ge(s("gat2_row_ready"), m + 1)
                sp.dma_start(table_gat2[m * P:m * P + rows(m), :], natv[0:rows(m), m, 0:D + 1]).then_inc(s("table4"), 16)
            sp.wait_ge(s("h2"), NT)
            sp.dma_start(res_nat[:, 0:NT - 1, :], table_gat1[0:(NT - 1) * P, 0:D].rearrange("(m p) d -> p m d", p=P)).then_inc(s("res_loaded"), 16)
            sp.dma_start(res_nat[0:W, NT - 1, :], table_gat1[(NT - 1) * P:NP, 0:D]).then_inc(s("res_loaded"), 16)
            for m in range(NT):
                sp.wait_ge(s("out_ready"), m + 1)
                sp.dma_start(out[m * P:m * P + real(m), :], natv[0:real(m), m, 0:D]).then_inc(s("out_stored"), 16)
            sp.wait_ge(s("out_stored"), 16 * NT)

        @block.gpsimd
        def _(pool):
            g = nc.gpsimd
            def sort_edges():
                o = [512]

                def buf(width):
                    o[0] += width
                    return onehot_w[:, o[0] - width:o[0]]

                row, eq, lower = buf(P), buf(P), buf(P)
                NBK = 64
                assert FAR // W == NBK - 1 and NBK > NW
                bucket, hot, run, count, wide = buf(NBK), buf(NBK), buf(NBK), buf(NBK), buf(P)
                cold = buf(8)
                row_t = buf(P).bitcast(I32)
                col_t = buf(4).bitcast(I32)
                once = [0]

                def link1(ins):
                    once[0] += 1
                    ins.then_inc(s("sort_once"), 1)
                    pool.wait_ge(s("sort_once"), once[0])

                link1(g.memset(lower, 1.0))
                link1(g.affine_select(out=lower, in_=lower, compare_op=ALU.is_gt, fill=0.0, base=0, pattern=[[-1, P]], channel_multiplier=1))
                link1(g.iota(bucket, [[1, NBK]], base=0, channel_multiplier=0, allow_small_or_imprecise_dtypes=True))
                link1(g.memset(run, 0.0))
                link1(g.memset(wide, 0.0))
                link1(g.tensor_copy(wide[0:EP, 0:NB], below))
                link1(g.partition_all_reduce(count, wide[:, 0:NBK], P, bass.bass_isa.ReduceOp.add))
                link1(g.tensor_copy(run[:, 1:1 + NB], count[:, 0:NB]))
                link1(g.memset(run[:, NBK - 1:NBK], float(E)))
                link1(g.memset(pad_i[:, 0:P], NBK - 1))
                pool.dma_start(edge_win[0:E].rearrange("(p k) -> p k", p=EP), win_all).then_inc(s("sort_dma"), 16)
                pool.dma_start(edge_win[E:ET * P - P].rearrange("(o c) -> o c", o=1), pad_i[:, 0:EPAD - P]).then_inc(s("sort_dma"), 16)
                pool.wait_ge(s("sort_dma"), 32)
                ws = edge_win.rearrange("(t e) -> t e", e=P)
                steps = 10 + 7 + 6
                with pool.Fori(0, ET - 1) as i:
                    at = [0]

                    def link(ins):
                        at[0] += 1
                        ins.then_inc(s("sort_step"), 1)
                        pool.wait_ge(s("sort_step"), i * steps + at[0])
                        pool.sem_inc(s("idx_passed"), 1)

                    pool.dma_start(row_t, ws[bass.ds(i, 1), :].broadcast_to([P, P])).then_inc(s("sort_dma"), 16)
                    for j, table in enumerate((ws, edge_src, edge_dst)):
                        pool.dma_start(col_t[:, j:j + 1], table[bass.ds(i, 1), :].rearrange("o e -> e o")).then_inc(s("sort_dma"), 16)
                    pool.wait_ge(s("sort_dma"), i * 96 + (32 + 64))
                    pool.sem_inc(s("idx_passed"), 1)
                    link(g.tensor_copy(row, row_t))
                    link(g.tensor_copy(cold[:, 0:1], col_t[:, 0:1]))
                    link(g.tensor_scalar(eq, row, cold[:, 0:1], None, ALU.is_equal))
                    link(g.tensor_tensor(eq, eq, lower, ALU.mult))
                    h = P // 2
                    while h:
                        link(g.tensor_tensor(eq[:, 0:h], eq[:, 0:h], eq[:, h:2 * h], ALU.add))
                        h //= 2
                    link(g.tensor_scalar(hot, bucket, cold[:, 0:1], None, ALU.is_equal))
                    link(g.tensor_tensor(wide[:, 0:NBK], hot, run, ALU.mult))
                    h = NBK // 2
                    while h:
                        link(g.tensor_tensor(wide[:, 0:h], wide[:, 0:h], wide[:, h:2 * h], ALU.add))
                        h //= 2
                    link(g.tensor_tensor(cold[:, 1:2], eq[:, 0:1], wide[:, 0:1], ALU.add))
                    link(g.tensor_copy(col_t[:, 3:4], cold[:, 1:2]))
                    link(g.partition_all_reduce(count, hot, P, bass.bass_isa.ReduceOp.add))
                    link(g.tensor_tensor(run, run, count, ALU.add))
                    assert at[0] == steps
                    for j, table in ((1, sorted_src), (2, sorted_dst)):
                        g.indirect_dma_start(table, bass.IndirectOffsetOnAxis(ap=col_t[:, 3:4], axis=0), col_t[:, j:j + 1], None).then_inc(s("sort_dma"), 16)
                    pool.wait_ge(s("sort_dma"), i * 96 + (32 + 96))
                for a_, b_ in ((edge_src, sorted_src), (edge_dst, sorted_dst)):
                    pool.dma_start(a_[0:ET - 1, :], b_[0:(ET - 1) * P, :].rearrange("(t e) o -> t (e o)", e=P)).then_inc(s("sort_dma"), 16)
                pool.wait_ge(s("sort_dma"), 32 + (ET - 1) * 96 + 32)

            g.memset(pad_i[:, 0:2 * P], 0).then_inc(s("pads"), 1)
            g.memset(pad_i[:, 2 * P:4 * P], FAR).then_inc(s("pads"), 1)
            g.iota(iota_v, [[1, V]], base=0, channel_multiplier=0, allow_small_or_imprecise_dtypes=True).then_inc(s("consts"), 1)
            g.iota(iota_w[:, :], [[1, W]], base=0, channel_multiplier=0, allow_small_or_imprecise_dtypes=True).then_inc(s("consts"), 1)
            g.iota(iota_c, [[VR, VC]], base=0, channel_multiplier=1, allow_small_or_imprecise_dtypes=True).then_inc(s("consts"), 1)
            g.iota(bound_2, [[2 * W, NB - NBV]], base=2 * W * (NBV + 1) - 1, channel_multiplier=0, allow_small_or_imprecise_dtypes=True).then_inc(s("bound_2"), 1)
            pool.wait_ge(s("bound_2"), 1)
            g.tensor_scalar(bound_at, bound_2, 0.5, None, ALU.mult).then_inc(s("consts"), 1)
            g.iota(iota_b, [[1, 1]], base=1, channel_multiplier=1, allow_small_or_imprecise_dtypes=True).then_inc(s("consts"), 1)
            g.memset(ones[:, :], 1.0).then_inc(s("consts"), 1)
            g.memset(ones_b[:, :], 1.0).then_inc(s("consts"), 1)
            g.memset(ident[:, :], 0.0).then_inc(s("ident_zero"), 1)
            pool.wait_ge(s("ident_zero"), 1)
            g.affine_select(out=ident[:, :], in_=ident[:, :], compare_op=ALU.not_equal, fill=1.0, base=0,
                            pattern=[[-1, P]], channel_multiplier=1).then_inc(s("ident_made"), 1)
            pool.wait_ge(s("ident_made"), 1)
            g.tensor_copy(ident_b[:, :], ident[:, :]).then_inc(s("consts"), 1)
            pool.wait_ge(s("edges_in"), 64)
            pool.wait_ge(s("order_known"), 1)
            unordered = pool.value_load(flag_i[0:1, 0:1], min_val=0, max_val=E)
            with pool.If(unordered > 0):
                sort_edges()
            pool.wait_ge(s("visit_rows_known"), 1)
            for c in range(VC):
                for k, t in enumerate((edge_src, edge_dst)):
                    g.indirect_dma_start(visit_rows_i[:, k, c, :], None, t,
                                         bass.IndirectOffsetOnAxis(ap=row_i[:, c:c + 1], axis=0)).then_inc(s("visit_rows"), 16)

            def exact_max(n, table, heads, stores):
                m_all = big[0:1, 0:NW * W * heads].rearrange("p (w c) -> p w c", w=NW)
                cand = onehot_w[:, 0:W * heads]
                cand3 = cand.rearrange("p (c h) -> p c h", h=heads)
                red = onehot_w[:, H * W:H * W + W * heads]
                red2 = onehot_w[:, 6 * H * W:6 * H * W + W * heads]
                hot_f = onehot_w[:, 2 * H * W:2 * H * W + W]
                off_f = onehot_w[:, 3 * H * W:3 * H * W + W]
                hot, off = (b.rearrange("p (c h) -> p c h", h=1) for b in (hot_f, off_f))
                col = onehot_w[:, 4 * H * W:4 * H * W + 1]
                own = onehot_w[:, 5 * H * W:5 * H * W + NT * heads].rearrange("p (m h) -> p m h", h=heads)
                g.memset(m_all, -3.0e38).then_inc(s(f"max_step{n}"), 1)
                pool.wait_ge(s(f"table{n}"), 16 * stores)
                pool.wait_ge(s(f"max_step{n}"), 1)
                steps = 10
                with pool.Fori(0, V) as i:
                    at = [0]

                    def link(ins):
                        at[0] += 1
                        ins.then_inc(s(f"max_step{n}"), 1)
                        pool.wait_ge(s(f"max_step{n}"), i * steps + (1 + at[0]))
                        pool.sem_inc(s("idx_passed"), 1)

                    link(g.tensor_copy(idx[:, 0:1], src_of[:, bass.ds(i, 1)]))
                    g.indirect_dma_start(ringv[:, 0, 0:D + heads], None, table,
                                         bass.IndirectOffsetOnAxis(ap=idx[:, 0:1], axis=0)).then_inc(s(f"max_dma{n}"), 16)
                    link(g.tensor_copy(col, dst_in[:, bass.ds(i, 1)]))
                    link(g.tensor_scalar(hot_f, iota_w[:, :], col, None, ALU.is_equal))
                    link(g.tensor_scalar(off_f, hot_f, 3.0e38, -3.0e38, ALU.mult, ALU.add))
                    pool.wait_ge(s(f"max_dma{n}"), i * 16 + 16)
                    pool.sem_inc(s("idx_passed"), 1)
                    link(g.tensor_tensor(cand3, hot.broadcast_to([P, W, heads]),
                                         ringv[:, 0:1, D:D + heads].broadcast_to([P, W, heads]), ALU.mult))
                    link(g.tensor_tensor(cand3, cand3, off.broadcast_to([P, W, heads]), ALU.add))
                    link(g.partition_all_reduce(red, cand, P, bass.bass_isa.ReduceOp.max))
                    win = pool.value_load(win_of[0:1, bass.ds(i, 1)], min_val=0, max_val=NW - 1)
                    link(g.tensor_copy(red[0:1, :].rearrange("p (o c) -> p o c", o=1), m_all[0:1, bass.ds(win, 1), :]))
                    link(g.partition_all_reduce(red2, red, P, bass.bass_isa.ReduceOp.max))
                    link(g.tensor_copy(m_all[0:1, bass.ds(win, 1), :], red2[0:1, :].rearrange("p (o c) -> p o c", o=1)))
                    assert at[0] == steps
                flat = node_max[0:NP * heads]
                pool.dma_start(flat.rearrange("(o c) -> o c", o=1), big[0:1, 0:NP * heads]).then_inc(s(f"max_dma{n}"), 16)
                pool.wait_ge(s(f"max_dma{n}"), V * 16 + 16)
                edge = (NT - 1) * P * heads
                pool.dma_start(own[:, 0:NT - 1, :], flat[0:edge].rearrange("(m p h) -> p m h", p=P, h=heads)).then_inc(s(f"max_dma{n}"), 16)
                pool.dma_start(own[0:W, NT - 1, :], flat[edge:NP * heads].rearrange("(p h) -> p h", h=heads)).then_inc(s(f"max_dma{n}"), 16)
                pool.wait_ge(s(f"max_dma{n}"), V * 16 + 16 + 32)
                sm = nat_of(smax_nat, 0, NT, heads)
                g.tensor_copy(sm[:, 0:NT - 1, :], own[:, 0:NT - 1, :]).then_inc(s(f"max_step{n}"), 1)
                g.tensor_copy(sm[0:W, NT - 1:NT, :], own[0:W, NT - 1:NT, :]).then_inc(s(f"max_step{n}"), 1)
                pool.wait_ge(s(f"max_step{n}"), 1 + V * steps + 2)

            def settle_max(n, table, heads, stores):
                pool.wait_ge(s(f"spread_known{n}"), 1)
                wide = pool.value_load(flag_i[0:1, n - 2:n - 1], min_val=0, max_val=1)
                with pool.If(wide > 0):
                    exact_max(n, table, heads, stores)
                pool.sem_inc(s(f"max_settled{n}"), 1)

            def gather_pass(n, table, width, spare_free=None):
                def indices(gr, q):
                    g.tensor_copy(idx[:, q * U:q * U + U], src_of[:, bass.ds(gr * U, U)]).then_inc(s("idx"), 1)

                def group(gr, q, rows_done):
                    if not early(gr, Q):
                        pool.wait_ge(s(f"agg_ready{n}"), (gr - (Q - 1)) * U)
                    if early(gr, Q) and gr == 2 and spare_free:
                        pool.wait_ge(*spare_free)
                    pool.wait_ge(s("idx"), gr + (NG * n + 1))
                    pool.sem_inc(s("idx_passed"), 1)
                    for u in range(U):
                        g.indirect_dma_start(ring_rows(n, q)[:, u, 0:width], None, table,
                                             bass.IndirectOffsetOnAxis(ap=idx[:, q * U + u:q * U + u + 1], axis=0)).then_inc(s(f"rows_{q}_{u // (U // 2)}"), 16)
                        if u == U // 2 and not (isinstance(gr, int) and gr == NG - 1):
                            if not early(gr, Q - 1):
                                for part in range(2):
                                    pool.wait_ge(s(f"rows_{(q + 1) % Q}_{part}"), rows_before(n, (q + 1) % Q) + (rows_done if q == Q - 1 else rows_done - 8 * U))
                                pool.sem_inc(s("idx_passed"), 1)
                            indices(gr + 1, (q + 1) % Q)

                indices(0, 0)
                each_group(pool, group)

            pool.wait_ge(s("setup_done"), 2)
            gather_pass(0, table_sage[0], D)
            pool.wait_ge(s("table1"), 16 * NT)
            gather_pass(1, table_sage[1], D)
            pool.wait_ge(s("table2"), 16 * NT)
            gather_pass(2, table_sage[2], D)
            settle_max(3, table_gat1, H, len(GAT1_STORES) + 1)
            pool.wait_ge(s("table3"), 16 * (len(GAT1_STORES) + 1))
            gather_pass(3, table_gat1, RW)
            pool.wait_ge(s("h2"), NT)
            settle_max(4, table_gat2, 1, NT)
            pool.wait_ge(s("table4"), 16 * NT)
            gather_pass(4, table_gat2, D + 1, (s("self_sum4"), KD * NT))

        @block.tensor
        def _(pe):
            t = nc.tensor
            pe.wait_ge(s("consts"), 8)
            pe.wait_ge(s("below_step"), NBV + 1)
            t.matmul(ps_d[0:NB, 0:1], lhsT=below, rhs=ones[0:EP, 0:1], start=True, stop=True).then_inc(s("bounds"), 1)
            pe.wait_ge(s("viol"), 1)
            t.matmul(ps_n[0:1, 8:10], lhsT=ones[0:EP, 0:1], rhs=viol, start=True, stop=True).then_inc(s("viol_sum"), 1)
            pe.wait_ge(s("cmp"), 1)
            t.matmul(ps[:, 0, 0:V], lhsT=ones[0:NB, :], rhs=cmp_bv, start=True, stop=True).then_inc(s("windows"), 1)
            for c in range(VC):
                t.matmul(ps_n[0:VR, c:c + 1], lhsT=cmp_bv[:, c * VR:(c + 1) * VR], rhs=ones[0:NB, 0:1],
                         start=True, stop=True).then_inc(s("windows"), 1)
            pe.wait_ge(s("visit_rows_f"), 1)
            for c in range(VC):
                for k in range(2):
                    t.transpose(ps[:, 1 + k, c * VR:(c + 1) * VR], visit_rows[:, k, c, :], ident[0:VR, 0:VR]).then_inc(s("visit_cols"), 1)

            turned = [0]

            def turn(src, gate, m):
                pe.wait_ge(*gate)
                if turned[0] >= 2:
                    pe.wait_ge(s("turned_out"), turned[0] - 1)
                b = turned[0] % 2
                for k in range(KD):
                    i = t.transpose(ps_t[:, b, k * P:k * P + rows(m)], src[0:rows(m), m, k * P:(k + 1) * P], ident[0:rows(m), 0:rows(m)])
                i.then_inc(s("turned"), 1)
                turned[0] += 1

            def sage_self(n):
                for m in range(NT):
                    turn(x_nat if n == 0 else natv, (s("x_loaded"), 32) if n == 0 else (s(f"row_ready{n}"), m + 1), m)
                pe.wait_ge(s("w_loaded"), 16 * 16)
                for m in range(NT):
                    pe.wait_ge(s("turned_out"), NT * n + m + 1)
                    if m >= 2:
                        pe.wait_ge(s("self_out"), NT * n + m - 1)
                    bank = ps_d if m % 2 == 0 else ps_n
                    for k in range(KD):
                        i = t.matmul(bank[0:rows(m), 0:D], lhsT=colsv[:, k, m * P:m * P + rows(m)], rhs=w_sage[:, 2 * n, k, :],
                                     start=(k == 0), stop=(k == KD - 1))
                    i.then_inc(s("self"), 1)

            def sage_pass(n):
                def group(gr, q, rows_done):
                    half = q % 2
                    pe.wait_ge(s(f"oh{n}"), gr + 1)
                    if n == 0:
                        if not early(gr, 2):
                            pe.wait_ge(s("den_step0"), (gr - 1) * U)
                        pe.wait_ge(s("ohd"), gr + 1)
                        for u in range(U):
                            i = t.matmul(deg_bank[half][0:W, u:u + 1], lhsT=ohd[:, half, u, :], rhs=ones_b[:, :], start=True, stop=True)
                        i.then_inc(s("den_ready0"), 1)
                    for u in range(U):
                        if u % (U // 2) == 0:
                            pe.wait_ge(s(f"rows_{q}_{u // (U // 2)}"), rows_done + rows_before(n, q))
                        bank, at = 2 * half + u // 4, (u % 4) * KD * W
                        if not early(gr, 2) and u % 4 == 0:
                            pe.wait_ge(s(f"added{n}"), gr * U + (u + 4 - 2 * U))
                        for k in range(KD):
                            i = t.matmul(ps[:, bank, at + k * W:at + (k + 1) * W], lhsT=ring_rows(n, q)[:, u, k * P:(k + 1) * P],
                                         rhs=oh[:, half, u, :], start=True, stop=True)
                        i.then_inc(s(f"agg_ready{n}"), 1)

                each_group(pe, group)

            def sage_neigh(n):
                pe.wait_ge(s(f"added{n}"), V)
                for m in range(NT):
                    if m >= QUAD:
                        pe.wait_ge(s("neigh_out"), NT * n + m - QUAD + 1)
                    for k in range(KD):
                        i = t.matmul(ps[0:rows(m), m % QUAD, 0:D], lhsT=sums_sage[:, k, m * P:m * P + rows(m)], rhs=w_sage[:, 2 * n + 1, k, :],
                                     start=(k == 0), stop=(k == KD - 1))
                    i.then_inc(s("neigh"), 1)

            def gat_pass(n, heads):
                def ahead(gr, half):
                    if not early(gr, 1):
                        pe.wait_ge(s(f"oht{n}"), gr)
                    pe.wait_ge(s(f"oh{n}"), gr + 1)
                    pe.sem_inc(s("oh_passed"), 1)
                    for u in range(U):
                        i = t.transpose(ps_t[0:W, 0, :].bitcast(BF16)[:, u * P:(u + 1) * P], ohb[:, half, u, :], ident_b[:, :])
                    i.then_inc(s(f"ohp{n}"), 1)

                def lookup(gr, half):
                    regs = windows_of(mybir.EngineType.PE, gr)
                    if not early(gr, 1):
                        pe.wait_ge(s(f"zs{n}"), (gr - 1) * 4 + 1)
                    pe.wait_ge(s(f"oht{n}"), gr + 1)
                    pe.sem_inc(s("oh_passed"), 1)
                    for u in range(U):
                        i = t.matmul(ps_d[:, u * 6 * heads:(u + 1) * 6 * heads], lhsT=oht[:, half, u * P:(u + 1) * P],
                                     rhs=parts_v(heads)[:, bass.ds(regs[u], 1), :, :], start=True, stop=True)
                    i.then_inc(s(f"look{n}"), 1)

                def denom(gr, half):
                    if not early(gr, 2):
                        pe.wait_ge(s(f"den_step{n}"), (gr - 1) * U)
                    pe.wait_ge(s(f"wparts{n}"), gr + 1)
                    for u in range(U):
                        i = t.matmul(den_bank[half][0:W, u * 3 * heads:(u + 1) * 3 * heads], lhsT=ohb[:, half, u, :],
                                     rhs=w_parts_v(heads, half)[:, u, :, :], start=True, stop=True)
                    i.then_inc(s(f"den_ready{n}"), 1)

                def agg(gr, q, us):
                    for u in us:
                        if u == 0:
                            pe.wait_ge(s(f"ohw{n}"), gr + 1)
                        if u >= UV:
                            pe.wait_ge(s(f"ohw_act{n}"), gr * (U - UV) + (u - UV + 1))
                        if not early(gr, 1) or u >= QUAD:
                            pe.wait_ge(s(f"added{n}"), gr * U + (u - QUAD + 1))
                        for k in range(KD):
                            i = t.matmul(ps[:, u % QUAD, k * heads * W:(k + 1) * heads * W], lhsT=ring_rows(n, q)[:, u, k * P:(k + 1) * P],
                                         rhs=ohw_v(heads)[:, q % 2, u, :], start=True, stop=True)
                        i.then_inc(s(f"agg_ready{n}"), 1)

                def step(gr, q, rows_done):
                    half = q % 2
                    last = isinstance(gr, int) and gr == NG - 1
                    pe.wait_ge(s(f"rows_{q}_0"), rows_done + rows_before(n, q))
                    agg(gr, q, range(0, 1))
                    if not last:
                        lookup(gr + 1, 1 - half)
                    denom(gr, half)
                    agg(gr, q, range(1, 4))
                    pe.wait_ge(s(f"rows_{q}_1"), rows_done + rows_before(n, q))
                    agg(gr, q, range(4, 6))
                    if not (isinstance(gr, int) and gr >= NG - 2):
                        ahead(gr + 2, half)
                    agg(gr, q, range(6, U))

                ahead(0, 0)
                lookup(0, 0)
                ahead(1, 1)
                each_group(pe, step)

            for n in range(3):
                sage_self(n)
                pe.wait_ge(s("self_out"), NT * (n + 1))
                sage_pass(n)
                sage_neigh(n)

            pe.wait_ge(s("att1"), 2)

            def scores(m):
                pe.wait_ge(s("turned_out"), 3 * NT + m + 1)
                for k in range(KD):
                    i = t.matmul(ps_d[0:rows(m), m * 2 * H:(m + 1) * 2 * H], lhsT=colsv[:, k, m * P:m * P + rows(m)], rhs=att1v[:, k, :],
                                 start=(k == 0), stop=(k == KD - 1))
                return i

            for m in range(NT):
                turn(natv, (s("ln0"), m + 1), m)
                if m >= 2:
                    scores(m - 2)
            scores(NT - 2)
            scores(NT - 1).then_inc(s("scores3"), 1)

            def bound(n, heads):
                pe.wait_ge(s(f"smax_col{n}"), 1)
                t.transpose(ps_n[0:2 * heads, 0:P], ext[:, 0:2 * heads], ident[:, :]).then_inc(s(f"smax_row{n}"), 1)
                pe.wait_ge(s(f"smax_diag{n}"), 1)
                t.matmul(ps_n[:, P:P + 2 * heads], lhsT=ones[0:2 * heads, :], rhs=ext[0:2 * heads, 16:16 + 2 * heads], start=True, stop=True).then_inc(s(f"smax_all{n}"), 1)

            def self_weight_rows():
                for m in range(NT):
                    pe.wait_ge(s("diag3"), m + 1)
                    if m >= QUAD:
                        pe.wait_ge(s("self_sum_out3"), m - QUAD + 1)
                    t.matmul(ps[:, m % QUAD, :].rearrange("p (h n) -> p h n", h=H)[:, :, 0:rows(m)], lhsT=ones[0:rows(m), :],
                             rhs=diag_v(H)[0:rows(m), m % 2, :, 0:rows(m)], start=True, stop=True).then_inc(s("self_sum3"), 1)

            def self_terms(n, heads):
                for m in range(NT):
                    pe.wait_ge(s(f"diag{n}"), m + 1)
                    for k in range(KD):
                        b = (2 * m + k) % QUAD
                        if 2 * m + k >= QUAD:
                            pe.wait_ge(s(f"self_sum_out{n}"), 2 * m + k - QUAD + 1)
                        t.matmul(ps[:, b, 0:heads * P].rearrange("p (h n) -> p h n", h=heads)[:, :, 0:rows(m)],
                                 lhsT=natv[0:rows(m), m, k * P:(k + 1) * P],
                                 rhs=diag_v(heads)[0:rows(m), m % 2, :, 0:rows(m)], start=True, stop=True).then_inc(s(f"self_sum{n}"), 1)

            bound(3, H)
            self_weight_rows()
            gat_pass(3, H)

            pe.wait_ge(s("w1_loaded"), 16)
            nblk = 0
            pe.wait_ge(s("rden_known"), 1)
            t.transpose(ps_t[0:NT * H, 0, 0:P], rden_by_head, ident[:, :]).then_inc(s("rden_turned"), 1)
            for b, bt in enumerate(blocks):
                c0, width = bt[0] * P, sum(rows(m) for m in bt)
                for h in range(H):
                    for f in range(KD):
                        if nblk >= QUAD:
                            pe.wait_ge(s("proj_out"), nblk - QUAD + 1)
                        for k in range(KD):
                            i = t.matmul(ps[:, nblk % QUAD, 0:width], lhsT=w1_sb[:, k, h * D + f * P:h * D + (f + 1) * P],
                                         rhs=bigv[:, k * H + h, c0:c0 + width], start=(k == 0), stop=(k == KD - 1))
                        i.then_inc(s("proj"), 1)
                        nblk += 1

            pe.wait_ge(s("w2_loaded"), 16)
            for m in range(NT):
                pe.wait_ge(s("normed"), KH * (1 + [m in bt for bt in norm_blocks].index(True)))
                if m >= QUAD:
                    pe.wait_ge(s("h2_out"), m - QUAD + 1)
                for c in range(KH):
                    i = t.matmul(ps[0:rows(m), m % QUAD, 0:D], lhsT=bigv[:, c, m * P:m * P + rows(m)], rhs=w2_sb[:, ch_order[c], :],
                                 start=(c == 0), stop=(c == KH - 1))
                i.then_inc(s("h2"), 1)
            bound(4, 1)
            self_terms(4, 1)
            gat_pass(4, 1)
            pe.wait_ge(s("added4"), V)
            for m in range(NT):
                if m >= QUAD:
                    pe.wait_ge(s("y_out"), m - QUAD + 1)
                for k in range(KD):
                    i = t.transpose(ps[0:rows(m), m % QUAD, k * P:(k + 1) * P], bigv[:, k, m * P:m * P + rows(m)], ident[:, :])
                i.then_inc(s("y_turned"), 1)

        @block.scalar
        def _(act):
            A = nc.scalar
            done = [0]

            def link(ins):
                done[0] += 1
                ins.then_inc(s("act_step"), 1)
                act.wait_ge(s("act_step"), done[0])

            act.wait_ge(s("consts"), 8)
            act.wait_ge(s("dst_known"), 1)
            for b in range(NBV, NB):
                if b >= NBV + 2:
                    act.wait_ge(s("below_act"), b - NBV - 1)
                A.activation(junk_act[:, b % 2, :], dst_f, ACT.Sign, scale=-1.0, bias=bound_at[0:EP, b - NBV:b - NBV + 1],
                             accum_out=below[:, b:b + 1]).then_inc(s("below_act"), 1)

            turned = [0]

            def turn_out(m):
                act.wait_ge(s("turned"), turned[0] + 1)
                A.activation(colsv[:, :, m * P:m * P + rows(m)],
                             ps_t[:, turned[0] % 2, 0:KD * P].rearrange("p (k n) -> p k n", k=KD)[:, :, 0:rows(m)], ACT.Copy).then_inc(s("turned_out"), 1)
                turned[0] += 1

            def degree_pass():
                def step(gr, q, _):
                    act.wait_ge(s("oh0"), gr + 1)
                    if not early(gr, 2):
                        act.wait_ge(s("den_ready0"), gr - 1)
                    A.activation(ohd[:, q % 2, :, :], oh[:, q % 2, :, :], ACT.Copy).then_inc(s("ohd"), 1)

                each_group(act, step)

            def gat_pass(n, heads):
                act.preload_act_table(ACT.Exp)

                def turned_out(gr, half):
                    act.wait_ge(s(f"ohp{n}"), gr + 1)
                    A.activation(oht[:, half, :], ps_t[0:W, 0, :].bitcast(BF16), ACT.Copy).then_inc(s(f"oht{n}"), 1)

                def weigh(gr, half, us):
                    for u in us:
                        for h in range(heads):
                            at = half * U * heads + u * heads + h
                            i = A.activation(ohw_v(heads)[:, half, u, h * W:(h + 1) * W], ohb[:, half, u, :], ACT.Copy, scale=w_buf[:, at:at + 1])
                        i.then_inc(s(f"ohw_act{n}"), 1)

                def step(gr, q, _):
                    half = q % 2
                    act.wait_ge(s(f"z{n}"), gr + 1)
                    if not early(gr, 2):
                        act.wait_ge(s(f"agg_ready{n}"), (gr - 1) * U)
                    A.activation(w_buf[:, half * U * heads:(half + 1) * U * heads], z_buf[:, 2 * U * H:2 * U * H + U * heads], ACT.Exp).then_inc(s(f"w{n}"), 1)
                    A.activation(w_parts_v(heads, half)[:, :, 0, :], z_buf[:, 2 * U * H:2 * U * H + U * heads].rearrange("p (u h) -> p u h", h=heads),
                                 ACT.Exp).then_inc(s(f"w{n}"), 1)
                    act.wait_ge(s(f"w{n}"), gr * 2 + 1)
                    weigh(gr, half, range(UV, UV + 1))
                    if not (isinstance(gr, int) and gr == NG - 1):
                        turned_out(gr + 1, 1 - half)
                    weigh(gr, half, range(UV + 1, U))

                turned_out(0, 0)
                each_group(act, step)

            for n in range(3):
                for m in range(NT):
                    turn_out(m)
                if n == 0:
                    degree_pass()
                if n < 2:
                    for m in range(NT):
                        act.wait_ge(s("neigh_out"), NT * n + m + 1)
                        A.activation(natv[0:rows(m), m, 0:D], natv[0:rows(m), m, 0:D], ACT.Relu).then_inc(s(f"row_ready{n + 1}"), 1)
            def ln_sqrt(k):
                for b, bt in enumerate(ln_batches):
                    act.wait_ge(s(f"ln_stats{k}"), b + 1)
                    A.activation(rstd[:, bt[0]:bt[-1] + 1], rstd[:, bt[0]:bt[-1] + 1], ACT.Sqrt).then_inc(s(f"ln_sqrt{k}"), 1)

            ln_sqrt(0)
            for m in range(NT):
                turn_out(m)

            def self_terms(n, heads):
                act.wait_ge(s(f"self_z{n}"), 1)
                A.activation(w_self[:, 0:NT * heads], e_nat[:, 0:NT * heads], ACT.Exp).then_inc(s(f"self_w{n}"), 1)
                for m in range(NT):
                    for k in range(KD):
                        act.wait_ge(s(f"self_sum{n}"), 2 * m + k + 1)
                        A.activation(bigv[:, k * heads:(k + 1) * heads, m * P:m * P + rows(m)],
                                     ps[:, (2 * m + k) % QUAD, 0:heads * P].rearrange("p (h n) -> p h n", h=heads)[:, :, 0:rows(m)],
                                     ACT.Copy).then_inc(s(f"self_sum_out{n}"), 1)

            act.wait_ge(s("self_z3"), 1)
            A.activation(w_self[:, 0:NT * H], e_nat[:, 0:NT * H], ACT.Exp).then_inc(s("self_w3"), 1)
            act.wait_ge(s("self_w3"), 1)
            for m in range(NT):
                if m >= 2:
                    act.wait_ge(s("self_sum3"), m - 1)
                for h in range(H):
                    i = A.activation(diag_v(H)[:, m % 2, h, :], ident[:, :], ACT.Copy, scale=w_self[:, m * H + h:m * H + h + 1])
                i.then_inc(s("diag3"), 1)
            gat_pass(3, H)
            act.wait_ge(s("rden_turned"), 1)
            A.activation(rden_by_row, ps_t[0:NT * H, 0, 0:P], ACT.Copy).then_inc(s("rden_turned_out"), 1)
            act.wait_ge(s("gn_var"), 1)
            A.activation(gn_v[:, 3 * KH:4 * KH], gn_v[:, 3 * KH:4 * KH], ACT.Sqrt).then_inc(s("gn_sqrt"), 1)
            act.wait_ge(s("gn_scale"), 1)
            for bt in norm_blocks:
                c0, width = bt[0] * P, sum(rows(m) for m in bt)
                for c in range(KH):
                    A.activation(bigv[:, c, c0:c0 + width], bigv[:, c, c0:c0 + width], ACT.Relu, bias=gn_v[:, 5 * KH + c:5 * KH + c + 1],
                                 scale=gn_v[:, 4 * KH + c:4 * KH + c + 1]).then_inc(s("normed"), 1)
            self_terms(4, 1)
            gat_pass(4, 1)
            ln_sqrt(1)

        @block.vector
        def _(v):
            X = nc.vector
            done = [0]

            def link(ins):
                done[0] += 1
                ins.then_inc(s("dve_step"), 1)
                v.wait_ge(s("dve_step"), done[0])

            X.memset(x_nat[:, NT - 1, :], 0.0).then_inc(s("x_cleared"), 1)
            link(X.memset(small_i[:, :], 0))
            v.wait_ge(s("dst_loaded"), 16)
            v.wait_ge(s("next_loaded"), 16)
            X.tensor_copy(dst_f, dst_i).then_inc(s("dst_known"), 1)
            v.wait_ge(s("dst_known"), 1)
            link(X.tensor_copy(next_f[0:EP - 1, :], next_i[0:EP - 1, :]))
            X.tensor_scalar(win_all, dst_i, W.bit_length() - 1, None, ALU.arith_shift_right)
            link(X.memset(viol, 0.0))
            X.tensor_tensor(junk[:, 0, 0:EK - 1], dst_f[:, 0:EK - 1], dst_f[:, 1:EK], ALU.is_gt)
            link(X.tensor_tensor(viol[0:EP - 1, 1:2], dst_f[0:EP - 1, EK - 1:EK], next_f[0:EP - 1, :], ALU.is_gt))
            X.tensor_reduce(viol[:, 0:1], junk[:, 0, 0:EK - 1], AX.X, ALU.add).then_inc(s("viol"), 1)
            v.wait_ge(s("viol"), 1)
            for b in range(NBV):
                if b >= 8:
                    v.wait_ge(s("below_step"), b - 7)
                X.tensor_scalar(junk[:, b % 8, :], dst_f, float(W * (b + 1)), 0.0, ALU.is_lt, ALU.add,
                                accum_out=below[:, b:b + 1]).then_inc(s("below_step"), 1)
            v.wait_ge(s("below_act"), NB - NBV)
            X.tensor_scalar(below[:, NBV:NB], below[:, NBV:NB], 0.5, 0.5 * EK, ALU.mult, ALU.add).then_inc(s("below_step"), 1)
            v.wait_ge(s("consts"), 8)
            v.wait_ge(s("bounds"), 1)
            link(X.tensor_copy(first_i, ps_d[0:NB, 0:1]))
            v.wait_ge(s("viol_sum"), 1)
            link(X.tensor_reduce(flag_f, ps_n[0:1, 8:10], AX.X, ALU.add))
            X.tensor_copy(flag_i[0:1, 0:1], flag_f).then_inc(s("order_known"), 1)
            link(X.tensor_scalar(tile_i, first_i, 7, None, ALU.arith_shift_right))
            link(X.tensor_copy(tile_f, tile_i))
            link(X.tensor_tensor(event, tile_f, iota_b[0:NB, :], ALU.add))
            X.tensor_scalar(cmp_bv, iota_v[0:NB, :], event, None, ALU.is_ge).then_inc(s("cmp"), 1)
            v.wait_ge(s("windows"), 1 + VC)
            X.tensor_tensor(row_i, iota_c[0:VR, :], ps_n[0:VR, 0:VC], ALU.subtract).then_inc(s("visit_rows_known"), 1)
            X.tensor_copy(win_of[:, :], ps[0:1, 0, 0:V]).then_inc(s("win_known"), 1)
            link(X.tensor_scalar(win_f, ps[:, 0, 0:V], float(W), None, ALU.mult))
            X.memset(s_nat[:, :], 0.0)
            X.memset(r_nat[:, :], 0.0)
            X.memset(den[:, :], 0.0)
            X.memset(mv[:, :], 1.0)
            X.memset(w_self[:, :], 0.0)
            X.memset(score_win[:, :], 0.0)
            X.memset(rden[:, :], 0.0)
            link(X.memset(sums_sage, 0.0))
            v.wait_ge(s("visit_rows"), 16 * 2 * VC)
            X.tensor_copy(visit_rows, visit_rows_i).then_inc(s("visit_rows_f"), 1)
            v.wait_ge(s("visit_cols"), 2 * VC)
            X.tensor_copy(src_of[:, :], ps[:, 1, 0:V])
            link(X.tensor_tensor(dst_in[:, :], ps[:, 2, 0:V], win_f, ALU.subtract))
            X.memset(small[:, 0:16], 0.0).then_inc(s("setup_done"), 2)

            turned = [0]

            def one_hots(n, gr, half):
                X.tensor_tensor((oh if n < 3 else ohb)[:, half, :, :], iota_w[:, :].rearrange("p (u w) -> p u w", u=1).broadcast_to([P, U, W]),
                                dst_in[:, bass.ds(gr * U, U)].rearrange("p (u w) -> p u w", w=1).broadcast_to([P, U, W]),
                                ALU.is_equal).then_inc(s(f"oh{n}"), 1)

            def attention_vectors(j):
                v.wait_ge(s("w1_pre_loaded"), 16)
                v.wait_ge(s("att_loaded"), 32)
                link(X.tensor_tensor(prod_pre, w1_pre, att_pre[:, j, :].rearrange("p (k n) -> p k n", k=1).broadcast_to([P, KD, HD]), ALU.mult))
                X.tensor_reduce(att1v[:, :, j * H:(j + 1) * H], prod_pre.rearrange("p k (h d) -> p k h d", h=H), AX.X, ALU.add).then_inc(s("att1"), 1)
                v.wait_ge(s("att1"), j + 1)

            def sage_pass(n):
                def group(gr, q, _):
                    half = q % 2
                    regs = windows_of(mybir.EngineType.DVE, gr)
                    if n == 0 and isinstance(gr, int) and gr in (2, 3):
                        attention_vectors(gr - 2)
                    if not (isinstance(gr, int) and gr == NG - 1):
                        if not early(gr, 1):
                            v.wait_ge(s(f"agg_ready{n}"), gr * U)
                        one_hots(n, gr + 1, 1 - half)
                    if n == 0:
                        v.wait_ge(s("den_ready0"), gr + 1)
                    for u in range(U):
                        if u % 4 == 0:
                            v.wait_ge(s(f"agg_ready{n}"), gr * U + (u + 4))
                        if not (early(gr, 1) and u == 0):
                            v.wait_ge(s(f"added{n}"), gr * U + u)
                        place = sums_sage.rearrange("p k (w c) -> p k w c", c=W)[:, :, bass.ds(regs[u], 1), :]
                        bank, at = 2 * half + u // 4, (u % 4) * KD * W
                        X.tensor_tensor(place, place, ps[:, bank, at:at + KD * W].rearrange("p (k o c) -> p k o c", k=KD, o=1),
                                        ALU.add).then_inc(s(f"added{n}"), 1)
                        if n == 0:
                            if not (early(gr, 1) and u == 0):
                                v.wait_ge(s("den_step0"), gr * U + u)
                            dplace = den_v(1)[:, bass.ds(regs[u], 1), :]
                            X.tensor_tensor(dplace, dplace, deg_bank[half][0:W, u:u + 1].rearrange("p (o c) -> p o c", o=1),
                                            ALU.add).then_inc(s("den_step0"), 1)

                one_hots(n, 0, 0)
                each_group(v, group)

            def by_row(dst, src, heads, to_rows):
                w = src if to_rows else dst
                r = dst if to_rows else src
                for par in range(2):
                    wins = w[:, par::2, :]
                    rws = r[par * W:(par + 1) * W, 0:wins.shape[1], :]
                    i = X.tensor_copy(rws, wins) if to_rows else X.tensor_copy(wins, rws)
                return i

            def sage_self(n):
                for m in range(NT):
                    v.wait_ge(s("self"), NT * n + m + 1)
                    bank = ps_d if m % 2 == 0 else ps_n
                    X.tensor_tensor(self_nat[0:rows(m), m, :], bank[0:rows(m), 0:D], biasv[0:rows(m), n, :], ALU.add).then_inc(s("self_out"), 1)
                if n == 2:
                    v.wait_ge(s("self_out"), 3 * NT)
                    link(X.tensor_tensor(self_nat[:, 0:NT - 1, :], self_nat[:, 0:NT - 1, :], x_nat[:, 0:NT - 1, :], ALU.add))
                    link(X.tensor_tensor(self_nat[0:W, NT - 1, :], self_nat[0:W, NT - 1, :], x_nat[0:W, NT - 1, :], ALU.add))

            def sage_neigh(n):
                if n == 0:
                    v.wait_ge(s("den_step0"), V)
                    link(by_row(nat_of(rden, 0, NT, 1), den_v(1), 1, True))
                    link(X.tensor_scalar(rden[:, 0:NT], rden[:, 0:NT], 1.0, None, ALU.max))
                    link(X.reciprocal(rden[:, 0:NT], rden[:, 0:NT]))
                def produce(m):
                    v.wait_ge(s("neigh"), NT * n + m + 1)
                    if n:
                        v.wait_ge(s(f"table{n}"), 16 * NT)
                        v.wait_ge(s("turned"), NT * (n + 1))
                    X.scalar_tensor_tensor(out=natv[0:rows(m), m, 0:D], in0=ps[0:rows(m), m % QUAD, 0:D], scalar=rden[0:rows(m), m:m + 1],
                                           in1=self_nat[0:rows(m), m, :], op0=ALU.mult, op1=ALU.add).then_inc(s("neigh_out"), 1)
                if n == 2:
                    layer_norm(0, produce, s("neigh_out"), 2 * NT)
                    return
                for m in range(NT):
                    produce(m)
                v.wait_ge(s("neigh"), NT * (n + 1))
                link(X.memset(sums_sage, 0.0))

            def layer_norm(k, produce, made, before):
                def finish(b):
                    bt = ln_batches[b]
                    v.wait_ge(s(f"ln_sqrt{k}"), b + 1)
                    link(X.reciprocal(rstd[:, bt[0]:bt[-1] + 1], rstd[:, bt[0]:bt[-1] + 1]))
                    for m in bt:
                        X.tensor_scalar(natv[0:rows(m), m, 0:D], natv[0:rows(m), m, 0:D], mv[0:rows(m), 2 * m:2 * m + 1], rstd[0:rows(m), m:m + 1],
                                        ALU.subtract, ALU.mult).then_inc(s("ln0" if k == 0 else "out_ready"), 1)

                for b, bt in enumerate(ln_batches):
                    for m in bt:
                        produce(m)
                    v.wait_ge(made, before + bt[-1] + 1)
                    for m in bt:
                        i = X.bn_stats(stats[0:rows(m), m * 6:(m + 1) * 6], natv[0:rows(m), m, 0:D])
                    link(i)
                    for m in bt:
                        i = X.bn_aggr(mv[0:rows(m), 2 * m:2 * m + 2], stats[0:rows(m), m * 6:(m + 1) * 6])
                    link(i)
                    m0, m1 = bt[0], bt[-1] + 1
                    X.tensor_scalar(rstd[:, m0:m1].rearrange("p (m o) -> p m o", o=1), mv[:, 2 * m0:2 * m1].rearrange("p (m s) -> p m s", s=2)[:, :, 1:2],
                                    EPS, None, ALU.add).then_inc(s(f"ln_stats{k}"), 1)
                    if b:
                        finish(b - 1)
                finish(len(ln_batches) - 1)

            def scores_nat(heads):
                return s_nat[:, 0:NT * 2 * heads].rearrange("p (m s) -> p m s", s=2 * heads)

            def bounds(n, heads):
                sv = scores_nat(heads)
                link(X.memset(ext[:, :], -3.0e38))
                link(X.memset(e_nat[:, 0:2 * heads], -3.0e38))
                X.tensor_reduce(ext[:, 0:heads], sv[:, 0:NT - 1, 0:heads].rearrange("p m h -> p h m"), AX.X, ALU.max)
                link(X.tensor_reduce(ext[:, heads:2 * heads], sv[:, 0:NT - 1, 0:heads].rearrange("p m h -> p h m"), AX.X, ALU.min))
                link(X.tensor_scalar(ext[:, heads:2 * heads], ext[:, heads:2 * heads], -1.0, None, ALU.mult))
                X.tensor_copy(e_nat[0:real(NT - 1), 0:heads], sv[0:real(NT - 1), NT - 1, 0:heads])
                link(X.tensor_scalar(e_nat[0:real(NT - 1), heads:2 * heads], sv[0:real(NT - 1), NT - 1, 0:heads], -1.0, None, ALU.mult))
                X.tensor_tensor(ext[:, 0:2 * heads], ext[:, 0:2 * heads], e_nat[:, 0:2 * heads], ALU.max).then_inc(s(f"smax_col{n}"), 1)
                v.wait_ge(s(f"smax_row{n}"), 1)
                link(X.tensor_reduce(ext[0:2 * heads, 8:9], ps_n[0:2 * heads, 0:P], AX.X, ALU.max))
                X.tensor_scalar(ext[0:2 * heads, 16:16 + 2 * heads], ident[0:2 * heads, 0:2 * heads], ext[0:2 * heads, 8:9], None, ALU.mult).then_inc(s(f"smax_diag{n}"), 1)
                v.wait_ge(s(f"smax_all{n}"), 1)
                link(X.tensor_copy(ext[:, 0:2 * heads], ps_n[:, P:P + 2 * heads]))
                rv, ev = nat_of(r_nat, 0, NT, heads), nat_of(e_nat, 0, NT, heads)
                sm = nat_of(smax_nat, 0, NT, heads)
                link(X.tensor_copy(sm, ext[:, 0:heads].rearrange("p (m h) -> p m h", m=1).broadcast_to([P, NT, heads])))
                link(X.tensor_tensor(ext[0:1, 8:8 + heads], ext[0:1, 0:heads], ext[0:1, heads:2 * heads], ALU.add))
                link(X.tensor_reduce(ext[0:1, 24:25], ext[0:1, 8:8 + heads], AX.X, ALU.max))
                link(X.tensor_scalar(ext[0:1, 25:26], ext[0:1, 24:25], SPREAD, None, ALU.is_gt))
                X.tensor_copy(flag_i[0:1, n - 2:n - 1], ext[0:1, 25:26]).then_inc(s(f"spread_known{n}"), 1)
                v.wait_ge(s(f"max_settled{n}"), 1)
                link(X.tensor_tensor(sm, sm, sv[:, :, 0:heads], ALU.max))
                link(X.tensor_tensor(rv, sv[:, :, heads:2 * heads], sm, ALU.add))
                link(X.scalar_tensor_tensor(out=rv, in0=rv, scalar=SLOPE, in1=rv, op0=ALU.mult, op1=ALU.max))
                link(X.tensor_tensor(ev, sv[:, :, 0:heads], sv[:, :, heads:2 * heads], ALU.add))
                link(X.scalar_tensor_tensor(out=ev, in0=ev, scalar=SLOPE, in1=ev, op0=ALU.mult, op1=ALU.max))
                link(X.tensor_tensor(ev, ev, rv, ALU.subtract))
                X.tensor_scalar(ev, ev, 0.0, None, ALU.min).then_inc(s(f"self_z{n}"), 1)
                if n == 4:
                    looked_up_parts(heads)

            def looked_up_parts(heads):
                sv, rv = scores_nat(heads), nat_of(r_nat, 0, NT, heads)
                wv = score_v(heads)
                by_row(wv[:, :, 0:heads], sv[:, :, heads:2 * heads], heads, False)
                link(by_row(wv[:, :, heads:2 * heads], rv, heads, False))
                pv = parts_v(heads)
                for j in range(3):
                    link(X.tensor_copy(pv[:, :, j, :], wv))
                    if j < 2:
                        link(X.tensor_tensor(wv, wv, pv[:, :, j, :], ALU.subtract))
                link(X.memset(den[:, :], 0.0))

            def diagonals(n, col, heads, gate, name, ms=range(NT)):
                for m in ms:
                    if m >= 2:
                        v.wait_ge(*gate(m))
                    X.tensor_tensor(diag_v(heads)[:, m % 2, :, :], ident[:, :].rearrange("p (h n) -> p h n", h=1).broadcast_to([P, heads, P]),
                                    col[:, m * heads:(m + 1) * heads].rearrange("p (h n) -> p h n", n=1).broadcast_to([P, heads, P]),
                                    ALU.mult).then_inc(s(name), 1)

            def gat_pass(n, heads):
                def place(reg):
                    return bigv[:, 0:KD * heads, :].rearrange("p c (w n) -> p c w n", n=W)[:, :, bass.ds(reg, 1), :]

                def z_steps(gr, q, rows_done):
                    sh = ring_rows(n, q)[:, :, D:D + heads]
                    parts = ps_d[:, 0:U * 6 * heads].rearrange("p (u j s) -> p u s j", u=U, j=3)
                    look = look_buf[:, 0:U * 2 * heads].rearrange("p (u s) -> p u s", u=U)
                    zz = [z_buf[:, i * U * H:i * U * H + U * heads].rearrange("p (u h) -> p u h", u=U) for i in range(3)]

                    def looked_up():
                        v.wait_ge(s(f"look{n}"), gr + 1)
                        X.tensor_reduce(look, parts, AX.X, ALU.add).then_inc(s(f"zs{n}"), 1)

                    def added():
                        for part in range(2):
                            v.wait_ge(s(f"rows_{q}_{part}"), rows_done + rows_before(n, q))
                        v.wait_ge(s(f"zs{n}"), gr * 4 + 1)
                        X.tensor_tensor(zz[0], sh, look[:, :, 0:heads], ALU.add).then_inc(s(f"zs{n}"), 1)

                    def leaky():
                        v.wait_ge(s(f"zs{n}"), gr * 4 + 2)
                        X.scalar_tensor_tensor(out=zz[1], in0=zz[0], scalar=SLOPE, in1=zz[0], op0=ALU.mult, op1=ALU.max).then_inc(s(f"zs{n}"), 1)

                    def less_r():
                        v.wait_ge(s(f"zs{n}"), gr * 4 + 3)
                        X.tensor_tensor(zz[0], zz[1], look[:, :, heads:2 * heads], ALU.subtract).then_inc(s(f"zs{n}"), 1)

                    def at_most_0():
                        v.wait_ge(s(f"zs{n}"), gr * 4 + 4)
                        if not early(gr, 1):
                            v.wait_ge(s(f"w{n}"), gr * 2)
                        X.tensor_scalar(zz[2], zz[0], 0.0, None, ALU.min).then_inc(s(f"z{n}"), 1)

                    return looked_up, added, leaky, less_r, at_most_0

                def w_in_parts(gr, half):
                    w = w_buf[:, half * U * heads:(half + 1) * U * heads].rearrange("p (u h) -> p u h", h=heads)
                    rest = w_rest[:, 0:U * heads].rearrange("p (u h) -> p u h", h=heads)
                    part = [w_parts_v(heads, half)[:, :, j, :] for j in range(3)]

                    def second():
                        v.wait_ge(s(f"w{n}"), gr * 2 + 2)
                        X.tensor_tensor(rest, w, part[0], ALU.subtract).then_inc(s(f"split{n}"), 1)
                        X.tensor_tensor(part[1], w, part[0], ALU.subtract).then_inc(s(f"split{n}"), 1)

                    def third():
                        v.wait_ge(s(f"split{n}"), gr * 2 + 2)
                        X.tensor_tensor(part[2], rest, part[1], ALU.subtract).then_inc(s(f"wparts{n}"), 1)

                    return second, third

                def weigh(gr, half):
                    v.wait_ge(s(f"w{n}"), gr * 2 + 1)
                    wv = w_buf[:, half * U * heads:(half + 1) * U * heads].rearrange("p (u h w) -> p u h w", u=U, w=1)[:, 0:UV]
                    X.tensor_tensor(ohw_v(heads)[:, half, 0:UV, :].rearrange("p u (h w) -> p u h w", h=heads),
                                    ohb[:, half, 0:UV, :].rearrange("p u (h w) -> p u h w", h=1).broadcast_to([P, UV, heads, W]),
                                    wv.broadcast_to([P, UV, heads, W]), ALU.mult).then_inc(s(f"ohw{n}"), 1)

                def residual(part):
                    if part == 0:
                        v.wait_ge(s("res_loaded"), 32)
                        X.tensor_tensor(res_nat[0:W, NT - 1, :], res_nat[0:W, NT - 1, :], biasv[0:W, 3, :], ALU.add).then_inc(s("res_added"), 1)
                    ms = slice(part * (NT - 1) // 4, (part + 1) * (NT - 1) // 4)
                    X.tensor_tensor(res_nat[:, ms, :], res_nat[:, ms, :], biasv[:, 3:4, :].broadcast_to([P, ms.stop - ms.start, D]), ALU.add).then_inc(s("res_added"), 1)

                def adds(gr, half, us, regs):
                    for u in us:
                        v.wait_ge(s(f"agg_ready{n}"), gr * U + (u + 1))
                        if not (early(gr, 1) and u == 0):
                            v.wait_ge(s(f"added{n}"), gr * U + u)
                        pl = place(regs[u])
                        X.tensor_tensor(pl, pl, ps[:, u % QUAD, 0:KD * heads * W].rearrange("p (c o n) -> p c o n", c=KD * heads, o=1),
                                        ALU.add).then_inc(s(f"added{n}"), 1)
                        if not (early(gr, 1) and u == 0):
                            v.wait_ge(s(f"den_step{n}"), gr * U + u)
                        dpl = den_v(3 * heads)[:, bass.ds(regs[u], 1), :]
                        X.tensor_tensor(dpl, dpl, den_bank[half][0:W, u * 3 * heads:(u + 1) * 3 * heads].rearrange("p (o c) -> p o c", o=1),
                                        ALU.add).then_inc(s(f"den_step{n}"), 1)

                def step(gr, q, rows_done):
                    half = q % 2
                    last = isinstance(gr, int) and gr == NG - 1
                    regs = windows_of(mybir.EngineType.DVE, gr)
                    v.wait_ge(s(f"den_ready{n}"), gr + 1)
                    if last:
                        adds(gr, half, range(U), regs)
                        return
                    z = z_steps(gr + 1, (q + 1) % Q, rows_done if q < Q - 1 else rows_done + 8 * U)
                    second, third = w_in_parts(gr + 1, 1 - half)
                    if n == 4 and early(gr, 4):
                        residual(gr)
                    adds(gr, half, range(0, 1), regs)
                    z[0]()
                    adds(gr, half, range(1, 2), regs)
                    z[1]()
                    adds(gr, half, range(2, 3), regs)
                    z[2]()
                    if not (isinstance(gr, int) and gr >= NG - 2):
                        v.wait_ge(s(f"ohw_act{n}"), (gr + 1) * (U - UV))
                        one_hots(n, gr + 2, half)
                    z[3]()
                    adds(gr, half, range(3, 4), regs)
                    z[4]()
                    adds(gr, half, range(4, 5), regs)
                    if not early(gr, 1):
                        v.wait_ge(s(f"agg_ready{n}"), gr * U)
                    weigh(gr + 1, 1 - half)
                    adds(gr, half, range(5, 6), regs)
                    second()
                    adds(gr, half, range(6, 7), regs)
                    third()
                    adds(gr, half, range(7, 8), regs)

                one_hots(n, 0, 0)
                one_hots(n, 1, 1)
                for z in z_steps(0, 0, 8 * U):
                    z()
                weigh(0, 0)
                for part in w_in_parts(0, 0):
                    part()
                each_group(v, step)

            def denominators(n, heads):
                v.wait_ge(s(f"added{n}"), V)
                v.wait_ge(s(f"den_step{n}"), V)
                dn = den_nat[:, 0:NT * 3 * heads].rearrange("p (m j h) -> p m j h", j=3, h=heads)
                link(X.memset(den_nat, 0.0))
                link(by_row(den_nat[:, 0:NT * 3 * heads].rearrange("p (m h) -> p m h", m=NT), den_v(3 * heads), 3 * heads, True))
                link(X.tensor_tensor(nat_of(rden, 0, NT, heads), dn[:, :, 1, :], dn[:, :, 2, :], ALU.add))
                link(X.tensor_tensor(nat_of(rden, 0, NT, heads), nat_of(rden, 0, NT, heads), dn[:, :, 0, :], ALU.add))
                link(X.tensor_tensor(rden[:, 0:NT * heads], rden[:, 0:NT * heads], w_self[:, 0:NT * heads], ALU.add))
                link(X.tensor_scalar(rden[:, 0:NT * heads], rden[:, 0:NT * heads], 1.0e-30, None, ALU.max))
                link(X.reciprocal(rden[:, 0:NT * heads], rden[:, 0:NT * heads]))

            v.wait_ge(s("w_loaded"), 16 * 16)
            for n in range(3):
                sage_self(n)
                sage_pass(n)
                sage_neigh(n)

            v.wait_ge(s("scores3"), 1)
            sv = scores_nat(H)
            link(X.tensor_copy(sv[:, 0:NT - 1, :], ps_d[:, 0:(NT - 1) * 2 * H].rearrange("p (m s) -> p m s", s=2 * H)))
            link(X.tensor_copy(sv[0:W, NT - 1, :], ps_d[0:W, (NT - 1) * 2 * H:NT * 2 * H]))
            v.wait_ge(s("ln0"), NT)
            X.tensor_copy(natv[:, 0:NT - 1, D:D + H], sv[:, 0:NT - 1, 0:H]).then_inc(s("gat1_rows_ready"), 1)
            X.tensor_copy(natv[0:W, NT - 1, D:D + H], sv[0:W, NT - 1, 0:H]).then_inc(s("gat1_rows_ready"), 1)
            bounds(3, H)
            for m in range(NT):
                v.wait_ge(s("self_sum3"), m + 1)
                X.tensor_tensor(bigv[:, :, m * P:m * P + rows(m)].rearrange("p (k h) n -> p k h n", k=KD),
                                ps[:, m % QUAD, :].rearrange("p (o h n) -> p o h n", o=1, h=H)[:, :, :, 0:rows(m)].broadcast_to([P, KD, H, rows(m)]),
                                colsv[:, :, m * P:m * P + rows(m)].rearrange("p k (o n) -> p k o n", o=1).broadcast_to([P, KD, H, rows(m)]),
                                ALU.mult).then_inc(s("self_sum_out3"), 1)
            v.wait_ge(s("self_sum_out3"), NT)
            looked_up_parts(H)
            gat_pass(3, H)
            denominators(3, H)
            def column_stats(n):
                b, h, f = n // KH, n % KH // KD, n % KD
                c0 = blocks[b][0] * P
                v.wait_ge(s("proj_out"), n + 1)
                at = ((f * H + h) * NBK + b) * 6
                return X.bn_stats(gn_stats[:, at:at + 6], bigv[:, f * H + h, c0:min(c0 + 4 * P, N)])

            nblk = 0
            X.tensor_copy(rden_by_head.rearrange("p (h m) -> p m h", h=H), nat_of(rden, 0, NT, H)).then_inc(s("rden_known"), 1)
            for b, bt in enumerate(blocks):
                c0, width = bt[0] * P, sum(rows(m) for m in bt)
                v.wait_ge(s(f"rden_loaded{b % 2}"), 16 * (b // 2 + 1))
                for h in range(H):
                    v.wait_ge(s("proj"), nblk + KD)
                    for f in range(KD):
                        X.tensor_tensor(bigv[:, f * H + h, c0:c0 + width], ps[:, nblk % QUAD, 0:width],
                                        rb_v(b)[:, h, 0:width], ALU.mult).then_inc(s("proj_out"), 1)
                        nblk += 1
                        if nblk > 1:
                            column_stats(nblk - 2)
            link(column_stats(nblk - 1))
            for c in range(KH):
                i = X.bn_aggr(gn_mv[:, 2 * c:2 * c + 2], gn_stats[:, c * NBK * 6:(c + 1) * NBK * 6])
            link(i)
            mean, var = (gn_mv[:, :].rearrange("p (f h s) -> p s f h", f=KD, s=2)[:, j] for j in range(2))
            gq = [gn_v[:, i * KH:(i + 1) * KH].rearrange("p (f h) -> p f h", f=KD) for i in range(6)]
            b1, gn_w, gn_b, gn_ms = (gv[:, i, :].rearrange("p (h f) -> p f h", h=H) for i in range(4))
            link(X.tensor_tensor(gq[0], mean, b1, ALU.add))
            link(X.tensor_tensor(gq[0], gq[0], gn_ms, ALU.mult))
            link(X.tensor_tensor(gq[1], b1, gq[0], ALU.subtract))
            link(X.tensor_tensor(gq[2], mean, gq[1], ALU.add))
            link(X.tensor_tensor(gq[2], gq[2], gq[2], ALU.mult))
            link(X.tensor_tensor(gq[3], var, gq[2], ALU.add))
            X.tensor_scalar(gq[3], gq[3], EPS, None, ALU.add).then_inc(s("gn_var"), 1)
            v.wait_ge(s("gn_sqrt"), 1)
            link(X.reciprocal(gn_v[:, 3 * KH:4 * KH], gn_v[:, 3 * KH:4 * KH]))
            link(X.tensor_tensor(gq[4], gq[3], gn_w, ALU.mult))
            link(X.tensor_tensor(gq[5], gq[4], gq[1], ALU.mult))
            X.tensor_tensor(gq[5], gq[5], gn_b, ALU.add).then_inc(s("gn_scale"), 1)
            sv = scores_nat(1)
            for m in range(NT):
                v.wait_ge(s("h2"), m + 1)
                X.tensor_copy(natv[0:rows(m), m, 0:D], ps[0:rows(m), m % QUAD, 0:D]).then_inc(s("h2_out"), 1)
                v.wait_ge(s("h2_out"), m + 1)
                for j in range(2):
                    i = X.tensor_tensor(cols[0:rows(m), (2 * (m % 2) + j) * D:(2 * (m % 2) + j + 1) * D],
                                    natv[0:rows(m), m, 0:D], att2v[0:rows(m), j, :], ALU.mult)
                link(i)
                link(X.tensor_reduce(sv[0:rows(m), m, :], cols[0:rows(m), 2 * (m % 2) * D:2 * (m % 2 + 1) * D].rearrange("p (j d) -> p j d", j=2), AX.X, ALU.add))
                X.tensor_copy(natv[0:rows(m), m, D:D + 1], sv[0:rows(m), m, 0:1]).then_inc(s("gat2_row_ready"), 1)
            bounds(4, 1)
            v.wait_ge(s("self_w4"), 1)
            diagonals(4, w_self, 1, lambda m: (s("self_sum4"), KD * (m - 1)), "diag4")
            v.wait_ge(s("self_sum_out4"), KD * NT)
            gat_pass(4, 1)
            denominators(4, 1)
            v.wait_ge(s("res_added"), 5)

            def last_rows(m):
                v.wait_ge(s("y_turned"), m + 1)
                X.scalar_tensor_tensor(out=natv[0:rows(m), m, 0:D], in0=ps[0:rows(m), m % QUAD, 0:D], scalar=rden[0:rows(m), m:m + 1],
                                       in1=res_nat[0:rows(m), m, :], op0=ALU.mult, op1=ALU.add).then_inc(s("y_out"), 1)
            layer_norm(1, last_rows, s("y_out"), 0)


_INS = ["x", "src", "dst", "L0_gnn_W0_self", "L0_gnn_W0_neigh", "L0_gnn_b0", "L0_gnn_W1_self", "L0_gnn_W1_neigh", "L0_gnn_b1",
        "L0_gnn_W2_self", "L0_gnn_W2_neigh", "L0_gnn_b2", "L1_gnn_W1", "L1_gnn_att_src1", "L1_gnn_att_dst1", "L1_gnn_b1",
        "L1_gnn_gn_w", "L1_gnn_gn_b", "L1_gnn_gn_ms", "L1_gnn_W2", "L1_gnn_att_src2", "L1_gnn_att_dst2", "L1_gnn_b2"]


def kernel(**inputs):
    import numpy as _np
    import concourse.bacc as _bacc
    from concourse import mybir as _mybir
    from concourse.bass_utils import run_bass_kernel_spmd as _run

    nc = _bacc.Bacc("TRN2", target_bir_lowering=False, num_devices=1)
    arrays, args = {}, {}
    for name in _INS:
        arr = _np.ascontiguousarray(inputs[name])
        arrays[f"in_{name}"] = arr
        args[name] = nc.dram_tensor(f"in_{name}", arr.shape, _mybir.dt.from_np(arr.dtype), kind="ExternalInput").ap()
    out = nc.dram_tensor("out_0", args["x"].shape, _mybir.dt.float32, kind="ExternalOutput").ap()
    build_gnn(nc, args, out)
    r = _run(nc, [arrays], core_ids=[0])
    return r.results[0]["out_0"]
```

```python
from contextlib import ExitStack

import concourse.bass as bass
from concourse import mybir

F32 = mybir.dt.float32
I32 = mybir.dt.int32
BF16 = mybir.dt.bfloat16
ALU = mybir.AluOpType
ACT = mybir.ActivationFunctionType
AX = mybir.AxisListType

P = 128


def build_gnn(nc, a, out):
    N, D = a["x"].shape
    E = a["src"].shape[0]
    H = a["L1_gnn_att_src1"].shape[0]
    KD = D // P
    HD = H * D
    KH = HD // P
    W = 64
    NW = -(-N // W)
    NP = NW * W
    NT = -(-N // P)
    ET = -(-E // P) + 1
    U = 8
    V = -(-(ET - 1 + NW - 1) // U) * U
    NG = V // U
    Q = 4
    VC = 4
    VR = V // VC
    WS = 2 * W
    NWS = -(-N // WS)
    NBS = NWS - 1
    VS = -(-(ET - 1 + NWS - 1) // U) * U
    VRS = VS // VC
    NPS = NWS * WS
    NB = NW - 1
    EP = 125
    EK = E // EP
    FAR = 4095
    RW = D + H
    EPS = 1e-5
    SLOPE = 0.2
    SPREAD = 40.0
    assert E == EP * EK and VR * VC == V and VR <= P and D == 2 * P
    assert VS - 1 - NBS < ET and VRS * VC == VS and VRS <= P and WS == P
    assert V - 1 - NB < ET and NW * W - (NT - 1) * P == W
    UV = 4
    GAT1_STORES = [(m, min(m + 4, NT - 1)) for m in range(0, NT - 1, 4)]
    NBV = NB * 2 // 3
    QUAD = 4

    def rows(m):
        return W if m == NT - 1 else P

    def real(m):
        return min(P, N - m * P)

    ctx = ExitStack()
    with ctx:
        def sb(name, shape, dt=F32):
            return ctx.enter_context(nc.sbuf_tensor(name, shape, dt))

        def sem(name):
            return ctx.enter_context(nc.semaphore(name))

        edge_src = nc.dram_tensor("edge_src", [ET, P], I32).ap()
        edge_dst = nc.dram_tensor("edge_dst", [ET, P], I32).ap()
        table_sage = [a["x"]] + [nc.dram_tensor(f"table_sage{i}", [NP, D], F32).ap() for i in (1, 2)]
        sorted_src = nc.dram_tensor("sorted_src", [ET * P, 1], I32).ap()
        sorted_dst = nc.dram_tensor("sorted_dst", [ET * P, 1], I32).ap()
        edge_win = nc.dram_tensor("edge_win", [ET * P], I32).ap()
        node_max = nc.dram_tensor("node_max", [NP * H], F32).ap()
        rden_rows = nc.dram_tensor("rden_rows", [H, NT, P], F32).ap()
        plan_src = nc.dram_tensor("plan_src", [P, V], I32).ap()
        plan_dst = nc.dram_tensor("plan_dst", [P, V], F32).ap()
        plan_win = nc.dram_tensor("plan_win", [1, V], I32).ap()
        table_gat1 = nc.dram_tensor("table_gat1", [NP, RW], F32).ap()
        table_gat2 = nc.dram_tensor("table_gat2", [NP, D + 1], F32).ap()

        big = sb("big", [P, KH * NP])
        cols = sb("cols", [P, KD * NP])
        nat = sb("nat", [P, NT * RW])
        ring = sb("ring", [P, 2 * U * RW])
        onehot = sb("onehot", [P, 2 * U * W])
        onehot_w = sb("onehot_w", [P, 2 * U * H * W])
        src_of = sb("src_of", [P, V], I32)
        dst_in = sb("dst_in", [P, V])
        win_of = sb("win_of", [1, V], I32)
        idx = sb("idx", [P, Q * U], I32)
        ident = sb("ident", [P, P])
        ident_b = sb("ident_b", [P, P], BF16)
        ones = sb("ones", [P, P])
        ones_b = sb("ones_b", [P, 1], BF16)
        iota_w = sb("iota_w", [P, 2 * W])
        bias_b = sb("bias_b", [P, 4 * D])
        att2 = sb("att2", [P, 2 * D])
        att1 = sb("att1", [P, KD * 2 * H])
        gvec = sb("gvec", [P, 4 * KH])
        den = sb("den", [W, NW * 3 * H])
        score_win = sb("score_win", [W, NW * 2 * H])
        s_nat = sb("s_nat", [P, NT * 2 * H])
        r_nat = sb("r_nat", [P, NT * H])
        e_nat = sb("e_nat", [P, NT * H])
        w_self = sb("w_self", [P, NT * H])
        rden = sb("rden", [P, NT * H])
        z_buf = sb("z_buf", [P, 3 * U * H])
        look_buf = sb("look_buf", [P, 2 * U * H])
        w_buf = sb("w_buf", [P, 2 * U * H])
        w_parts = sb("w_parts", [P, 2 * 3 * U * H], BF16)
        w_rest = sb("w_rest", [P, U * H])
        mv = sb("mv", [P, NT * 2])
        stats = sb("stats", [P, NT * 6])
        rstd = sb("rstd", [P, NT])
        ln_shift = sb("ln_shift", [P, NT])
        gn_v = sb("gn_v", [P, 8 * KH])
        small = sb("small", [P, 16])
        ext = sb("ext", [P, 32])
        small_i = sb("small_i", [P, 16], I32)
        flag_i = sb("flag_i", [1, 3], I32)
        smax_nat = sb("smax_nat", [P, NT * H])

        ps = ctx.enter_context(nc.psum_tensor("ps", [P, QUAD, 512], F32))
        ps_t = ctx.enter_context(nc.psum_tensor("ps_t", [P, 2, 512], F32))
        ps_d = ctx.enter_context(nc.psum_tensor("ps_d", [P, 512], F32))
        ps_n = ctx.enter_context(nc.psum_tensor("ps_n", [P, 512], F32))

        sums_sage = big[:, 0:KD * NPS].rearrange("p (k n) -> p k n", k=KD)
        o = KD * NPS
        self_nat = big[:, o:o + NT * D].rearrange("p (m d) -> p m d", m=NT)
        o += NT * D
        x_nat = big[:, o:o + NT * D].rearrange("p (m d) -> p m d", m=NT)
        o += NT * D
        w_sage = big[:, o:o + 6 * KD * D].rearrange("p (w k d) -> p w k d", w=6, k=KD)
        o += 6 * KD * D
        assert o <= KH * NP
        w1_pre = nat[:, 0:KD * HD].rearrange("p (k n) -> p k n", k=KD)
        prod_pre = nat[:, KD * HD:2 * KD * HD].rearrange("p (k n) -> p k n", k=KD)
        att_pre = [onehot[:, 0:HD], nat[:, 5 * HD:6 * HD]]
        oh_flat = big[:, o:o + 2 * U * WS]
        oh = oh_flat.rearrange("p (b u w) -> p b u w", b=2, u=U)
        o += 2 * U * WS
        plan_src_sb = onehot[:, 0:V].bitcast(I32)
        plan_dst_sb = onehot[:, V:2 * V]
        plan_win_sb = big[0:1, o:o + V].bitcast(I32)
        assert o + V <= KH * NP and 2 * V <= 2 * U * W and 2 * KD * HD + U * WS <= 5 * HD
        res_nat = big[:, KD * NP:KD * NP + NT * D].rearrange("p (m d) -> p m d", m=NT)
        w1_sb = ring[:, 0:KD * HD].rearrange("p (k n) -> p k n", k=KD)
        w2_sb = ring[:, KD * HD:KD * HD + KH * D].rearrange("p (c d) -> p c d", c=KH)
        colsv = cols[:, :].rearrange("p (k n) -> p k n", k=KD)
        bigv = big[:, :].rearrange("p (c n) -> p c n", c=KH)
        natv = nat[:, :].rearrange("p (m r) -> p m r", m=NT)
        ringv = ring[:, :].rearrange("p (v r) -> p v r", r=RW)
        ohb = onehot[:, 0:U * W].bitcast(BF16).rearrange("p (b u w) -> p b u w", b=2, u=U)
        ohd = nat[:, 2 * KD * HD:2 * KD * HD + U * WS].bitcast(BF16).rearrange("p (b u w) -> p b u w", b=2, u=U)
        oht = cols[0:W, 0:U * P].bitcast(BF16).rearrange("p (b c) -> p b c", b=2)
        score_parts = cols[0:W, U * P:U * P + NW * 3 * H].bitcast(BF16)
        den_nat = cols[:, 2 * U * P:2 * U * P + NT * 3 * H]
        biasv = bias_b[:, :].rearrange("p (s d) -> p s d", s=4)
        att2v = att2[:, :].rearrange("p (s d) -> p s d", s=2)
        att1v = att1[:, :].rearrange("p (k s) -> p k s", k=KD)
        gv = gvec[:, :].rearrange("p (s c) -> p s c", s=4)

        S = {}

        def s(name):
            if name not in S:
                S[name] = sem(name)
            return S[name]

        dst_i = nat[0:EP, 0:EK].bitcast(I32)
        next_i = nat[0:EP, EK:EK + 1].bitcast(I32)
        dst_f = nat[0:EP, 2 * EK:3 * EK]
        next_f = nat[0:EP, 3 * EK:3 * EK + 1]
        junk = onehot_w[0:EP, 0:8 * EK].rearrange("p (j k) -> p j k", j=8)
        below = nat[0:EP, 5 * EK:5 * EK + NB]
        bound_2 = nat[:, 5 * EK + 128:5 * EK + 128 + NB - NBV]
        bound_at = nat[:, 5 * EK + 256:5 * EK + 256 + NB - NBV]
        junk_act = cols[0:EP, 0:2 * EK].rearrange("p (j k) -> p j k", j=2)
        iota_v = nat[:, 6 * EK:6 * EK + V]
        pad_i = nat[0:1, 6 * EK + 2 * V:6 * EK + 2 * V + 4 * P].bitcast(I32)
        iota_b = small[:, VC:VC + 1]
        viol = small[0:EP, VC + 3:VC + 5]
        win_all = nat[0:EP, 4 * EK:5 * EK].bitcast(I32)
        flag_f = small[0:1, VC + 5:VC + 6]
        EPAD = ET * P - E

        class Plan:
            def __init__(self, i):
                self.i = i
                self.W, self.NB, self.V, self.VR = ((WS, NBS, VS, VRS), (W, NB, V, VR))[i]
                VRi, Vi, g = self.VR, self.V, i * 8
                scratch = (ring[0:VRi, 0:4 * VC * P], oh_flat[0:VRi, 0:4 * VC * P])[i]
                self.rows_i = scratch[:, 0:2 * VC * P].bitcast(I32).rearrange("p (s c e) -> p s c e", s=2, c=VC)
                self.rows_f = scratch[:, 2 * VC * P:4 * VC * P].rearrange("p (s c e) -> p s c e", s=2, c=VC)
                self.cmp = onehot_w[0:self.NB, (3200 * i):(3200 * i) + Vi]
                self.below = below[:, 1:2 * NBS:2] if i == 0 else below
                self.first_i, self.tile_i = (small_i[0:self.NB, g + j:g + j + 1] for j in range(2))
                self.row_i = small_i[0:VRi, g + 2:g + 2 + VC]
                self.tile_f, self.event = ((small[0:self.NB, j:j + 1] for j in ((VC + 1, VC + 2), (VC + 6, VC + 7))[i]))
                self.iota_c = small[:, (0, VC + 8)[i]:(0, VC + 8)[i] + VC]
                self.win_f = nat[:, (6 * EK + V, 3800)[i]:(6 * EK + V, 3800)[i] + Vi]
                self.first_ps = ps_d[0:self.NB, i:i + 1]
                self.win_ps = ps[:, 3 * i, 0:Vi]
                self.count_ps = ps_n[0:VRi, 16 * i:16 * i + VC]
                self.cols_ps = [(ps[:, 1 + k, 0:Vi], ps_t[:, k, 0:Vi])[i] for k in range(2)]
                self.src = (src_of[:, 0:Vi], plan_src_sb)[i]
                self.dst = (dst_in[:, 0:Vi], plan_dst_sb)[i]
                self.win = (win_of[:, 0:Vi], plan_win_sb)[i]

        plans = [Plan(0), Plan(1)]

        def groups(n):
            return (VS if n < 3 else V) // U


        def score_v(heads):
            return score_win[:, 0:NW * 2 * heads].rearrange("p (w s) -> p w s", s=2 * heads)

        def den_v(width):
            return den[:, 0:NW * width].rearrange("p (w h) -> p w h", h=width)

        def parts_v(heads):
            return score_parts[:, 0:NW * 6 * heads].rearrange("p (w j s) -> p w j s", j=3, s=2 * heads)

        def w_parts_v(heads, half):
            return w_parts[:, half * 3 * U * H:half * 3 * U * H + 3 * U * heads].rearrange("p (u j h) -> p u j h", j=3, h=heads)

        def ohw_v(heads):
            return onehot_w[:, 0:2 * U * heads * W].rearrange("p (b u n) -> p b u n", b=2, u=U)

        def diag_v(heads):
            return onehot_w[:, 0:2 * heads * P].rearrange("p (b h n) -> p b h n", b=2, h=heads)

        ch_order = [h * KD + f for f in range(KD) for h in range(H)]

        def nat_of(buf, m0, m1, heads):
            return buf[:, m0 * heads:m1 * heads].rearrange("p (m h) -> p m h", h=heads)

        rden_by_head = r_nat[:, :]
        rden_by_row = onehot[0:NT * H, U * W + 3 * P:U * W + 4 * P]

        def rb_v(b):
            if b % 2 == 0:
                return onehot_w[:, 2 * H * P:2 * H * P + H * 4 * P].rearrange("p (h n) -> p h n", h=H)
            return cols[:, 0:H * 4 * P].rearrange("p (h n) -> p h n", h=H)

        blocks = [range(b0, min(b0 + 4, NT)) for b0 in range(0, NT, 4)]
        norm_blocks = [range(0, 1), range(1, 4)] + blocks[1:]
        NBK = len(blocks)
        ln_batches = [range(b0, min(b0 + 5, NT)) for b0 in range(0, NT, 5)]
        gn_stats = onehot[:, U * W:U * W + KH * NBK * 6]
        gn_mv = gn_v[:, 6 * KH:8 * KH]

        deg_bank = [ps_n, ps_d]
        den_bank = [ps_n, ps_t[:, 1, :]]

        def ring_rows(n, q):
            if q < 2:
                return ringv[:, q * U:(q + 1) * U, :]
            if n < 3:
                return onehot_w[:, (q - 2) * U * D:(q - 1) * U * D].rearrange("p (u r) -> p u r", u=U)
            return nat[:, (q - 2) * U * RW:(q - 1) * U * RW].rearrange("p (u r) -> p u r", u=U)

        def windows_of(engine, gr, windows=NW):
            _, regs = nc.values_load_multi_w_load_instructions(
                win_of[0:1, bass.ds(gr * U, U)], engines=[engine], min_val=0, max_val=windows - 1,
                skip_runtime_bounds_check_because="a count of the boundaries, which are one fewer than the windows")
            return regs

        def rows_before(n, q):
            return 8 * U * sum(len(range(q, groups(i), Q)) for i in range(n))

        def early(gr, k):
            return isinstance(gr, int) and gr < k

        def each_group(eng, n, body):
            for q in range(Q):
                body(q, q, 8 * U)
            end = (groups(n) - 1) // Q
            with eng.Fori(1, end) as i:
                for q in range(Q):
                    body(i * Q + q, q, i * (8 * U) + 8 * U)
            for q in range(groups(n) - end * Q):
                body(end * Q + q, q, (end + 1) * 8 * U)

        ctx.enter_context(nc.allow_non_contiguous_dma(reason="a few hundred single elements, once"))
        block = ctx.enter_context(nc.Block())

        @block.sync
        def _(sp):
            sp.dma_start(dst_i, a["dst"].rearrange("(p k) -> p k", p=EP)).then_inc(s("dst_loaded"), 16)
            sp.dma_start(next_i[0:EP - 1, :], a["dst"][EK:E].rearrange("(p k) -> p k", k=EK)[:, 0:1]).then_inc(s("next_loaded"), 16)
            sp.wait_ge(s("pads"), 2)
            es, ed = edge_src.rearrange("t e -> (t e)"), edge_dst.rearrange("t e -> (t e)")
            sp.dma_start(es[0:E], a["src"]).then_inc(s("edges_in"), 16)
            sp.dma_start(ed[0:E], a["dst"]).then_inc(s("edges_in"), 16)
            sp.dma_start(es[E:ET * P].rearrange("(p k) -> p k", p=1), pad_i[:, 0:EPAD]).then_inc(s("edges_in"), 16)
            sp.dma_start(ed[E:ET * P].rearrange("(p k) -> p k", p=1), pad_i[:, 2 * P:2 * P + EPAD]).then_inc(s("edges_in"), 16)
            sp.wait_ge(s("x_cleared"), 1)
            sp.dma_start(x_nat[:, 0:NT - 1, :], a["x"][0:(NT - 1) * P, :].rearrange("(m p) d -> p m d", p=P)).then_inc(s("x_loaded"), 16)
            sp.dma_start(x_nat[0:real(NT - 1), NT - 1, :], a["x"][(NT - 1) * P:N, :]).then_inc(s("x_loaded"), 16)
            for i in range(3):
                for j, kind in enumerate(("self", "neigh")):
                    sp.dma_start(w_sage[:, 2 * i + j], a[f"L0_gnn_W{i}_{kind}"].rearrange("(k p) d -> p k d", p=P)).then_inc(s("w_loaded"), 16)
            for i, name in enumerate(("L0_gnn_b0", "L0_gnn_b1", "L0_gnn_b2", "L1_gnn_b2")):
                sp.dma_start(biasv[:, i, :], a[name].rearrange("(a d) -> a d", a=1).broadcast_to([P, D])).then_inc(s("w_loaded"), 16)
            sp.dma_start(att2v[:, 0, :], a["L1_gnn_att_src2"].broadcast_to([P, D])).then_inc(s("w_loaded"), 16)
            sp.dma_start(att2v[:, 1, :], a["L1_gnn_att_dst2"].broadcast_to([P, D])).then_inc(s("w_loaded"), 16)
            for i, name in enumerate(("L1_gnn_b1", "L1_gnn_gn_w", "L1_gnn_gn_b", "L1_gnn_gn_ms")):
                sp.dma_start(gv[:, i, :], a[name].rearrange("(c p) -> p c", p=P)).then_inc(s("w_loaded"), 16)
            sp.wait_ge(s("setup_done"), 2)
            for dram, made in ((plan_src, plan_src_sb), (plan_dst, plan_dst_sb), (plan_win, plan_win_sb)):
                sp.dma_start(dram, made).then_inc(s("plan_stored"), 16)
            sp.wait_ge(s("plan_stored"), 48)
            for i, name in enumerate(("L1_gnn_att_src1", "L1_gnn_att_dst1")):
                sp.dma_start(att_pre[i], a[name].rearrange("(a h) d -> a (h d)", a=1).broadcast_to([P, HD])).then_inc(s("att_loaded"), 16)
            sp.dma_start(w1_pre, a["L1_gnn_W1"].rearrange("(k p) n -> p k n", p=P)).then_inc(s("att_loaded"), 16)
            for i in (1, 2):
                for m in range(NT):
                    sp.wait_ge(s(f"row_ready{i}"), m + 1)
                    sp.dma_start(table_sage[i][m * P:m * P + rows(m), :], natv[0:rows(m), m, 0:D]).then_inc(s(f"table{i}"), 16)
            sp.wait_ge(s("added2"), VS)
            for dram, made in ((plan_src, src_of[:, :]), (plan_dst, dst_in[:, :]), (plan_win, win_of[:, :])):
                sp.dma_start(made, dram).then_inc(s("plan_loaded"), 16)
            sp.wait_ge(s("gat1_rows_ready"), 2)
            for m0, m1 in GAT1_STORES:
                sp.dma_start(table_gat1[m0 * P:m1 * P, :].rearrange("(m p) r -> p m r", p=P), natv[:, m0:m1, :]).then_inc(s("table3"), 16)
            sp.dma_start(table_gat1[(NT - 1) * P:NP, :], natv[0:W, NT - 1, :]).then_inc(s("table3"), 16)
            sp.wait_ge(s("agg_ready3"), V)
            sp.dma_start(w1_sb, a["L1_gnn_W1"].rearrange("(k p) n -> p k n", p=P)).then_inc(s("w1_loaded"), 16)
            sp.dma_start(w2_sb, a["L1_gnn_W2"].rearrange("(c p) d -> p c d", p=P)).then_inc(s("w2_loaded"), 16)
            sp.wait_ge(s("rden_turned_out"), 1)
            sp.dma_start(rden_rows.rearrange("h m n -> (h m) n"), rden_by_row).then_inc(s("rden_stored"), 16)
            sp.wait_ge(s("rden_stored"), 16)
            for b, bt in enumerate(blocks):
                if b >= 2:
                    sp.wait_ge(s("proj_out"), (b - 1) * KH)
                sp.dma_start(rb_v(b)[:, :, 0:len(bt) * P], rden_rows[:, bt[0]:bt[-1] + 1, :].rearrange("h m n -> h (m n)").rearrange("(o h) n -> o h n", o=1)
                             .broadcast_to([P, H, len(bt) * P])).then_inc(s(f"rden_loaded{b % 2}"), 16)
            for m in range(NT):
                sp.wait_ge(s("gat2_row_ready"), m + 1)
                sp.dma_start(table_gat2[m * P:m * P + rows(m), :], natv[0:rows(m), m, 0:D + 1]).then_inc(s("table4"), 16)
            sp.wait_ge(s("h2"), NT)
            sp.dma_start(res_nat[:, 0:NT - 1, :], table_gat1[0:(NT - 1) * P, 0:D].rearrange("(m p) d -> p m d", p=P)).then_inc(s("res_loaded"), 16)
            sp.dma_start(res_nat[0:W, NT - 1, :], table_gat1[(NT - 1) * P:NP, 0:D]).then_inc(s("res_loaded"), 16)
            for m in range(NT):
                sp.wait_ge(s("out_ready"), m + 1)
                sp.dma_start(out[m * P:m * P + real(m), :], natv[0:real(m), m, 0:D]).then_inc(s("out_stored"), 16)
            sp.wait_ge(s("out_stored"), 16 * NT)

        @block.gpsimd
        def _(pool):
            g = nc.gpsimd
            def sort_edges():
                o = [512]

                def buf(width):
                    o[0] += width
                    return onehot_w[:, o[0] - width:o[0]]

                row, eq, lower = buf(P), buf(P), buf(P)
                NBK = 64
                assert FAR // W == NBK - 1 and NBK > NW
                bucket, hot, run, count, wide = buf(NBK), buf(NBK), buf(NBK), buf(NBK), buf(P)
                cold = buf(8)
                row_t = buf(P).bitcast(I32)
                col_t = buf(4).bitcast(I32)
                once = [0]

                def link1(ins):
                    once[0] += 1
                    ins.then_inc(s("sort_once"), 1)
                    pool.wait_ge(s("sort_once"), once[0])

                link1(g.memset(lower, 1.0))
                link1(g.affine_select(out=lower, in_=lower, compare_op=ALU.is_gt, fill=0.0, base=0, pattern=[[-1, P]], channel_multiplier=1))
                link1(g.iota(bucket, [[1, NBK]], base=0, channel_multiplier=0, allow_small_or_imprecise_dtypes=True))
                link1(g.memset(run, 0.0))
                link1(g.memset(wide, 0.0))
                link1(g.tensor_copy(wide[0:EP, 0:NB], below))
                link1(g.partition_all_reduce(count, wide[:, 0:NBK], P, bass.bass_isa.ReduceOp.add))
                link1(g.tensor_copy(run[:, 1:1 + NB], count[:, 0:NB]))
                link1(g.memset(run[:, NBK - 1:NBK], float(E)))
                link1(g.memset(pad_i[:, 0:P], NBK - 1))
                pool.dma_start(edge_win[0:E].rearrange("(p k) -> p k", p=EP), win_all).then_inc(s("sort_dma"), 16)
                pool.dma_start(edge_win[E:ET * P - P].rearrange("(o c) -> o c", o=1), pad_i[:, 0:EPAD - P]).then_inc(s("sort_dma"), 16)
                pool.wait_ge(s("sort_dma"), 32)
                ws = edge_win.rearrange("(t e) -> t e", e=P)
                steps = 10 + 7 + 6
                with pool.Fori(0, ET - 1) as i:
                    at = [0]

                    def link(ins):
                        at[0] += 1
                        ins.then_inc(s("sort_step"), 1)
                        pool.wait_ge(s("sort_step"), i * steps + at[0])
                        pool.sem_inc(s("idx_passed"), 1)

                    pool.dma_start(row_t, ws[bass.ds(i, 1), :].broadcast_to([P, P])).then_inc(s("sort_dma"), 16)
                    for j, table in enumerate((ws, edge_src, edge_dst)):
                        pool.dma_start(col_t[:, j:j + 1], table[bass.ds(i, 1), :].rearrange("o e -> e o")).then_inc(s("sort_dma"), 16)
                    pool.wait_ge(s("sort_dma"), i * 96 + (32 + 64))
                    pool.sem_inc(s("idx_passed"), 1)
                    link(g.tensor_copy(row, row_t))
                    link(g.tensor_copy(cold[:, 0:1], col_t[:, 0:1]))
                    link(g.tensor_scalar(eq, row, cold[:, 0:1], None, ALU.is_equal))
                    link(g.tensor_tensor(eq, eq, lower, ALU.mult))
                    h = P // 2
                    while h:
                        link(g.tensor_tensor(eq[:, 0:h], eq[:, 0:h], eq[:, h:2 * h], ALU.add))
                        h //= 2
                    link(g.tensor_scalar(hot, bucket, cold[:, 0:1], None, ALU.is_equal))
                    link(g.tensor_tensor(wide[:, 0:NBK], hot, run, ALU.mult))
                    h = NBK // 2
                    while h:
                        link(g.tensor_tensor(wide[:, 0:h], wide[:, 0:h], wide[:, h:2 * h], ALU.add))
                        h //= 2
                    link(g.tensor_tensor(cold[:, 1:2], eq[:, 0:1], wide[:, 0:1], ALU.add))
                    link(g.tensor_copy(col_t[:, 3:4], cold[:, 1:2]))
                    link(g.partition_all_reduce(count, hot, P, bass.bass_isa.ReduceOp.add))
                    link(g.tensor_tensor(run, run, count, ALU.add))
                    assert at[0] == steps
                    for j, table in ((1, sorted_src), (2, sorted_dst)):
                        g.indirect_dma_start(table, bass.IndirectOffsetOnAxis(ap=col_t[:, 3:4], axis=0), col_t[:, j:j + 1], None).then_inc(s("sort_dma"), 16)
                    pool.wait_ge(s("sort_dma"), i * 96 + (32 + 96))
                for a_, b_ in ((edge_src, sorted_src), (edge_dst, sorted_dst)):
                    pool.dma_start(a_[0:ET - 1, :], b_[0:(ET - 1) * P, :].rearrange("(t e) o -> t (e o)", e=P)).then_inc(s("sort_dma"), 16)
                pool.wait_ge(s("sort_dma"), 32 + (ET - 1) * 96 + 32)

            g.memset(pad_i[:, 0:2 * P], 0).then_inc(s("pads"), 1)
            g.memset(pad_i[:, 2 * P:4 * P], FAR).then_inc(s("pads"), 1)
            g.iota(iota_v, [[1, V]], base=0, channel_multiplier=0, allow_small_or_imprecise_dtypes=True).then_inc(s("consts"), 1)
            g.iota(iota_w[:, :], [[1, WS]], base=0, channel_multiplier=0, allow_small_or_imprecise_dtypes=True).then_inc(s("consts"), 1)
            for pl in plans:
                g.iota(pl.iota_c, [[pl.VR, VC]], base=0, channel_multiplier=1, allow_small_or_imprecise_dtypes=True).then_inc(s("consts"), 1)
            g.iota(bound_2, [[2 * W, NB - NBV]], base=2 * W * (NBV + 1) - 1, channel_multiplier=0, allow_small_or_imprecise_dtypes=True).then_inc(s("bound_2"), 1)
            pool.wait_ge(s("bound_2"), 1)
            g.tensor_scalar(bound_at, bound_2, 0.5, None, ALU.mult).then_inc(s("consts"), 1)
            g.iota(iota_b, [[1, 1]], base=1, channel_multiplier=1, allow_small_or_imprecise_dtypes=True).then_inc(s("consts"), 1)
            g.memset(ones[:, :], 1.0).then_inc(s("consts"), 1)
            g.memset(ones_b[:, :], 1.0).then_inc(s("consts"), 1)
            g.memset(ident[:, :], 0.0).then_inc(s("ident_zero"), 1)
            pool.wait_ge(s("ident_zero"), 1)
            g.affine_select(out=ident[:, :], in_=ident[:, :], compare_op=ALU.not_equal, fill=1.0, base=0,
                            pattern=[[-1, P]], channel_multiplier=1).then_inc(s("ident_made"), 1)
            pool.wait_ge(s("ident_made"), 1)
            g.tensor_copy(ident_b[:, :], ident[:, :]).then_inc(s("consts"), 1)
            pool.wait_ge(s("edges_in"), 64)
            pool.wait_ge(s("order_known"), 1)
            unordered = pool.value_load(flag_i[0:1, 0:1], min_val=0, max_val=E)
            with pool.If(unordered > 0):
                sort_edges()
            pool.wait_ge(s("visit_rows_known"), 1)
            for pl in plans:
                for c in range(VC):
                    for k, t in enumerate((edge_src, edge_dst)):
                        g.indirect_dma_start(pl.rows_i[:, k, c, :], None, t,
                                             bass.IndirectOffsetOnAxis(ap=pl.row_i[:, c:c + 1], axis=0)).then_inc(s(f"visit_rows{pl.i}"), 16)

            def exact_max(n, table, heads, stores):
                m_all = big[0:1, 0:NW * W * heads].rearrange("p (w c) -> p w c", w=NW)
                cand = onehot_w[:, 0:W * heads]
                cand3 = cand.rearrange("p (c h) -> p c h", h=heads)
                red = onehot_w[:, H * W:H * W + W * heads]
                red2 = onehot_w[:, 6 * H * W:6 * H * W + W * heads]
                hot_f = onehot_w[:, 2 * H * W:2 * H * W + W]
                off_f = onehot_w[:, 3 * H * W:3 * H * W + W]
                hot, off = (b.rearrange("p (c h) -> p c h", h=1) for b in (hot_f, off_f))
                col = onehot_w[:, 4 * H * W:4 * H * W + 1]
                own = onehot_w[:, 5 * H * W:5 * H * W + NT * heads].rearrange("p (m h) -> p m h", h=heads)
                g.memset(m_all, -3.0e38).then_inc(s(f"max_step{n}"), 1)
                pool.wait_ge(s(f"table{n}"), 16 * stores)
                pool.wait_ge(s(f"max_step{n}"), 1)
                steps = 10
                with pool.Fori(0, V) as i:
                    at = [0]

                    def link(ins):
                        at[0] += 1
                        ins.then_inc(s(f"max_step{n}"), 1)
                        pool.wait_ge(s(f"max_step{n}"), i * steps + (1 + at[0]))
                        pool.sem_inc(s("idx_passed"), 1)

                    link(g.tensor_copy(idx[:, 0:1], src_of[:, bass.ds(i, 1)]))
                    g.indirect_dma_start(ringv[:, 0, 0:D + heads], None, table,
                                         bass.IndirectOffsetOnAxis(ap=idx[:, 0:1], axis=0)).then_inc(s(f"max_dma{n}"), 16)
                    link(g.tensor_copy(col, dst_in[:, bass.ds(i, 1)]))
                    link(g.tensor_scalar(hot_f, iota_w[:, 0:W], col, None, ALU.is_equal))
                    link(g.tensor_scalar(off_f, hot_f, 3.0e38, -3.0e38, ALU.mult, ALU.add))
                    pool.wait_ge(s(f"max_dma{n}"), i * 16 + 16)
                    pool.sem_inc(s("idx_passed"), 1)
                    link(g.tensor_tensor(cand3, hot.broadcast_to([P, W, heads]),
                                         ringv[:, 0:1, D:D + heads].broadcast_to([P, W, heads]), ALU.mult))
                    link(g.tensor_tensor(cand3, cand3, off.broadcast_to([P, W, heads]), ALU.add))
                    link(g.partition_all_reduce(red, cand, P, bass.bass_isa.ReduceOp.max))
                    win = pool.value_load(win_of[0:1, bass.ds(i, 1)], min_val=0, max_val=NW - 1)
                    link(g.tensor_copy(red[0:1, :].rearrange("p (o c) -> p o c", o=1), m_all[0:1, bass.ds(win, 1), :]))
                    link(g.partition_all_reduce(red2, red, P, bass.bass_isa.ReduceOp.max))
                    link(g.tensor_copy(m_all[0:1, bass.ds(win, 1), :], red2[0:1, :].rearrange("p (o c) -> p o c", o=1)))
                    assert at[0] == steps
                flat = node_max[0:NP * heads]
                pool.dma_start(flat.rearrange("(o c) -> o c", o=1), big[0:1, 0:NP * heads]).then_inc(s(f"max_dma{n}"), 16)
                pool.wait_ge(s(f"max_dma{n}"), V * 16 + 16)
                edge = (NT - 1) * P * heads
                pool.dma_start(own[:, 0:NT - 1, :], flat[0:edge].rearrange("(m p h) -> p m h", p=P, h=heads)).then_inc(s(f"max_dma{n}"), 16)
                pool.dma_start(own[0:W, NT - 1, :], flat[edge:NP * heads].rearrange("(p h) -> p h", h=heads)).then_inc(s(f"max_dma{n}"), 16)
                pool.wait_ge(s(f"max_dma{n}"), V * 16 + 16 + 32)
                sm = nat_of(smax_nat, 0, NT, heads)
                g.tensor_copy(sm[:, 0:NT - 1, :], own[:, 0:NT - 1, :]).then_inc(s(f"max_step{n}"), 1)
                g.tensor_copy(sm[0:W, NT - 1:NT, :], own[0:W, NT - 1:NT, :]).then_inc(s(f"max_step{n}"), 1)
                pool.wait_ge(s(f"max_step{n}"), 1 + V * steps + 2)

            def settle_max(n, table, heads, stores):
                pool.wait_ge(s(f"spread_known{n}"), 1)
                wide = pool.value_load(flag_i[0:1, n - 2:n - 1], min_val=0, max_val=1)
                with pool.If(wide > 0):
                    exact_max(n, table, heads, stores)
                pool.sem_inc(s(f"max_settled{n}"), 1)

            def gather_pass(n, table, width, spare_free=None):
                def indices(gr, q):
                    g.tensor_copy(idx[:, q * U:q * U + U], src_of[:, bass.ds(gr * U, U)]).then_inc(s("idx"), 1)

                def group(gr, q, rows_done):
                    if not early(gr, Q):
                        pool.wait_ge(s(f"agg_ready{n}"), (gr - (Q - 1)) * U)
                    if early(gr, Q) and gr == 2 and spare_free:
                        pool.wait_ge(*spare_free)
                    pool.wait_ge(s("idx"), gr + (sum(groups(j) for j in range(n)) + 1))
                    pool.sem_inc(s("idx_passed"), 1)
                    for u in range(U):
                        g.indirect_dma_start(ring_rows(n, q)[:, u, 0:width], None, table,
                                             bass.IndirectOffsetOnAxis(ap=idx[:, q * U + u:q * U + u + 1], axis=0)).then_inc(s(f"rows_{q}_{u // (U // 2)}"), 16)
                        if u == U // 2 and not (isinstance(gr, int) and gr == groups(n) - 1):
                            if not early(gr, Q - 1):
                                for part in range(2):
                                    pool.wait_ge(s(f"rows_{(q + 1) % Q}_{part}"), rows_before(n, (q + 1) % Q) + (rows_done if q == Q - 1 else rows_done - 8 * U))
                                pool.sem_inc(s("idx_passed"), 1)
                            indices(gr + 1, (q + 1) % Q)

                indices(0, 0)
                each_group(pool, n, group)

            pool.wait_ge(s("setup_done"), 1)
            gather_pass(0, table_sage[0], D)
            pool.wait_ge(s("table1"), 16 * NT)
            gather_pass(1, table_sage[1], D)
            pool.wait_ge(s("table2"), 16 * NT)
            gather_pass(2, table_sage[2], D)
            pool.wait_ge(s("plan_loaded"), 48)
            settle_max(3, table_gat1, H, len(GAT1_STORES) + 1)
            pool.wait_ge(s("table3"), 16 * (len(GAT1_STORES) + 1))
            gather_pass(3, table_gat1, RW)
            pool.wait_ge(s("h2"), NT)
            settle_max(4, table_gat2, 1, NT)
            pool.wait_ge(s("table4"), 16 * NT)
            gather_pass(4, table_gat2, D + 1, (s("self_sum4"), KD * NT))

        @block.tensor
        def _(pe):
            t = nc.tensor
            turned = [0]

            def turn(src, gate, m):
                pe.wait_ge(*gate)
                if turned[0] >= 2:
                    pe.wait_ge(s("turned_out"), turned[0] - 1)
                b = turned[0] % 2
                for k in range(KD):
                    i = t.transpose(ps_t[:, b, k * P:k * P + rows(m)], src[0:rows(m), m, k * P:(k + 1) * P], ident[0:rows(m), 0:rows(m)])
                i.then_inc(s("turned"), 1)
                turned[0] += 1

            def turn_x():
                for m in range(NT):
                    turn(x_nat, (s("x_loaded"), 32), m)

            pe.wait_ge(s("consts"), 9)
            pe.wait_ge(s("below_step"), NBV + 1)
            for pl in plans:
                i = t.matmul(pl.first_ps, lhsT=pl.below, rhs=ones[0:EP, 0:1], start=True, stop=True)
            i.then_inc(s("bounds"), 1)
            pe.wait_ge(s("viol"), 1)
            t.matmul(ps_n[0:1, 8:10], lhsT=ones[0:EP, 0:1], rhs=viol, start=True, stop=True).then_inc(s("viol_sum"), 1)
            pe.wait_ge(s("cmp"), 2)
            pe.wait_ge(s("order_known"), 1)
            for pl in plans:
                t.matmul(pl.win_ps, lhsT=ones[0:pl.NB, :], rhs=pl.cmp, start=True, stop=True).then_inc(s("windows"), 1)
                for c in range(VC):
                    t.matmul(pl.count_ps[:, c:c + 1], lhsT=pl.cmp[:, c * pl.VR:(c + 1) * pl.VR], rhs=ones[0:pl.NB, 0:1],
                             start=True, stop=True).then_inc(s("windows"), 1)
            turn_x()
            for pl in plans:
                pe.wait_ge(s("visit_rows_f"), pl.i + 1)
                if pl.i:
                    pe.wait_ge(s("turned_out"), NT)
                for c in range(VC):
                    for k in range(2):
                        t.transpose(pl.cols_ps[k][:, c * pl.VR:(c + 1) * pl.VR], pl.rows_f[:, k, c, :], ident[0:pl.VR, 0:pl.VR]).then_inc(s("visit_cols"), 1)
            pe.wait_ge(s("setup_done"), 2)

            def sage_self(n):
                if n:
                    for m in range(NT):
                        turn(natv, (s(f"row_ready{n}"), m + 1), m)
                pe.wait_ge(s("w_loaded"), 16 * 16)
                for m in range(NT):
                    pe.wait_ge(s("turned_out"), NT * n + m + 1)
                    if m >= 2:
                        pe.wait_ge(s("self_out"), NT * n + m - 1)
                    bank = ps_d if m % 2 == 0 else ps_n
                    for k in range(KD):
                        i = t.matmul(bank[0:rows(m), 0:D], lhsT=colsv[:, k, m * P:m * P + rows(m)], rhs=w_sage[:, 2 * n, k, :],
                                     start=(k == 0), stop=(k == KD - 1))
                    i.then_inc(s("self"), 1)

            def sage_pass(n):
                def group(gr, q, rows_done):
                    half = q % 2
                    pe.wait_ge(s(f"oh{n}"), gr + 1)
                    if n == 0:
                        if not early(gr, 2):
                            pe.wait_ge(s("den_step0"), (gr - 1) * U)
                        pe.wait_ge(s("ohd"), gr + 1)
                        for u in range(U):
                            i = t.matmul(deg_bank[half][:, u:u + 1], lhsT=ohd[:, half, u, :], rhs=ones_b[:, :], start=True, stop=True)
                        i.then_inc(s("den_ready0"), 1)
                    for u in range(U):
                        if u % (U // 2) == 0:
                            pe.wait_ge(s(f"rows_{q}_{u // (U // 2)}"), rows_done + rows_before(n, q))
                        bank, at = u // 2, (u % 2) * KD * WS
                        if not early(gr, 1) and u % 2 == 0:
                            pe.wait_ge(s(f"added{n}"), gr * U + (u + 2 - U))
                        for k in range(KD):
                            i = t.matmul(ps[:, bank, at + k * WS:at + (k + 1) * WS], lhsT=ring_rows(n, q)[:, u, k * P:(k + 1) * P],
                                         rhs=oh[:, half, u, :], start=True, stop=True)
                        i.then_inc(s(f"agg_ready{n}"), 1)

                each_group(pe, n, group)

            def sage_neigh(n):
                pe.wait_ge(s(f"added{n}"), VS)
                for m in range(NT):
                    if m >= QUAD:
                        pe.wait_ge(s("neigh_out"), NT * n + m - QUAD + 1)
                    for k in range(KD):
                        i = t.matmul(ps[0:rows(m), m % QUAD, 0:D], lhsT=sums_sage[:, k, m * P:m * P + rows(m)], rhs=w_sage[:, 2 * n + 1, k, :],
                                     start=(k == 0), stop=(k == KD - 1))
                    i.then_inc(s("neigh"), 1)

            def gat_pass(n, heads):
                def ahead(gr, half):
                    if not early(gr, 1):
                        pe.wait_ge(s(f"oht{n}"), gr)
                    pe.wait_ge(s(f"oh{n}"), gr + 1)
                    pe.sem_inc(s("oh_passed"), 1)
                    for u in range(U):
                        i = t.transpose(ps_t[0:W, 0, :].bitcast(BF16)[:, u * P:(u + 1) * P], ohb[:, half, u, :], ident_b[:, :])
                    i.then_inc(s(f"ohp{n}"), 1)

                def lookup(gr, half):
                    regs = windows_of(mybir.EngineType.PE, gr)
                    if not early(gr, 1):
                        pe.wait_ge(s(f"zs{n}"), (gr - 1) * 4 + 1)
                    pe.wait_ge(s(f"oht{n}"), gr + 1)
                    pe.sem_inc(s("oh_passed"), 1)
                    for u in range(U):
                        i = t.matmul(ps_d[:, u * 6 * heads:(u + 1) * 6 * heads], lhsT=oht[:, half, u * P:(u + 1) * P],
                                     rhs=parts_v(heads)[:, bass.ds(regs[u], 1), :, :], start=True, stop=True)
                    i.then_inc(s(f"look{n}"), 1)

                def denom(gr, half):
                    if not early(gr, 2):
                        pe.wait_ge(s(f"den_step{n}"), (gr - 1) * U)
                    pe.wait_ge(s(f"wparts{n}"), gr + 1)
                    for u in range(U):
                        i = t.matmul(den_bank[half][0:W, u * 3 * heads:(u + 1) * 3 * heads], lhsT=ohb[:, half, u, :],
                                     rhs=w_parts_v(heads, half)[:, u, :, :], start=True, stop=True)
                    i.then_inc(s(f"den_ready{n}"), 1)

                def agg(gr, q, us):
                    for u in us:
                        if u == 0:
                            pe.wait_ge(s(f"ohw{n}"), gr + 1)
                        if u >= UV:
                            pe.wait_ge(s(f"ohw_act{n}"), gr * (U - UV) + (u - UV + 1))
                        if not early(gr, 1) or u >= QUAD:
                            pe.wait_ge(s(f"added{n}"), gr * U + (u - QUAD + 1))
                        for k in range(KD):
                            i = t.matmul(ps[:, u % QUAD, k * heads * W:(k + 1) * heads * W], lhsT=ring_rows(n, q)[:, u, k * P:(k + 1) * P],
                                         rhs=ohw_v(heads)[:, q % 2, u, :], start=True, stop=True)
                        i.then_inc(s(f"agg_ready{n}"), 1)

                def step(gr, q, rows_done):
                    half = q % 2
                    last = isinstance(gr, int) and gr == NG - 1
                    pe.wait_ge(s(f"rows_{q}_0"), rows_done + rows_before(n, q))
                    agg(gr, q, range(0, 1))
                    if not last:
                        lookup(gr + 1, 1 - half)
                    denom(gr, half)
                    agg(gr, q, range(1, 4))
                    pe.wait_ge(s(f"rows_{q}_1"), rows_done + rows_before(n, q))
                    agg(gr, q, range(4, 6))
                    if not (isinstance(gr, int) and gr >= NG - 2):
                        ahead(gr + 2, half)
                    agg(gr, q, range(6, U))

                ahead(0, 0)
                lookup(0, 0)
                ahead(1, 1)
                each_group(pe, n, step)

            for n in range(3):
                sage_self(n)
                pe.wait_ge(s("self_out"), NT * (n + 1))
                sage_pass(n)
                sage_neigh(n)

            pe.wait_ge(s("att1"), 2)

            def scores(m):
                pe.wait_ge(s("turned_out"), 3 * NT + m + 1)
                for k in range(KD):
                    i = t.matmul(ps_d[0:rows(m), m * 2 * H:(m + 1) * 2 * H], lhsT=colsv[:, k, m * P:m * P + rows(m)], rhs=att1v[:, k, :],
                                 start=(k == 0), stop=(k == KD - 1))
                return i

            for m in range(NT):
                turn(natv, (s("ln0"), m + 1), m)
                if m >= 2:
                    scores(m - 2)
            scores(NT - 2)
            scores(NT - 1).then_inc(s("scores3"), 1)

            def bound(n, heads):
                pe.wait_ge(s(f"smax_col{n}"), 1)
                t.transpose(ps_n[0:2 * heads, 0:P], ext[:, 0:2 * heads], ident[:, :]).then_inc(s(f"smax_row{n}"), 1)
                pe.wait_ge(s(f"smax_diag{n}"), 1)
                t.matmul(ps_n[:, P:P + 2 * heads], lhsT=ones[0:2 * heads, :], rhs=ext[0:2 * heads, 16:16 + 2 * heads], start=True, stop=True).then_inc(s(f"smax_all{n}"), 1)

            def self_weight_rows():
                for m in range(NT):
                    pe.wait_ge(s("diag3"), m + 1)
                    if m >= QUAD:
                        pe.wait_ge(s("self_sum_out3"), m - QUAD + 1)
                    t.matmul(ps[:, m % QUAD, :].rearrange("p (h n) -> p h n", h=H)[:, :, 0:rows(m)], lhsT=ones[0:rows(m), :],
                             rhs=diag_v(H)[0:rows(m), m % 2, :, 0:rows(m)], start=True, stop=True).then_inc(s("self_sum3"), 1)

            def self_terms(n, heads):
                for m in range(NT):
                    pe.wait_ge(s(f"diag{n}"), m + 1)
                    for k in range(KD):
                        b = (2 * m + k) % QUAD
                        if 2 * m + k >= QUAD:
                            pe.wait_ge(s(f"self_sum_out{n}"), 2 * m + k - QUAD + 1)
                        t.matmul(ps[:, b, 0:heads * P].rearrange("p (h n) -> p h n", h=heads)[:, :, 0:rows(m)],
                                 lhsT=natv[0:rows(m), m, k * P:(k + 1) * P],
                                 rhs=diag_v(heads)[0:rows(m), m % 2, :, 0:rows(m)], start=True, stop=True).then_inc(s(f"self_sum{n}"), 1)

            bound(3, H)
            self_weight_rows()
            pe.wait_ge(s("plan_loaded"), 48)
            gat_pass(3, H)

            pe.wait_ge(s("w1_loaded"), 16)
            nblk = 0
            pe.wait_ge(s("rden_known"), 1)
            t.transpose(ps_t[0:NT * H, 0, 0:P], rden_by_head, ident[:, :]).then_inc(s("rden_turned"), 1)
            for b, bt in enumerate(blocks):
                c0, width = bt[0] * P, sum(rows(m) for m in bt)
                for h in range(H):
                    for f in range(KD):
                        if nblk >= QUAD:
                            pe.wait_ge(s("proj_out"), nblk - QUAD + 1)
                        for k in range(KD):
                            i = t.matmul(ps[:, nblk % QUAD, 0:width], lhsT=w1_sb[:, k, h * D + f * P:h * D + (f + 1) * P],
                                         rhs=bigv[:, k * H + h, c0:c0 + width], start=(k == 0), stop=(k == KD - 1))
                        i.then_inc(s("proj"), 1)
                        nblk += 1

            pe.wait_ge(s("w2_loaded"), 16)
            for m in range(NT):
                pe.wait_ge(s("normed"), KH * (1 + [m in bt for bt in norm_blocks].index(True)))
                if m >= QUAD:
                    pe.wait_ge(s("h2_out"), m - QUAD + 1)
                for c in range(KH):
                    i = t.matmul(ps[0:rows(m), m % QUAD, 0:D], lhsT=bigv[:, c, m * P:m * P + rows(m)], rhs=w2_sb[:, ch_order[c], :],
                                 start=(c == 0), stop=(c == KH - 1))
                i.then_inc(s("h2"), 1)
            bound(4, 1)
            self_terms(4, 1)
            gat_pass(4, 1)
            pe.wait_ge(s("added4"), V)
            for m in range(NT):
                if m >= QUAD:
                    pe.wait_ge(s("y_out"), m - QUAD + 1)
                for k in range(KD):
                    i = t.transpose(ps[0:rows(m), m % QUAD, k * P:(k + 1) * P], bigv[:, k, m * P:m * P + rows(m)], ident[:, :])
                i.then_inc(s("y_turned"), 1)

        @block.scalar
        def _(act):
            A = nc.scalar
            act.wait_ge(s("consts"), 9)
            act.wait_ge(s("dst_known"), 1)
            for b in range(NBV, NB):
                if b >= NBV + 2:
                    act.wait_ge(s("below_act"), b - NBV - 1)
                A.activation(junk_act[:, b % 2, :], dst_f, ACT.Sign, scale=-1.0, bias=bound_at[0:EP, b - NBV:b - NBV + 1],
                             accum_out=below[:, b:b + 1]).then_inc(s("below_act"), 1)

            turned = [0]

            def turn_out(m):
                act.wait_ge(s("turned"), turned[0] + 1)
                A.activation(colsv[:, :, m * P:m * P + rows(m)],
                             ps_t[:, turned[0] % 2, 0:KD * P].rearrange("p (k n) -> p k n", k=KD)[:, :, 0:rows(m)], ACT.Copy).then_inc(s("turned_out"), 1)
                turned[0] += 1

            def degree_pass():
                def step(gr, q, _):
                    act.wait_ge(s("oh0"), gr + 1)
                    if not early(gr, 2):
                        act.wait_ge(s("den_ready0"), gr - 1)
                    A.activation(ohd[:, q % 2, :, :], oh[:, q % 2, :, :], ACT.Copy).then_inc(s("ohd"), 1)

                each_group(act, 0, step)

            def gat_pass(n, heads):
                act.preload_act_table(ACT.Exp)

                def turned_out(gr, half):
                    act.wait_ge(s(f"ohp{n}"), gr + 1)
                    A.activation(oht[:, half, :], ps_t[0:W, 0, :].bitcast(BF16), ACT.Copy).then_inc(s(f"oht{n}"), 1)

                def weigh(gr, half, us):
                    for u in us:
                        for h in range(heads):
                            at = half * U * heads + u * heads + h
                            i = A.activation(ohw_v(heads)[:, half, u, h * W:(h + 1) * W], ohb[:, half, u, :], ACT.Copy, scale=w_buf[:, at:at + 1])
                        i.then_inc(s(f"ohw_act{n}"), 1)

                def step(gr, q, _):
                    half = q % 2
                    act.wait_ge(s(f"z{n}"), gr + 1)
                    if not early(gr, 2):
                        act.wait_ge(s(f"agg_ready{n}"), (gr - 1) * U)
                    A.activation(w_buf[:, half * U * heads:(half + 1) * U * heads], z_buf[:, 2 * U * H:2 * U * H + U * heads], ACT.Exp).then_inc(s(f"w{n}"), 1)
                    A.activation(w_parts_v(heads, half)[:, :, 0, :], z_buf[:, 2 * U * H:2 * U * H + U * heads].rearrange("p (u h) -> p u h", h=heads),
                                 ACT.Exp).then_inc(s(f"w{n}"), 1)
                    act.wait_ge(s(f"w{n}"), gr * 2 + 1)
                    weigh(gr, half, range(UV, UV + 1))
                    if not (isinstance(gr, int) and gr == NG - 1):
                        turned_out(gr + 1, 1 - half)
                    weigh(gr, half, range(UV + 1, U))

                turned_out(0, 0)
                each_group(act, n, step)

            for n in range(3):
                for m in range(NT):
                    turn_out(m)
                if n == 0:
                    degree_pass()
                if n < 2:
                    for m in range(NT):
                        act.wait_ge(s("neigh_out"), NT * n + m + 1)
                        A.activation(natv[0:rows(m), m, 0:D], natv[0:rows(m), m, 0:D], ACT.Relu).then_inc(s(f"row_ready{n + 1}"), 1)
            def ln_apply(k):
                def normed(b):
                    act.wait_ge(s(f"ln_scale{k}"), b + 1)
                    for m in ln_batches[b]:
                        A.activation(natv[0:rows(m), m, 0:D], natv[0:rows(m), m, 0:D], ACT.Identity, scale=rstd[0:rows(m), m:m + 1],
                                     bias=ln_shift[0:rows(m), m:m + 1]).then_inc(s("ln0" if k == 0 else "out_ready"), 1)

                for b, bt in enumerate(ln_batches):
                    act.wait_ge(s(f"ln_stats{k}"), b + 1)
                    A.activation(rstd[:, bt[0]:bt[-1] + 1], rstd[:, bt[0]:bt[-1] + 1], ACT.Sqrt).then_inc(s(f"ln_sqrt{k}"), 1)
                    if k == 0 and b == len(ln_batches) - 1:
                        for m in ln_batches[0]:
                            turn_out(m)
                    if b:
                        normed(b - 1)
                normed(len(ln_batches) - 1)

            ln_apply(0)
            for m in range(ln_batches[1][0], NT):
                turn_out(m)

            def self_terms(n, heads):
                act.wait_ge(s(f"self_z{n}"), 1)
                A.activation(w_self[:, 0:NT * heads], e_nat[:, 0:NT * heads], ACT.Exp).then_inc(s(f"self_w{n}"), 1)
                for m in range(NT):
                    for k in range(KD):
                        act.wait_ge(s(f"self_sum{n}"), 2 * m + k + 1)
                        A.activation(bigv[:, k * heads:(k + 1) * heads, m * P:m * P + rows(m)],
                                     ps[:, (2 * m + k) % QUAD, 0:heads * P].rearrange("p (h n) -> p h n", h=heads)[:, :, 0:rows(m)],
                                     ACT.Copy).then_inc(s(f"self_sum_out{n}"), 1)

            act.wait_ge(s("self_z3"), 1)
            A.activation(w_self[:, 0:NT * H], e_nat[:, 0:NT * H], ACT.Exp).then_inc(s("self_w3"), 1)
            act.wait_ge(s("self_w3"), 1)
            for m in range(NT):
                if m >= 2:
                    act.wait_ge(s("self_sum3"), m - 1)
                for h in range(H):
                    i = A.activation(diag_v(H)[:, m % 2, h, :], ident[:, :], ACT.Copy, scale=w_self[:, m * H + h:m * H + h + 1])
                i.then_inc(s("diag3"), 1)
            gat_pass(3, H)
            act.wait_ge(s("rden_turned"), 1)
            A.activation(rden_by_row, ps_t[0:NT * H, 0, 0:P], ACT.Copy).then_inc(s("rden_turned_out"), 1)
            act.wait_ge(s("gn_var"), 1)
            A.activation(gn_v[:, 3 * KH:4 * KH], gn_v[:, 3 * KH:4 * KH], ACT.Sqrt).then_inc(s("gn_sqrt"), 1)
            act.wait_ge(s("gn_scale"), 1)
            for bt in norm_blocks:
                c0, width = bt[0] * P, sum(rows(m) for m in bt)
                for c in range(KH):
                    A.activation(bigv[:, c, c0:c0 + width], bigv[:, c, c0:c0 + width], ACT.Relu, bias=gn_v[:, 5 * KH + c:5 * KH + c + 1],
                                 scale=gn_v[:, 4 * KH + c:4 * KH + c + 1]).then_inc(s("normed"), 1)
            self_terms(4, 1)
            gat_pass(4, 1)
            ln_apply(1)

        @block.vector
        def _(v):
            X = nc.vector
            done = [0]

            def link(ins):
                done[0] += 1
                ins.then_inc(s("dve_step"), 1)
                v.wait_ge(s("dve_step"), done[0])

            X.memset(x_nat[:, NT - 1, :], 0.0).then_inc(s("x_cleared"), 1)
            link(X.memset(small_i[:, :], 0))
            v.wait_ge(s("dst_loaded"), 16)
            v.wait_ge(s("next_loaded"), 16)
            X.tensor_copy(dst_f, dst_i).then_inc(s("dst_known"), 1)
            v.wait_ge(s("dst_known"), 1)
            link(X.tensor_copy(next_f[0:EP - 1, :], next_i[0:EP - 1, :]))
            X.tensor_scalar(win_all, dst_i, W.bit_length() - 1, None, ALU.arith_shift_right)
            link(X.memset(viol, 0.0))
            X.tensor_tensor(junk[:, 0, 0:EK - 1], dst_f[:, 0:EK - 1], dst_f[:, 1:EK], ALU.is_gt)
            link(X.tensor_tensor(viol[0:EP - 1, 1:2], dst_f[0:EP - 1, EK - 1:EK], next_f[0:EP - 1, :], ALU.is_gt))
            X.tensor_reduce(viol[:, 0:1], junk[:, 0, 0:EK - 1], AX.X, ALU.add).then_inc(s("viol"), 1)
            v.wait_ge(s("viol"), 1)
            for b in range(NBV):
                if b >= 8:
                    v.wait_ge(s("below_step"), b - 7)
                X.tensor_scalar(junk[:, b % 8, :], dst_f, float(W * (b + 1)), 0.0, ALU.is_lt, ALU.add,
                                accum_out=below[:, b:b + 1]).then_inc(s("below_step"), 1)
            v.wait_ge(s("below_act"), NB - NBV)
            X.tensor_scalar(below[:, NBV:NB], below[:, NBV:NB], 0.5, 0.5 * EK, ALU.mult, ALU.add).then_inc(s("below_step"), 1)
            v.wait_ge(s("consts"), 9)
            v.wait_ge(s("bounds"), 1)
            v.wait_ge(s("viol_sum"), 1)
            link(X.tensor_reduce(flag_f, ps_n[0:1, 8:10], AX.X, ALU.add))
            X.tensor_copy(flag_i[0:1, 0:1], flag_f).then_inc(s("order_known"), 1)
            for pl in plans:
                link(X.tensor_copy(pl.first_i, pl.first_ps))
                link(X.tensor_scalar(pl.tile_i, pl.first_i, 7, None, ALU.arith_shift_right))
                link(X.tensor_copy(pl.tile_f, pl.tile_i))
                link(X.tensor_tensor(pl.event, pl.tile_f, iota_b[0:pl.NB, :], ALU.add))
                X.tensor_scalar(pl.cmp, iota_v[0:pl.NB, 0:pl.V], pl.event, None, ALU.is_ge).then_inc(s("cmp"), 1)
            v.wait_ge(s("windows"), 2 * (1 + VC))
            for pl in plans:
                i = X.tensor_tensor(pl.row_i, pl.iota_c[0:pl.VR, :], pl.count_ps, ALU.subtract)
            i.then_inc(s("visit_rows_known"), 1)
            for pl in plans:
                X.tensor_copy(pl.win, pl.win_ps[0:1, :])
                link(X.tensor_scalar(pl.win_f, pl.win_ps, float(pl.W), None, ALU.mult))
            X.memset(s_nat[:, :], 0.0)
            X.memset(r_nat[:, :], 0.0)
            X.memset(den[:, :], 0.0)
            X.memset(mv[:, :], 1.0)
            X.memset(w_self[:, :], 0.0)
            X.memset(score_win[:, :], 0.0)
            X.memset(rden[:, :], 0.0)
            link(X.memset(sums_sage, 0.0))
            for pl in plans:
                v.wait_ge(s(f"visit_rows{pl.i}"), 16 * 2 * VC)
                X.tensor_copy(pl.rows_f, pl.rows_i).then_inc(s("visit_rows_f"), 1)
                v.wait_ge(s("visit_cols"), (pl.i + 1) * 2 * VC)
                X.tensor_copy(pl.src, pl.cols_ps[0])
                link(X.tensor_tensor(pl.dst, pl.cols_ps[1], pl.win_f, ALU.subtract))
                v.sem_inc(s("setup_done"), 1)

            def one_hots(n, gr, half):
                to, w = (oh, WS) if n < 3 else (ohb, W)
                X.tensor_tensor(to[:, half, :, :], iota_w[:, 0:w].rearrange("p (u w) -> p u w", u=1).broadcast_to([P, U, w]),
                                dst_in[:, bass.ds(gr * U, U)].rearrange("p (u w) -> p u w", w=1).broadcast_to([P, U, w]),
                                ALU.is_equal).then_inc(s(f"oh{n}"), 1)

            def attention_vectors(j):
                v.wait_ge(s("att_loaded"), 48)
                link(X.tensor_tensor(prod_pre, w1_pre, att_pre[j].rearrange("p (k n) -> p k n", k=1).broadcast_to([P, KD, HD]), ALU.mult))
                X.tensor_reduce(att1v[:, :, j * H:(j + 1) * H], prod_pre.rearrange("p k (h d) -> p k h d", h=H), AX.X, ALU.add).then_inc(s("att1"), 1)
                v.wait_ge(s("att1"), j + 1)

            def sage_pass(n):
                def group(gr, q, _):
                    half = q % 2
                    regs = windows_of(mybir.EngineType.DVE, gr, NWS)
                    if n == 0 and isinstance(gr, int) and gr in (2, 3):
                        attention_vectors(gr - 2)
                    if not (isinstance(gr, int) and gr == groups(n) - 1):
                        if not early(gr, 1):
                            v.wait_ge(s(f"agg_ready{n}"), gr * U)
                        one_hots(n, gr + 1, 1 - half)
                    if n == 0:
                        v.wait_ge(s("den_ready0"), gr + 1)
                    for u in range(U):
                        if u % 2 == 0:
                            v.wait_ge(s(f"agg_ready{n}"), gr * U + (u + 2))
                        if not (early(gr, 1) and u == 0):
                            v.wait_ge(s(f"added{n}"), gr * U + u)
                        place = sums_sage.rearrange("p k (w c) -> p k w c", c=WS)[:, :, bass.ds(regs[u], 1), :]
                        bank, at = u // 2, (u % 2) * KD * WS
                        X.tensor_tensor(place, place, ps[:, bank, at:at + KD * WS].rearrange("p (k o c) -> p k o c", k=KD, o=1),
                                        ALU.add).then_inc(s(f"added{n}"), 1)
                        if n == 0:
                            if not (early(gr, 1) and u == 0):
                                v.wait_ge(s("den_step0"), gr * U + u)
                            dplace = rden[:, 0:NT].rearrange("p (m o) -> p m o", o=1)[:, bass.ds(regs[u], 1), :]
                            X.tensor_tensor(dplace, dplace, deg_bank[half][:, u:u + 1].rearrange("p (o c) -> p o c", o=1),
                                            ALU.add).then_inc(s("den_step0"), 1)

                one_hots(n, 0, 0)
                each_group(v, n, group)

            def by_row(dst, src, heads, to_rows):
                w = src if to_rows else dst
                r = dst if to_rows else src
                for par in range(2):
                    wins = w[:, par::2, :]
                    rws = r[par * W:(par + 1) * W, 0:wins.shape[1], :]
                    i = X.tensor_copy(rws, wins) if to_rows else X.tensor_copy(wins, rws)
                return i

            def sage_self(n):
                for m in range(NT):
                    v.wait_ge(s("self"), NT * n + m + 1)
                    bank = ps_d if m % 2 == 0 else ps_n
                    X.tensor_tensor(self_nat[0:rows(m), m, :], bank[0:rows(m), 0:D], biasv[0:rows(m), n, :], ALU.add).then_inc(s("self_out"), 1)
                if n == 2:
                    v.wait_ge(s("self_out"), 3 * NT)
                    link(X.tensor_tensor(self_nat[:, 0:NT - 1, :], self_nat[:, 0:NT - 1, :], x_nat[:, 0:NT - 1, :], ALU.add))
                    link(X.tensor_tensor(self_nat[0:W, NT - 1, :], self_nat[0:W, NT - 1, :], x_nat[0:W, NT - 1, :], ALU.add))

            def sage_neigh(n):
                if n == 0:
                    v.wait_ge(s("den_step0"), VS)
                    link(X.tensor_scalar(rden[:, 0:NT], rden[:, 0:NT], 1.0, None, ALU.max))
                    link(X.reciprocal(rden[:, 0:NT], rden[:, 0:NT]))
                def produce(m):
                    v.wait_ge(s("neigh"), NT * n + m + 1)
                    if n:
                        v.wait_ge(s(f"table{n}"), 16 * NT)
                        v.wait_ge(s("turned"), NT * (n + 1))
                    X.scalar_tensor_tensor(out=natv[0:rows(m), m, 0:D], in0=ps[0:rows(m), m % QUAD, 0:D], scalar=rden[0:rows(m), m:m + 1],
                                           in1=self_nat[0:rows(m), m, :], op0=ALU.mult, op1=ALU.add).then_inc(s("neigh_out"), 1)
                if n == 2:
                    layer_norm(0, produce, s("neigh_out"), 2 * NT)
                    return
                for m in range(NT):
                    produce(m)
                v.wait_ge(s("neigh"), NT * (n + 1))
                link(X.memset(sums_sage, 0.0))

            def layer_norm(k, produce, made, before):
                def finish(b):
                    bt = ln_batches[b]
                    v.wait_ge(s(f"ln_sqrt{k}"), b + 1)
                    m0, m1 = bt[0], bt[-1] + 1
                    link(X.reciprocal(rstd[:, m0:m1], rstd[:, m0:m1]))
                    X.scalar_tensor_tensor(out=ln_shift[:, m0:m1].rearrange("p (m o) -> p m o", o=1), in0=mv[:, 2 * m0:2 * m1].rearrange("p (m s) -> p m s", s=2)[:, :, 0:1],
                                           scalar=-1.0, in1=rstd[:, m0:m1].rearrange("p (m o) -> p m o", o=1), op0=ALU.mult, op1=ALU.mult).then_inc(s(f"ln_scale{k}"), 1)

                for b, bt in enumerate(ln_batches):
                    for m in bt:
                        produce(m)
                    v.wait_ge(made, before + bt[-1] + 1)
                    for m in bt:
                        i = X.bn_stats(stats[0:rows(m), m * 6:(m + 1) * 6], natv[0:rows(m), m, 0:D])
                    link(i)
                    for m in bt:
                        i = X.bn_aggr(mv[0:rows(m), 2 * m:2 * m + 2], stats[0:rows(m), m * 6:(m + 1) * 6])
                    link(i)
                    m0, m1 = bt[0], bt[-1] + 1
                    X.tensor_scalar(rstd[:, m0:m1].rearrange("p (m o) -> p m o", o=1), mv[:, 2 * m0:2 * m1].rearrange("p (m s) -> p m s", s=2)[:, :, 1:2],
                                    EPS, None, ALU.add).then_inc(s(f"ln_stats{k}"), 1)
                    if b:
                        finish(b - 1)
                finish(len(ln_batches) - 1)

            def scores_nat(heads):
                return s_nat[:, 0:NT * 2 * heads].rearrange("p (m s) -> p m s", s=2 * heads)

            def bounds(n, heads):
                sv = scores_nat(heads)
                link(X.memset(ext[:, :], -3.0e38))
                link(X.memset(e_nat[:, 0:2 * heads], -3.0e38))
                X.tensor_reduce(ext[:, 0:heads], sv[:, 0:NT - 1, 0:heads].rearrange("p m h -> p h m"), AX.X, ALU.max)
                link(X.tensor_reduce(ext[:, heads:2 * heads], sv[:, 0:NT - 1, 0:heads].rearrange("p m h -> p h m"), AX.X, ALU.min))
                link(X.tensor_scalar(ext[:, heads:2 * heads], ext[:, heads:2 * heads], -1.0, None, ALU.mult))
                X.tensor_copy(e_nat[0:real(NT - 1), 0:heads], sv[0:real(NT - 1), NT - 1, 0:heads])
                link(X.tensor_scalar(e_nat[0:real(NT - 1), heads:2 * heads], sv[0:real(NT - 1), NT - 1, 0:heads], -1.0, None, ALU.mult))
                X.tensor_tensor(ext[:, 0:2 * heads], ext[:, 0:2 * heads], e_nat[:, 0:2 * heads], ALU.max).then_inc(s(f"smax_col{n}"), 1)
                v.wait_ge(s(f"smax_row{n}"), 1)
                link(X.tensor_reduce(ext[0:2 * heads, 8:9], ps_n[0:2 * heads, 0:P], AX.X, ALU.max))
                X.tensor_scalar(ext[0:2 * heads, 16:16 + 2 * heads], ident[0:2 * heads, 0:2 * heads], ext[0:2 * heads, 8:9], None, ALU.mult).then_inc(s(f"smax_diag{n}"), 1)
                v.wait_ge(s(f"smax_all{n}"), 1)
                link(X.tensor_copy(ext[:, 0:2 * heads], ps_n[:, P:P + 2 * heads]))
                rv, ev = nat_of(r_nat, 0, NT, heads), nat_of(e_nat, 0, NT, heads)
                sm = nat_of(smax_nat, 0, NT, heads)
                link(X.tensor_copy(sm, ext[:, 0:heads].rearrange("p (m h) -> p m h", m=1).broadcast_to([P, NT, heads])))
                link(X.tensor_tensor(ext[0:1, 8:8 + heads], ext[0:1, 0:heads], ext[0:1, heads:2 * heads], ALU.add))
                link(X.tensor_reduce(ext[0:1, 24:25], ext[0:1, 8:8 + heads], AX.X, ALU.max))
                link(X.tensor_scalar(ext[0:1, 25:26], ext[0:1, 24:25], SPREAD, None, ALU.is_gt))
                X.tensor_copy(flag_i[0:1, n - 2:n - 1], ext[0:1, 25:26]).then_inc(s(f"spread_known{n}"), 1)
                v.wait_ge(s(f"max_settled{n}"), 1)
                link(X.tensor_tensor(sm, sm, sv[:, :, 0:heads], ALU.max))
                link(X.tensor_tensor(rv, sv[:, :, heads:2 * heads], sm, ALU.add))
                link(X.scalar_tensor_tensor(out=rv, in0=rv, scalar=SLOPE, in1=rv, op0=ALU.mult, op1=ALU.max))
                link(X.tensor_tensor(ev, sv[:, :, 0:heads], sv[:, :, heads:2 * heads], ALU.add))
                link(X.scalar_tensor_tensor(out=ev, in0=ev, scalar=SLOPE, in1=ev, op0=ALU.mult, op1=ALU.max))
                link(X.tensor_tensor(ev, ev, rv, ALU.subtract))
                X.tensor_scalar(ev, ev, 0.0, None, ALU.min).then_inc(s(f"self_z{n}"), 1)
                if n == 4:
                    looked_up_parts(heads)

            def looked_up_parts(heads):
                sv, rv = scores_nat(heads), nat_of(r_nat, 0, NT, heads)
                wv = score_v(heads)
                by_row(wv[:, :, 0:heads], sv[:, :, heads:2 * heads], heads, False)
                link(by_row(wv[:, :, heads:2 * heads], rv, heads, False))
                pv = parts_v(heads)
                for j in range(3):
                    link(X.tensor_copy(pv[:, :, j, :], wv))
                    if j < 2:
                        link(X.tensor_tensor(wv, wv, pv[:, :, j, :], ALU.subtract))
                link(X.memset(den[:, :], 0.0))

            def diagonals(n, col, heads, gate, name, ms=range(NT)):
                for m in ms:
                    if m >= 2:
                        v.wait_ge(*gate(m))
                    X.tensor_tensor(diag_v(heads)[:, m % 2, :, :], ident[:, :].rearrange("p (h n) -> p h n", h=1).broadcast_to([P, heads, P]),
                                    col[:, m * heads:(m + 1) * heads].rearrange("p (h n) -> p h n", n=1).broadcast_to([P, heads, P]),
                                    ALU.mult).then_inc(s(name), 1)

            def gat_pass(n, heads):
                v.wait_ge(s("plan_loaded"), 48)

                def place(reg):
                    return bigv[:, 0:KD * heads, :].rearrange("p c (w n) -> p c w n", n=W)[:, :, bass.ds(reg, 1), :]

                def z_steps(gr, q, rows_done):
                    sh = ring_rows(n, q)[:, :, D:D + heads]
                    parts = ps_d[:, 0:U * 6 * heads].rearrange("p (u j s) -> p u s j", u=U, j=3)
                    look = look_buf[:, 0:U * 2 * heads].rearrange("p (u s) -> p u s", u=U)
                    zz = [z_buf[:, i * U * H:i * U * H + U * heads].rearrange("p (u h) -> p u h", u=U) for i in range(3)]

                    def looked_up():
                        v.wait_ge(s(f"look{n}"), gr + 1)
                        X.tensor_reduce(look, parts, AX.X, ALU.add).then_inc(s(f"zs{n}"), 1)

                    def added():
                        for part in range(2):
                            v.wait_ge(s(f"rows_{q}_{part}"), rows_done + rows_before(n, q))
                        v.wait_ge(s(f"zs{n}"), gr * 4 + 1)
                        X.tensor_tensor(zz[0], sh, look[:, :, 0:heads], ALU.add).then_inc(s(f"zs{n}"), 1)

                    def leaky():
                        v.wait_ge(s(f"zs{n}"), gr * 4 + 2)
                        X.scalar_tensor_tensor(out=zz[1], in0=zz[0], scalar=SLOPE, in1=zz[0], op0=ALU.mult, op1=ALU.max).then_inc(s(f"zs{n}"), 1)

                    def less_r():
                        v.wait_ge(s(f"zs{n}"), gr * 4 + 3)
                        X.tensor_tensor(zz[0], zz[1], look[:, :, heads:2 * heads], ALU.subtract).then_inc(s(f"zs{n}"), 1)

                    def at_most_0():
                        v.wait_ge(s(f"zs{n}"), gr * 4 + 4)
                        if not early(gr, 1):
                            v.wait_ge(s(f"w{n}"), gr * 2)
                        X.tensor_scalar(zz[2], zz[0], 0.0, None, ALU.min).then_inc(s(f"z{n}"), 1)

                    return looked_up, added, leaky, less_r, at_most_0

                def w_in_parts(gr, half):
                    w = w_buf[:, half * U * heads:(half + 1) * U * heads].rearrange("p (u h) -> p u h", h=heads)
                    rest = w_rest[:, 0:U * heads].rearrange("p (u h) -> p u h", h=heads)
                    part = [w_parts_v(heads, half)[:, :, j, :] for j in range(3)]

                    def second():
                        v.wait_ge(s(f"w{n}"), gr * 2 + 2)
                        X.tensor_tensor(rest, w, part[0], ALU.subtract).then_inc(s(f"split{n}"), 1)
                        X.tensor_tensor(part[1], w, part[0], ALU.subtract).then_inc(s(f"split{n}"), 1)

                    def third():
                        v.wait_ge(s(f"split{n}"), gr * 2 + 2)
                        X.tensor_tensor(part[2], rest, part[1], ALU.subtract).then_inc(s(f"wparts{n}"), 1)

                    return second, third

                def weigh(gr, half):
                    v.wait_ge(s(f"w{n}"), gr * 2 + 1)
                    wv = w_buf[:, half * U * heads:(half + 1) * U * heads].rearrange("p (u h w) -> p u h w", u=U, w=1)[:, 0:UV]
                    X.tensor_tensor(ohw_v(heads)[:, half, 0:UV, :].rearrange("p u (h w) -> p u h w", h=heads),
                                    ohb[:, half, 0:UV, :].rearrange("p u (h w) -> p u h w", h=1).broadcast_to([P, UV, heads, W]),
                                    wv.broadcast_to([P, UV, heads, W]), ALU.mult).then_inc(s(f"ohw{n}"), 1)

                def residual(part):
                    if part == 0:
                        v.wait_ge(s("res_loaded"), 32)
                        X.tensor_tensor(res_nat[0:W, NT - 1, :], res_nat[0:W, NT - 1, :], biasv[0:W, 3, :], ALU.add).then_inc(s("res_added"), 1)
                    ms = slice(part * (NT - 1) // 4, (part + 1) * (NT - 1) // 4)
                    X.tensor_tensor(res_nat[:, ms, :], res_nat[:, ms, :], biasv[:, 3:4, :].broadcast_to([P, ms.stop - ms.start, D]), ALU.add).then_inc(s("res_added"), 1)

                def adds(gr, half, us, regs):
                    for u in us:
                        v.wait_ge(s(f"agg_ready{n}"), gr * U + (u + 1))
                        if not (early(gr, 1) and u == 0):
                            v.wait_ge(s(f"added{n}"), gr * U + u)
                        pl = place(regs[u])
                        X.tensor_tensor(pl, pl, ps[:, u % QUAD, 0:KD * heads * W].rearrange("p (c o n) -> p c o n", c=KD * heads, o=1),
                                        ALU.add).then_inc(s(f"added{n}"), 1)
                        if not (early(gr, 1) and u == 0):
                            v.wait_ge(s(f"den_step{n}"), gr * U + u)
                        dpl = den_v(3 * heads)[:, bass.ds(regs[u], 1), :]
                        X.tensor_tensor(dpl, dpl, den_bank[half][0:W, u * 3 * heads:(u + 1) * 3 * heads].rearrange("p (o c) -> p o c", o=1),
                                        ALU.add).then_inc(s(f"den_step{n}"), 1)

                def step(gr, q, rows_done):
                    half = q % 2
                    last = isinstance(gr, int) and gr == NG - 1
                    regs = windows_of(mybir.EngineType.DVE, gr)
                    v.wait_ge(s(f"den_ready{n}"), gr + 1)
                    if last:
                        adds(gr, half, range(U), regs)
                        return
                    z = z_steps(gr + 1, (q + 1) % Q, rows_done if q < Q - 1 else rows_done + 8 * U)
                    second, third = w_in_parts(gr + 1, 1 - half)
                    if n == 4 and early(gr, 4):
                        residual(gr)
                    adds(gr, half, range(0, 1), regs)
                    z[0]()
                    adds(gr, half, range(1, 2), regs)
                    z[1]()
                    adds(gr, half, range(2, 3), regs)
                    z[2]()
                    if not (isinstance(gr, int) and gr >= NG - 2):
                        v.wait_ge(s(f"ohw_act{n}"), (gr + 1) * (U - UV))
                        one_hots(n, gr + 2, half)
                    z[3]()
                    adds(gr, half, range(3, 4), regs)
                    z[4]()
                    adds(gr, half, range(4, 5), regs)
                    if not early(gr, 1):
                        v.wait_ge(s(f"agg_ready{n}"), gr * U)
                    weigh(gr + 1, 1 - half)
                    adds(gr, half, range(5, 6), regs)
                    second()
                    adds(gr, half, range(6, 7), regs)
                    third()
                    adds(gr, half, range(7, 8), regs)

                one_hots(n, 0, 0)
                one_hots(n, 1, 1)
                for z in z_steps(0, 0, 8 * U):
                    z()
                weigh(0, 0)
                for part in w_in_parts(0, 0):
                    part()
                each_group(v, n, step)

            def denominators(n, heads):
                v.wait_ge(s(f"added{n}"), V)
                v.wait_ge(s(f"den_step{n}"), V)
                dn = den_nat[:, 0:NT * 3 * heads].rearrange("p (m j h) -> p m j h", j=3, h=heads)
                link(X.memset(den_nat, 0.0))
                link(by_row(den_nat[:, 0:NT * 3 * heads].rearrange("p (m h) -> p m h", m=NT), den_v(3 * heads), 3 * heads, True))
                link(X.tensor_tensor(nat_of(rden, 0, NT, heads), dn[:, :, 1, :], dn[:, :, 2, :], ALU.add))
                link(X.tensor_tensor(nat_of(rden, 0, NT, heads), nat_of(rden, 0, NT, heads), dn[:, :, 0, :], ALU.add))
                link(X.tensor_tensor(rden[:, 0:NT * heads], rden[:, 0:NT * heads], w_self[:, 0:NT * heads], ALU.add))
                link(X.tensor_scalar(rden[:, 0:NT * heads], rden[:, 0:NT * heads], 1.0e-30, None, ALU.max))
                link(X.reciprocal(rden[:, 0:NT * heads], rden[:, 0:NT * heads]))

            v.wait_ge(s("w_loaded"), 16 * 16)
            for n in range(3):
                sage_self(n)
                sage_pass(n)
                sage_neigh(n)

            v.wait_ge(s("scores3"), 1)
            sv = scores_nat(H)
            link(X.tensor_copy(sv[:, 0:NT - 1, :], ps_d[:, 0:(NT - 1) * 2 * H].rearrange("p (m s) -> p m s", s=2 * H)))
            link(X.tensor_copy(sv[0:W, NT - 1, :], ps_d[0:W, (NT - 1) * 2 * H:NT * 2 * H]))
            v.wait_ge(s("ln0"), NT)
            X.tensor_copy(natv[:, 0:NT - 1, D:D + H], sv[:, 0:NT - 1, 0:H]).then_inc(s("gat1_rows_ready"), 1)
            X.tensor_copy(natv[0:W, NT - 1, D:D + H], sv[0:W, NT - 1, 0:H]).then_inc(s("gat1_rows_ready"), 1)
            bounds(3, H)
            for m in range(NT):
                v.wait_ge(s("self_sum3"), m + 1)
                X.tensor_tensor(bigv[:, :, m * P:m * P + rows(m)].rearrange("p (k h) n -> p k h n", k=KD),
                                ps[:, m % QUAD, :].rearrange("p (o h n) -> p o h n", o=1, h=H)[:, :, :, 0:rows(m)].broadcast_to([P, KD, H, rows(m)]),
                                colsv[:, :, m * P:m * P + rows(m)].rearrange("p k (o n) -> p k o n", o=1).broadcast_to([P, KD, H, rows(m)]),
                                ALU.mult).then_inc(s("self_sum_out3"), 1)
            v.wait_ge(s("self_sum_out3"), NT)
            looked_up_parts(H)
            gat_pass(3, H)
            denominators(3, H)
            def column_stats(n):
                b, h, f = n // KH, n % KH // KD, n % KD
                c0 = blocks[b][0] * P
                v.wait_ge(s("proj_out"), n + 1)
                at = ((f * H + h) * NBK + b) * 6
                return X.bn_stats(gn_stats[:, at:at + 6], bigv[:, f * H + h, c0:min(c0 + 4 * P, N)])

            nblk = 0
            X.tensor_copy(rden_by_head.rearrange("p (h m) -> p m h", h=H), nat_of(rden, 0, NT, H)).then_inc(s("rden_known"), 1)
            for b, bt in enumerate(blocks):
                c0, width = bt[0] * P, sum(rows(m) for m in bt)
                v.wait_ge(s(f"rden_loaded{b % 2}"), 16 * (b // 2 + 1))
                for h in range(H):
                    v.wait_ge(s("proj"), nblk + KD)
                    for f in range(KD):
                        X.tensor_tensor(bigv[:, f * H + h, c0:c0 + width], ps[:, nblk % QUAD, 0:width],
                                        rb_v(b)[:, h, 0:width], ALU.mult).then_inc(s("proj_out"), 1)
                        nblk += 1
                        if nblk > 1:
                            column_stats(nblk - 2)
            link(column_stats(nblk - 1))
            for c in range(KH):
                i = X.bn_aggr(gn_mv[:, 2 * c:2 * c + 2], gn_stats[:, c * NBK * 6:(c + 1) * NBK * 6])
            link(i)
            mean, var = (gn_mv[:, :].rearrange("p (f h s) -> p s f h", f=KD, s=2)[:, j] for j in range(2))
            gq = [gn_v[:, i * KH:(i + 1) * KH].rearrange("p (f h) -> p f h", f=KD) for i in range(6)]
            b1, gn_w, gn_b, gn_ms = (gv[:, i, :].rearrange("p (h f) -> p f h", h=H) for i in range(4))
            link(X.tensor_tensor(gq[0], mean, b1, ALU.add))
            link(X.tensor_tensor(gq[0], gq[0], gn_ms, ALU.mult))
            link(X.tensor_tensor(gq[1], b1, gq[0], ALU.subtract))
            link(X.tensor_tensor(gq[2], mean, gq[1], ALU.add))
            link(X.tensor_tensor(gq[2], gq[2], gq[2], ALU.mult))
            link(X.tensor_tensor(gq[3], var, gq[2], ALU.add))
            X.tensor_scalar(gq[3], gq[3], EPS, None, ALU.add).then_inc(s("gn_var"), 1)
            v.wait_ge(s("gn_sqrt"), 1)
            link(X.reciprocal(gn_v[:, 3 * KH:4 * KH], gn_v[:, 3 * KH:4 * KH]))
            link(X.tensor_tensor(gq[4], gq[3], gn_w, ALU.mult))
            link(X.tensor_tensor(gq[5], gq[4], gq[1], ALU.mult))
            X.tensor_tensor(gq[5], gq[5], gn_b, ALU.add).then_inc(s("gn_scale"), 1)
            sv = scores_nat(1)
            for m in range(NT):
                v.wait_ge(s("h2"), m + 1)
                X.tensor_copy(natv[0:rows(m), m, 0:D], ps[0:rows(m), m % QUAD, 0:D]).then_inc(s("h2_out"), 1)
                v.wait_ge(s("h2_out"), m + 1)
                for j in range(2):
                    i = X.tensor_tensor(cols[0:rows(m), (2 * (m % 2) + j) * D:(2 * (m % 2) + j + 1) * D],
                                    natv[0:rows(m), m, 0:D], att2v[0:rows(m), j, :], ALU.mult)
                link(i)
                link(X.tensor_reduce(sv[0:rows(m), m, :], cols[0:rows(m), 2 * (m % 2) * D:2 * (m % 2 + 1) * D].rearrange("p (j d) -> p j d", j=2), AX.X, ALU.add))
                X.tensor_copy(natv[0:rows(m), m, D:D + 1], sv[0:rows(m), m, 0:1]).then_inc(s("gat2_row_ready"), 1)
            bounds(4, 1)
            v.wait_ge(s("self_w4"), 1)
            diagonals(4, w_self, 1, lambda m: (s("self_sum4"), KD * (m - 1)), "diag4")
            v.wait_ge(s("self_sum_out4"), KD * NT)
            gat_pass(4, 1)
            denominators(4, 1)
            v.wait_ge(s("res_added"), 5)

            def last_rows(m):
                v.wait_ge(s("y_turned"), m + 1)
                X.scalar_tensor_tensor(out=natv[0:rows(m), m, 0:D], in0=ps[0:rows(m), m % QUAD, 0:D], scalar=rden[0:rows(m), m:m + 1],
                                       in1=res_nat[0:rows(m), m, :], op0=ALU.mult, op1=ALU.add).then_inc(s("y_out"), 1)
            layer_norm(1, last_rows, s("y_out"), 0)


_INS = ["x", "src", "dst", "L0_gnn_W0_self", "L0_gnn_W0_neigh", "L0_gnn_b0", "L0_gnn_W1_self", "L0_gnn_W1_neigh", "L0_gnn_b1",
        "L0_gnn_W2_self", "L0_gnn_W2_neigh", "L0_gnn_b2", "L1_gnn_W1", "L1_gnn_att_src1", "L1_gnn_att_dst1", "L1_gnn_b1",
        "L1_gnn_gn_w", "L1_gnn_gn_b", "L1_gnn_gn_ms", "L1_gnn_W2", "L1_gnn_att_src2", "L1_gnn_att_dst2", "L1_gnn_b2"]


def kernel(**inputs):
    import numpy as _np
    import concourse.bacc as _bacc
    from concourse import mybir as _mybir
    from concourse.bass_utils import run_bass_kernel_spmd as _run

    nc = _bacc.Bacc("TRN2", target_bir_lowering=False, num_devices=1)
    arrays, args = {}, {}
    for name in _INS:
        arr = _np.ascontiguousarray(inputs[name])
        arrays[f"in_{name}"] = arr
        args[name] = nc.dram_tensor(f"in_{name}", arr.shape, _mybir.dt.from_np(arr.dtype), kind="ExternalInput").ap()
    out = nc.dram_tensor("out_0", args["x"].shape, _mybir.dt.float32, kind="ExternalOutput").ap()
    build_gnn(nc, args, out)
    r = _run(nc, [arrays], core_ids=[0])
    return r.results[0]["out_0"]
```
